# Optimizing a Trainium2 kernel written in Bass

```python
import numpy as np
import jax
import jax.numpy as jnp

def _softmax(x, axis=-1):
    return jax.nn.softmax(x, axis=axis)

def _gelu(x):
    return jax.nn.gelu(x, approximate=True)

def _silu(x):
    return jax.nn.silu(x)

def _sigmoid(x):
    return jax.nn.sigmoid(x)

def _layernorm(x, axis=-1, eps=1e-05):
    m = jnp.mean(x, axis=axis, keepdims=True)
    v = jnp.var(x, axis=axis, keepdims=True)
    return (x - m) / jnp.sqrt(v + eps)

def _scatter_add(tgt, idx, src, axis=0):
    return tgt.at[idx].add(src)

def _segment_sum(src, seg, n):
    return jax.ops.segment_sum(src, seg, n)
kernel_name = 'mk_seq_preln_d2_jaxref_r8_58861c'

def setup_inputs(seed: int=0):
    np.random.seed(seed)
    _w = jnp.asarray

    def _L0_attn_setup():
        import jax, jax.numpy as jnp
        import numpy as np
        B, S, D = (1, 256, 128)
        H = 16
        DH = D // H
        WIN = 128
        DIL = 4
        key = jax.random.key(seed)
        k1, k2, k3 = jax.random.split(key, 3)
        x = jax.random.normal(k1, (B, S, D), jnp.float32)
        w_qkv = jax.random.normal(k2, (D, 3 * D), jnp.float32) * 0.02
        w_out = jax.random.normal(k3, (D, D), jnp.float32) * 0.02
        return {'x': x, 'w_qkv': w_qkv, 'w_out': w_out}
    _L0_attn_in = _L0_attn_setup()

    def _L0_ffn_setup():
        import jax, jax.numpy as jnp
        import numpy as np
        D_MODEL = 128
        HIDDEN = 512
        NUM_ROUTED = 7
        TOP_K = 2

        def _swiglu(x_flat, wg, wu, wd):
            g = jnp.einsum('nd,edh->enh', x_flat, wg)
            u = jnp.einsum('nd,edh->enh', x_flat, wu)
            h = jax.nn.silu(g) * u
            return jnp.einsum('enh,ehd->end', h, wd)
        key = jax.random.key(seed)
        ks = jax.random.split(key, 8)
        s = 0.02
        return {'x': jax.random.normal(ks[0], (4, 256, D_MODEL), jnp.float32), 'router_w': jax.random.normal(ks[1], (NUM_ROUTED, D_MODEL), jnp.float32) * s, 'w_gate': jax.random.normal(ks[2], (NUM_ROUTED, D_MODEL, HIDDEN), jnp.float32) * s, 'w_up': jax.random.normal(ks[3], (NUM_ROUTED, D_MODEL, HIDDEN), jnp.float32) * s, 'w_down': jax.random.normal(ks[4], (NUM_ROUTED, HIDDEN, D_MODEL), jnp.float32) * s, 'sw_gate': jax.random.normal(ks[5], (1, D_MODEL, HIDDEN), jnp.float32) * s, 'sw_up': jax.random.normal(ks[6], (1, D_MODEL, HIDDEN), jnp.float32) * s, 'sw_down': jax.random.normal(ks[7], (1, HIDDEN, D_MODEL), jnp.float32) * s}
    _L0_ffn_in = _L0_ffn_setup()

    def _L1_attn_setup():
        import jax, jax.numpy as jnp
        import numpy as np
        D_MODEL = 128
        NUM_HEADS = 16
        HEAD_DIM = D_MODEL // NUM_HEADS
        THETA = 10000.0
        B, T = (4, 256)

        def _cos_sin(seq_len, head_dim, theta):
            freqs = 1.0 / theta ** (jnp.arange(0, head_dim, 2, dtype=jnp.float32) / head_dim)
            t = jnp.arange(seq_len, dtype=jnp.float32)
            angles = jnp.outer(t, freqs)
            return jnp.concatenate([jnp.cos(angles), jnp.sin(angles)], axis=-1)

        def _apply_rope(x, cos_sin):
            x1 = x[..., 0::2]
            x2 = x[..., 1::2]
            half = x.shape[-1] // 2
            cos = cos_sin[:, :half]
            sin = cos_sin[:, half:]
            out = jnp.stack([x1 * cos - x2 * sin, x1 * sin + x2 * cos], axis=-1)
            return out.reshape(x.shape)
        key = jax.random.key(seed)
        k1, k2, k3 = jax.random.split(key, 3)
        x = jax.random.normal(k1, (B, T, D_MODEL), dtype=jnp.float32)
        W_qkv = jax.random.normal(k2, (3 * D_MODEL, D_MODEL), dtype=jnp.float32) * D_MODEL ** (-0.5)
        W_out = jax.random.normal(k3, (D_MODEL, D_MODEL), dtype=jnp.float32) * D_MODEL ** (-0.5)
        return {'x': x, 'W_qkv': W_qkv, 'W_out': W_out}
    _L1_attn_in = _L1_attn_setup()

    def _L1_ffn_setup():
        import jax, jax.numpy as jnp
        import numpy as np
        D = 128
        E = 8
        H = 256
        TOP_K = 2
        ALPHA = 0.5
        LN_EPS = 1e-05

        def _experts_all(x, W1, b1, W2, b2):
            h = jax.nn.relu(jnp.einsum('bld,edh->eblh', x, W1) + b1[:, None, None, :])
            return jnp.einsum('eblh,ehd->ebld', h, W2) + b2[:, None, None, :]

        def _selected_expert(x, expert_idx, W1, b1, W2, b2):
            oh = jax.nn.one_hot(expert_idx, E, dtype=x.dtype)
            return jnp.einsum('ebld,ble->bld', _experts_all(x, W1, b1, W2, b2), oh)

        def _layer_norm(x, gamma, beta):
            mu = jnp.mean(x, axis=-1, keepdims=True)
            var = jnp.mean(jnp.square(x - mu), axis=-1, keepdims=True)
            return (x - mu) * jax.lax.rsqrt(var + LN_EPS) * gamma + beta
        key = jax.random.key(seed)
        ks = jax.random.split(key, 8)
        x = jax.random.normal(ks[0], (2, 256, D), dtype=jnp.float32)
        gate_W = jax.random.normal(ks[1], (D, E), dtype=jnp.float32) * 0.02
        gate_b = jnp.zeros((E,), dtype=jnp.float32)
        W1 = jax.random.normal(ks[2], (E, D, H), dtype=jnp.float32) * 0.02
        b1 = jnp.zeros((E, H), dtype=jnp.float32)
        W2 = jax.random.normal(ks[3], (E, H, D), dtype=jnp.float32) * 0.02
        b2 = jnp.zeros((E, D), dtype=jnp.float32)
        ln_gamma = jnp.ones((D,), dtype=jnp.float32)
        ln_beta = jnp.zeros((D,), dtype=jnp.float32)
        return {'x': x, 'gate_W': gate_W, 'gate_b': gate_b, 'W1': W1, 'b1': b1, 'W2': W2, 'b2': b2, 'ln_gamma': ln_gamma, 'ln_beta': ln_beta}
    _L1_ffn_in = _L1_ffn_setup()
    _d = {'L0_attn_x': _L0_attn_in['x'], 'L0_attn_w_qkv': _L0_attn_in['w_qkv'], 'L0_attn_w_out': _L0_attn_in['w_out'], 'L0_ffn_router_w': _L0_ffn_in['router_w'], 'L0_ffn_w_gate': _L0_ffn_in['w_gate'], 'L0_ffn_w_up': _L0_ffn_in['w_up'], 'L0_ffn_w_down': _L0_ffn_in['w_down'], 'L0_ffn_sw_gate': _L0_ffn_in['sw_gate'], 'L0_ffn_sw_up': _L0_ffn_in['sw_up'], 'L0_ffn_sw_down': _L0_ffn_in['sw_down'], 'L1_attn_W_qkv': _L1_attn_in['W_qkv'], 'L1_attn_W_out': _L1_attn_in['W_out'], 'L1_ffn_gate_W': _L1_ffn_in['gate_W'], 'L1_ffn_gate_b': _L1_ffn_in['gate_b'], 'L1_ffn_W1': _L1_ffn_in['W1'], 'L1_ffn_b1': _L1_ffn_in['b1'], 'L1_ffn_W2': _L1_ffn_in['W2'], 'L1_ffn_b2': _L1_ffn_in['b2'], 'L1_ffn_ln_gamma': _L1_ffn_in['ln_gamma'], 'L1_ffn_ln_beta': _L1_ffn_in['ln_beta']}
    _x0 = _d['L0_attn_x']
    _d['L0_attn_x'] = jax.random.normal(jax.random.fold_in(jax.random.key(seed), 1), (8, 512, 128), dtype=_x0.dtype)
    del _x0
    return _d

def reference(L0_attn_x, L0_attn_w_qkv, L0_attn_w_out, L0_ffn_router_w, L0_ffn_w_gate, L0_ffn_w_up, L0_ffn_w_down, L0_ffn_sw_gate, L0_ffn_sw_up, L0_ffn_sw_down, L1_attn_W_qkv, L1_attn_W_out, L1_ffn_gate_W, L1_ffn_gate_b, L1_ffn_W1, L1_ffn_b1, L1_ffn_W2, L1_ffn_b2, L1_ffn_ln_gamma, L1_ffn_ln_beta):

    def _L0_attn_ref(x, w_qkv, w_out):
        import jax, jax.numpy as jnp
        import numpy as np
        B, S, D = (1, 256, 128)
        H = 16
        DH = D // H
        WIN = 128
        DIL = 4
        b, s, d = x.shape
        scale = 1.0 / np.sqrt(DH).astype(np.float32)
        qkv = x @ w_qkv
        q, k, v = jnp.split(qkv, 3, axis=-1)
        q = q.reshape(b, s, H, DH)
        k = k.reshape(b, s, H, DH)
        v = v.reshape(b, s, H, DH)
        nw = s // WIN
        qw = q.reshape(b, nw, WIN, H, DH)
        kw = k.reshape(b, nw, WIN, H, DH)
        vw = v.reshape(b, nw, WIN, H, DH)
        s_loc = jnp.einsum('bnihd,bnjhd->bnhij', qw, kw) * scale
        p_loc = jax.nn.softmax(s_loc, axis=-1)
        o_loc = jnp.einsum('bnhij,bnjhd->bnihd', p_loc, vw).reshape(b, s, H, DH)
        n = s // DIL
        qd = q.reshape(b, n, DIL, H, DH)
        kd = k.reshape(b, n, DIL, H, DH)
        vd = v.reshape(b, n, DIL, H, DH)
        s_dil = jnp.einsum('bighd,bjghd->bghij', qd, kd) * scale
        p_dil = jax.nn.softmax(s_dil, axis=-1)
        o_dil = jnp.einsum('bghij,bjghd->bighd', p_dil, vd).reshape(b, s, H, DH)
        s_glb = jnp.einsum('bihd,bjhd->bhij', q, k) * scale
        p_glb = jax.nn.softmax(s_glb, axis=-1)
        o_glb = jnp.einsum('bhij,bjhd->bihd', p_glb, v)
        o = (o_loc + o_dil + o_glb) * (1.0 / 3.0)
        return o.reshape(b, s, d) @ w_out

    def _L0_ffn_ref(x, router_w, w_gate, w_up, w_down, sw_gate, sw_up, sw_down):
        import jax, jax.numpy as jnp
        import numpy as np
        D_MODEL = 128
        HIDDEN = 512
        NUM_ROUTED = 7
        TOP_K = 2

        def _swiglu(x_flat, wg, wu, wd):
            g = jnp.einsum('nd,edh->enh', x_flat, wg)
            u = jnp.einsum('nd,edh->enh', x_flat, wu)
            h = jax.nn.silu(g) * u
            return jnp.einsum('enh,ehd->end', h, wd)
        orig_shape = x.shape
        x_flat = x.reshape(-1, orig_shape[-1])
        N = x_flat.shape[0]
        logits = x_flat @ router_w.T
        top_vals, top_idx = jax.lax.top_k(logits, TOP_K)
        top_w = jax.nn.softmax(top_vals, axis=-1)
        combine = jnp.sum(jax.nn.one_hot(top_idx, NUM_ROUTED, dtype=x.dtype) * top_w[..., None], axis=1)
        routed_out = _swiglu(x_flat, w_gate, w_up, w_down)
        mixed = jnp.einsum('end,ne->nd', routed_out, combine)
        shared_out = _swiglu(x_flat, sw_gate, sw_up, sw_down)
        mixed = mixed + jnp.mean(shared_out, axis=0)
        return mixed.reshape(orig_shape)

    def _L1_attn_ref(x, W_qkv, W_out):
        import jax, jax.numpy as jnp
        import numpy as np
        D_MODEL = 128
        NUM_HEADS = 16
        HEAD_DIM = D_MODEL // NUM_HEADS
        THETA = 10000.0
        B, T = (4, 256)

        def _cos_sin(seq_len, head_dim, theta):
            freqs = 1.0 / theta ** (jnp.arange(0, head_dim, 2, dtype=jnp.float32) / head_dim)
            t = jnp.arange(seq_len, dtype=jnp.float32)
            angles = jnp.outer(t, freqs)
            return jnp.concatenate([jnp.cos(angles), jnp.sin(angles)], axis=-1)

        def _apply_rope(x, cos_sin):
            x1 = x[..., 0::2]
            x2 = x[..., 1::2]
            half = x.shape[-1] // 2
            cos = cos_sin[:, :half]
            sin = cos_sin[:, half:]
            out = jnp.stack([x1 * cos - x2 * sin, x1 * sin + x2 * cos], axis=-1)
            return out.reshape(x.shape)
        Bsz, Tlen, _ = x.shape
        qkv = jnp.einsum('bti,oi->bto', x, W_qkv)
        qkv = qkv.reshape(Bsz, Tlen, 3 * NUM_HEADS, HEAD_DIM).transpose(0, 2, 1, 3)
        q, k, v = jnp.split(qkv, 3, axis=1)
        cos_sin = _cos_sin(Tlen, HEAD_DIM, THETA)
        q = _apply_rope(q, cos_sin)
        k = _apply_rope(k, cos_sin)
        scores = jnp.einsum('bhqd,bhkd->bhqk', q, k) / np.sqrt(HEAD_DIM).astype(np.float32)
        causal = jnp.tril(jnp.ones((Tlen, Tlen), dtype=bool))
        scores = jnp.where(causal[None, None], scores, -jnp.inf)
        attn = jax.nn.softmax(scores, axis=-1)
        o = jnp.einsum('bhqk,bhkd->bhqd', attn, v)
        o = o.transpose(0, 2, 1, 3).reshape(Bsz, Tlen, D_MODEL)
        return jnp.einsum('bti,oi->bto', o, W_out)

    def _L1_ffn_ref(x, gate_W, gate_b, W1, b1, W2, b2, ln_gamma, ln_beta):
        import jax, jax.numpy as jnp
        import numpy as np
        D = 128
        E = 8
        H = 256
        TOP_K = 2
        ALPHA = 0.5
        LN_EPS = 1e-05

        def _experts_all(x, W1, b1, W2, b2):
            h = jax.nn.relu(jnp.einsum('bld,edh->eblh', x, W1) + b1[:, None, None, :])
            return jnp.einsum('eblh,ehd->ebld', h, W2) + b2[:, None, None, :]

        def _selected_expert(x, expert_idx, W1, b1, W2, b2):
            oh = jax.nn.one_hot(expert_idx, E, dtype=x.dtype)
            return jnp.einsum('ebld,ble->bld', _experts_all(x, W1, b1, W2, b2), oh)

        def _layer_norm(x, gamma, beta):
            mu = jnp.mean(x, axis=-1, keepdims=True)
            var = jnp.mean(jnp.square(x - mu), axis=-1, keepdims=True)
            return (x - mu) * jax.lax.rsqrt(var + LN_EPS) * gamma + beta
        residual = x
        gate_logits = jnp.einsum('bld,de->ble', x, gate_W) + gate_b
        gate_weights = jax.nn.softmax(gate_logits, axis=-1)
        topk_vals, topk_idx = jax.lax.top_k(gate_weights, TOP_K)
        boost = jax.lax.stop_gradient(x)
        outs = []
        for i in range(TOP_K):
            eo = _selected_expert(boost, topk_idx[:, :, i], W1, b1, W2, b2)
            outs.append(eo)
            if i < TOP_K - 1:
                boost = boost + ALPHA * jax.lax.stop_gradient(eo)
        fused = sum((topk_vals[:, :, i:i + 1] * outs[i] for i in range(TOP_K)))
        return _layer_norm(residual + fused, ln_gamma, ln_beta)
    x = L0_attn_x
    x = x + _L0_attn_ref(_layernorm(x, axis=-1), L0_attn_w_qkv, L0_attn_w_out)
    x = x + _L0_ffn_ref(_layernorm(x, axis=-1), L0_ffn_router_w, L0_ffn_w_gate, L0_ffn_w_up, L0_ffn_w_down, L0_ffn_sw_gate, L0_ffn_sw_up, L0_ffn_sw_down)
    x = x + _L1_attn_ref(_layernorm(x, axis=-1), L1_attn_W_qkv, L1_attn_W_out)
    x = x + _L1_ffn_ref(_layernorm(x, axis=-1), L1_ffn_gate_W, L1_ffn_gate_b, L1_ffn_W1, L1_ffn_b1, L1_ffn_W2, L1_ffn_b2, L1_ffn_ln_gamma, L1_ffn_ln_beta)
    return x

_drawn_inputs = setup_inputs


def setup_inputs(seed=0):
    import zlib

    import numpy as np

    out = dict(_drawn_inputs(seed))
    spreads = {'L1_ffn_gate_b': (0.0, 0.8),
     'L1_ffn_b1': (0.0, 0.8),
     'L1_ffn_b2': (0.0, 0.682),
     'L1_ffn_ln_gamma': (1.0, 0.2),
     'L1_ffn_ln_beta': (0.0, 0.356)}
    factors = {'L0_attn_w_qkv': 8.0,
     'L0_attn_w_out': 8.0,
     'L0_ffn_router_w': 7.604,
     'L0_ffn_w_gate': 6.483,
     'L0_ffn_w_up': 6.453,
     'L0_ffn_w_down': 6.461,
     'L0_ffn_sw_gate': 4.626,
     'L0_ffn_sw_up': 4.585,
     'L0_ffn_sw_down': 4.567,
     'L1_ffn_gate_W': 4.987,
     'L1_ffn_W1': 8.0,
     'L1_ffn_W2': 8.0}
    for name, (base, spread) in spreads.items():
        noise = np.random.default_rng([zlib.crc32(name.encode()), seed]).standard_normal(out[name].shape)
        drawn = base * np.exp(spread * noise) if base else spread * noise
        out[name] = jnp.asarray(drawn.astype(out[name].dtype))
    for name, factor in factors.items():
        out[name] = (out[name] * factor).astype(out[name].dtype)
    return out
```

```python
from contextlib import ExitStack

import concourse.bass as bass
from concourse import mybir

F32 = mybir.dt.float32
BF16 = mybir.dt.bfloat16
ALU = mybir.AluOpType
ACT = mybir.ActivationFunctionType
AX = mybir.AxisListType

P = 128
D = 128
S = 512
B = 8
NT = S // P
H = 16
DH = D // H
HG = 4
NG = H // HG
DIL = 4
SPLIT = 3
KR = SPLIT * SPLIT * DH
MR0 = 96
SCALE = float(DH) ** -0.5
VW = 32
OC = DH + 1
KC = 10
EPS = 1e-5


def wait_apart(eng, sem, value, passed):
    eng.wait_ge(sem, value)
    if not isinstance(value, int):
        eng.sem_inc(passed, 1)


class Turns:

    def __init__(self, prologue, first, middle, last, tail):
        self.order = {"prologue": prologue, "first": first, "middle": middle, "last": last, "tail": tail}
        self.before = {}
        n = 0
        for part, uses in self.order.items():
            self.before[part] = n
            n += len(uses) * (B - 2 if part == "middle" else 1)

    def number(self, part, b, use):
        n = self.before[part] + self.order[part].index(use)
        return n + (b - 1) * len(self.order["middle"]) if part == "middle" else n

    def previous(self, part, b, use):
        at = self.order[part].index(use)
        if at:
            return part, b, self.order[part][at - 1]
        if part == "prologue":
            return None
        names = list(self.order)
        before = names[names.index(part) - 1]
        last = self.order[before][-1]
        assert part != "middle" or last == self.order["middle"][-1]
        return before, b if part == "first" else b - 1, last


def attention(nc, X, const, w, scratch, causal):
    L = "c" if causal else "w"
    KINDS = 1 if causal else 3
    U = 8 if causal else 12
    R = U // HG
    SMU = HG * NT
    MROWS = KINDS * HG * SPLIT
    NE = 2 * HG
    VC = 0 if causal else KC

    with ExitStack() as ctx:
        def sb(name, shape, dt=F32):
            return ctx.enter_context(nc.sbuf_tensor(L + name, shape, dt))

        def sem(name):
            return ctx.enter_context(nc.semaphore(L + name))

        QS = sb("qs", [P, H, S], BF16)
        KS = sb("ks", [P, H, S], BF16)
        ML = sb("ml", [SPLIT, 2, 2 * HG, S], BF16)
        E = sb("e", [P, NE, 2 * S])
        V = sb("v", [P, NT, H, 2 * VC + VW])
        VP = V if causal else sb("vp", [P, DIL, H, VW])
        VS = sb("vs", [P, 2, NT, D])
        stats = sb("stats", [P, NT, 6])
        mv = sb("mv", [P, NT, 2])
        rstd = sb("rstd", [P, NT])
        xn = sb("xn", [P, NT, D])
        xnT = sb("xnT", [P, S])
        QK = sb("qk", [P, 2, S])
        QR = sb("qr", [P, 2, S])
        PT = sb("pt", [P, 2, SPLIT, S], BF16)
        TQ = sb("tq", [P, 2, S])
        M = sb("m", [P, HG, NT, NT * DIL])
        MD = sb("md", [P, HG, NT, NT * DIL])
        NM = sb("nm", [P, KINDS * HG, NT])
        NR = sb("nr", [P, KINDS * HG, NT])
        MT = sb("mt", [P, NT, MROWS], BF16)
        MR = sb("mr", [MROWS, S], BF16)
        OS = sb("os", [P, 2, S])
        RL = sb("rl", [P, NT, KINDS * HG, 1])
        PR = sb("pr", [P, NT, KINDS * HG, DH])
        ON = sb("on", [P, NT, D])
        OT = sb("ot", [P, S])

        ST = ctx.enter_context(nc.psum_tensor(L + "st", [P, 2, 2 * S], F32))
        SM = ctx.enter_context(nc.psum_tensor(L + "sm", [P, 2, S], F32))
        OA = ctx.enter_context(nc.psum_tensor(L + "oa", [P, S], F32))
        MI = ctx.enter_context(nc.psum_tensor(L + "mi", [P, S], F32))

        s_zero = sem("zero")
        s_init = sem("init")
        s_ln = sem("ln")
        s_bn = sem("bn")
        s_pow = sem("pow")
        s_pj = sem("pj")
        s_vs = sem("vs")
        s_rope = sem("rope")
        s_xt = sem("xt")
        s_pa = [sem("paq"), sem("pak")]
        s_pt = [sem("ptq"), sem("ptk")]
        s_pw = [sem("pwq"), sem("pwk")]
        s_rd = [sem(f"rd{g}") for g in range(NG)]
        s_vc = sem("vc")
        s_sm = sem("sm")
        s_mx = sem("mx")
        s_mp = sem("mp")
        s_ms = sem("ms")
        s_mr = sem("mr")
        s_mw = sem("mw")
        s_ml = sem("ml")
        s_st = sem("st")
        s_ex = sem("ex")
        s_pv = sem("pv")
        s_ev = sem("ev")
        s_no = sem("no")
        s_ot = sem("ot")
        s_res = sem("res")
        s_full = sem("full")
        MRD = 1 if causal else 2
        NNO = 2 if causal else 3
        NV = 1 if causal else 2
        NPT = 3 if causal else 2

        passed = sem("passed")
        sdram, mdram = scratch

        def slot(part, g):
            ev = []
            has_prev = not (part == "first" and g == 0)
            has1 = not (part == "last" and g == NG - 1)
            has2 = not (part == "last" and g >= NG - 2)
            has_next = part != "last"
            half = U // 2
            cuts = [round(i * (SMU // 2) / half) for i in range(half + 1)]
            at = {}

            def put(i, *steps):
                at.setdefault(i, []).extend(steps)

            if g == 0:
                put(-1, ("stacks", 0, 3))
            if has_next and g == 2:
                put(0, ("stacks", 1, 0), ("stacks", 1, 1))
            if has_next and g == 3:
                put(0, ("stacks", 1, 2))
            if has_prev:
                put(1, ("pv", -1, R - 1))
                put(3 if not causal else 2, ("evac", -1))
                put(4 if not causal else 3, ("sel", -1))
            put(5, ("pv", 0, 0))
            if not causal:
                put(9, ("pv", 0, 1))
            if has1:
                put(half - 1, ("maxima", 1))
                put(7 if not causal else 5, ("rows", 1))
            if g == 0 and part != "first":
                put(8 if not causal else 6, ("heads_T", -1))
                put(10 if not causal else 7, ("out_proj", -1))
            if has_next:
                if g == 0:
                    put(9 if not causal else 6, ("norm_stats", 1))
                    put(11 if not causal else 7, ("norm_rows", 1))
                if g == 1:
                    if causal:
                        put(0, ("xT", 1))
                        put(1, ("proj", 1, 0))
                        put(2, ("rot", 1, 0))
                        put(2, ("parts", 1, 0))
                        put(3, ("part1", 1, 0))
                        put(4, ("proj", 1, 1), ("rot", 1, 1), ("parts", 1, 1))
                        put(4, ("part2", 1, 0))
                        put(5, ("part1", 1, 1), ("parts_out", 1, 0))
                        put(6, ("part2", 1, 1))
                        put(7, ("parts_out", 1, 1))
                    else:
                        put(0, ("xT", 1))
                        put(2, ("proj", 1, 0))
                        put(3, ("part1", 1, 0), ("parts", 1, 0))
                        put(4, ("part2", 1, 0))
                        put(5, ("proj", 1, 1))
                        put(6, ("part1", 1, 1), ("parts", 1, 1), ("parts_out", 1, 0))
                        put(8, ("part2", 1, 1))
                        put(9, ("parts_out", 1, 1))
                if g == 2:
                    put(1, ("values", 1, 0))
                    if not causal:
                        put(9, ("values", 1, 1))
                if g == 3:
                    put(0, ("vcopy", 1, 0), ("vcopy", 1, 1))
            if g == 0:
                put(half, ("vcopy", 0, 2))
            if g == 1:
                put(half, ("vcopy", 0, 3))
            ev += at.get(-1, [])
            for i in range(U):
                ev.append(("scores", 0, i))
                if i < half and has1:
                    ev += [("smax", 1, SMU // 2 + j) for j in range(cuts[i], cuts[i + 1])]
                if i >= half and has2:
                    ev += [("smax", 2, j) for j in range(cuts[i - half], cuts[i - half + 1])]
                ev += at.get(i, [])
            return ev

        prep = [("norm_stats", 0), ("norm_rows", 0), ("xT", 0)]
        for side in range(2):
            prep.append(("proj", 0, side))
            if causal:
                prep.append(("rot", 0, side))
            prep += [("part1", 0, side), ("parts", 0, side), ("part2", 0, side), ("parts_out", 0, side)]
        prep += [("stacks", 0, 0), ("stacks", 0, 1), ("stacks", 0, 2), ("values", 0, 0)]
        if not causal:
            prep.append(("values", 0, 1))
        prep += [("vcopy", 0, 0), ("vcopy", 0, 1)]
        prep += [("smax", 0, j) for j in range(SMU)]
        prep += [("maxima", 0), ("rows", 0)]
        prep += [("smax", 1, j) for j in range(SMU // 2)]
        parts = {
            "prologue": [(0, e) for e in prep],
            "tail": [(NG, e) for e in [("pv", -1, R - 1), ("evac", -1), ("sel", -1), ("heads_T", -1),
                                      ("out_proj", -1)]],
        }
        for part in ("first", "middle", "last"):
            parts[part] = [(g, e) for g in range(NG) for e in slot(part, g)]

        SEQ = {"norm_stats", "norm_rows", "xT", "proj", "rot", "part1", "part2", "parts", "parts_out", "stacks", "values",
               "vcopy", "heads_T", "out_proj"}
        BANK = {"xT", "proj", "rot", "values", "rows", "sel", "heads_T", "out_proj"}
        turns = Turns(*[[(g, e) for g, e in parts[p] if e[0] in BANK] for p in
                        ("prologue", "first", "middle", "last", "tail")])

        def place(g, e, b, part):
            name, off = e[0], e[1]
            if name in SEQ:
                return (b + off,)
            gg = (0 if part == "tail" else g) + off
            return b * NG + gg, gg % NG, b + gg // NG

        def emptied(part, b, use):
            found = turns.previous(part, b, use)
            if found is None:
                return None
            part, b, (g, e) = found
            n = place(g, e, b, part)[0]
            return {
                "xT": lambda: (s_xt, n + 1),
                "proj": lambda: (s_rope, 4 * n + 2 * e[2] + 1) if causal else (s_pj, 2 * n + e[2] + 1),
                "rot": lambda: (s_rope, 4 * n + 2 * e[2] + 2),
                "values": lambda: (s_vs, NV * n + e[2] + 1),
                "rows": lambda: (s_mr, n + 1),
                "sel": lambda: (s_no, NNO * n + 2),
                "heads_T": lambda: (s_ot, n + 1),
                "out_proj": lambda: (s_res, n + 1),
            }[e[0]]()

        def walk(eng, handlers):
            def run(part, b):
                for g, e in parts[part]:
                    if e[0] not in handlers:
                        continue
                    turn = None
                    if e[0] in BANK and eng is nc.tensor:
                        free = emptied(part, b, (g, e))
                        if free:
                            eng.wait_ge(*free)
                    elif e[0] in BANK:
                        turn = turns.number(part, b, (g, e))
                    handlers[e[0]](*place(g, e, b, part), turn, *e[2:])

            run("prologue", 0)
            run("first", 0)
            with eng.Fori(1, B - 1) as b:
                run("middle", b)
            run("last", B - 1)
            run("tail", B)

        def window(x, t):
            n = P // DIL
            return x.rearrange("p (f i) -> p f i", f=DIL)[:, :, t * n:(t + 1) * n]

        def e_slot(g, i):
            return (U * g + i) % NE

        def cols(r):
            a, c = 2 * r, 2 * r + 1
            return [(a, 0, S - a * P), (c, S - a * P, S - c * P)]

        block = ctx.enter_context(nc.Block())

        @block.tensor
        def _(pe):
            pe.wait_ge(s_init, 2 * NV)

            def xT(b, turn):
                pe.wait_ge(s_ln, 2 * b + 2)
                for t in range(NT):
                    m = pe.transpose(MI[:, t * P:(t + 1) * P], xn[:, t, :], const["ident"])
                m.then_inc(s_full, 1)

            def proj(b, turn, side):
                pe.wait_ge(s_xt, b + 1)
                pe.matmul(MI[:, :], w["qkv"][:, side * D:(side + 1) * D], xnT[:, :], start=True, stop=True
                          ).then_inc(s_full, 1)

            def rot(b, turn, side):
                pe.matmul(MI[:, :], w["rot"][:, side * D:(side + 1) * D], xnT[:, :], start=True, stop=True
                          ).then_inc(s_full, 1)

            def values(b, turn, which):
                for t in range(NT):
                    tok = xnT[:, t * P:(t + 1) * P] if which == 0 else xnT[:, t::DIL]
                    m = pe.matmul(MI[:, t * P:(t + 1) * P], tok, w["qkv"][:, 2 * D:3 * D], start=True, stop=True)
                m.then_inc(s_full, 1)

            def smax(n, g, b, turn, j):
                h, t = g * HG + j // NT, j % NT
                if j == 0:
                    pe.wait_ge(s_rd[g], 32 * b + 32)
                if not (isinstance(n, int) and n == 0 and j < 2):
                    pe.wait_ge(s_mx, SMU * n + j - 1)
                keys = (t + 1) * P if causal else S
                m = pe.matmul(SM[:, j % 2, 0:keys], QS[0:MR0, h, t * P:(t + 1) * P], KS[0:MR0, h, 0:keys],
                              start=True, stop=not causal, skip_group_check=True)
                if causal:
                    m = pe.matmul(SM[:, j % 2, t * P:keys], const["ident_b"], const["mask_q_b"], start=False, stop=True,
                                  skip_group_check=True)
                m.then_inc(s_sm, 1)

            def rows(n, g, b, turn):
                wait_apart(pe, s_ms, 4 * n + 4, passed)
                out = MI[0:MROWS, 0:S // 2].bitcast(BF16)
                for t in range(NT):
                    m = pe.transpose(out[:, t * P:(t + 1) * P], MT[:, t, :], const["ident_b"])
                m.then_inc(s_full, 1)

            def scores(n, g, b, turn, i):
                hs = i % HG
                h = g * HG + hs
                u = U * g + i
                if i == 0:
                    pe.wait_ge(s_ml, 16 * MRD * (n + 1))
                if not (isinstance(n, int) and n == 0 and i < 2):
                    pe.wait_ge(s_ex, U * n + i - 1)
                st = ST[:, u % 2, :]
                if causal:
                    for kb, at, width in cols(i // HG):
                        pe.matmul(st[:, at:at + width], KS[:, h, kb * P:(kb + 1) * P], QS[:, h, kb * P:S],
                                  start=True, stop=False, skip_group_check=True)
                        m = pe.matmul(st[:, at:at + P], const["ident_b"], const["mask_k_b"], start=False, stop=True,
                                      skip_group_check=True)
                elif i < HG:
                    for kind in range(2):
                        at = kind * S
                        pe.matmul(st[:, at:at + S], const["ones_b"][0:SPLIT, :], ML[:, g % 2, kind * HG + hs, :],
                                  start=True, stop=False, skip_group_check=True)
                        for t in range(NT):
                            q, k, out = QS[0:MR0, h, :], KS[0:MR0, h, :], st[:, at:at + S]
                            if kind == 0:
                                q, k, out = window(q, t), k[:, t * P:(t + 1) * P], window(out, t)
                            else:
                                q, k, out = q[:, t * P:(t + 1) * P], k[:, t::DIL], out[:, t * P:(t + 1) * P]
                            m = pe.matmul(out, k, q, start=False, stop=(t == NT - 1), skip_group_check=True)
                else:
                    for c in range(2):
                        kb = 2 * (i // HG - 1) + c
                        m = pe.matmul(st[:, c * S:(c + 1) * S], KS[:, h, kb * P:(kb + 1) * P], QS[:, h, :],
                                      start=True, stop=True)
                m.then_inc(s_st, 1)

            def pv(n, g, b, turn, r):
                pe.wait_ge(s_ex, U * n + HG * (r + 1))
                if r == 0:
                    pe.wait_ge(s_vc, n + 1)
                    if not (isinstance(n, int) and n == 0):
                        pe.wait_ge(s_ev, n)
                if not causal and r == 0:
                    for kind in range(2):
                        for t in range(NT):
                            for hs in range(HG):
                                out = OA[VW * hs:VW * (hs + 1), :]
                                e = E[:, e_slot(g, hs), kind * S:(kind + 1) * S]
                                if kind == 0:
                                    out, e = window(out, t), window(e, t)
                                    val = V[:, t, g * HG + hs, 2 * VC:2 * VC + VW]
                                else:
                                    out, e = out[:, t * P:(t + 1) * P], e[:, t * P:(t + 1) * P]
                                    val = VP[:, t, g * HG + hs, :]
                                m = pe.matmul(out, val, e, start=(kind == 0 and t == 0), stop=False,
                                              skip_group_check=True)
                else:
                    blocks = cols(r) if causal else [(2 * (r - 1) + c, c * S, S) for c in range(2)]
                    for kb, at, width in blocks:
                        for hs in range(HG):
                            m = pe.matmul(OA[VW * hs:VW * (hs + 1), S - width:S], V[:, kb, g * HG + hs, 0:VW],
                                          E[:, e_slot(g, HG * r + hs), at:at + width],
                                          start=(causal and kb == 0), stop=(kb == NT - 1), skip_group_check=True)
                m.then_inc(s_pv, 1)

            def sel(n, g, b, turn):
                pe.wait_ge(s_ev, n + 1)
                c = KINDS * HG * OC
                for t in range(NT):
                    m = pe.matmul(MI[:, c * t:c * (t + 1)], OS[:, g % 2, t * P:(t + 1) * P], const["pick"][:, 0:c],
                                  start=True, stop=True, skip_group_check=True)
                m.then_inc(s_full, 1)

            def heads_T(b, turn):
                pe.wait_ge(s_no, NNO * NG * (b + 1))
                for t in range(NT):
                    m = pe.transpose(MI[:, t * P:(t + 1) * P], ON[:, t, :], const["ident"])
                m.then_inc(s_full, 1)

            def out_proj(b, turn):
                pe.wait_ge(s_ot, b + 1)
                for t in range(NT):
                    m = pe.matmul(MI[:, t * P:(t + 1) * P], OT[:, t * P:(t + 1) * P], w["out"], start=True, stop=True)
                m.then_inc(s_full, 1)

            walk(pe, dict(xT=xT, proj=proj, rot=rot, values=values, smax=smax, rows=rows, scores=scores, pv=pv,
                          sel=sel, heads_T=heads_T, out_proj=out_proj))

        @block.scalar
        def _(act):
            def xT(b, turn):
                if not (isinstance(b, int) and b == 0):
                    act.wait_ge(s_vs, NV * b)
                lay(turn, xnT[:, :], s_xt)

            def lay(turn, out, done, order=None):
                got = MI[:, :]
                if order and not causal:
                    out, got = order(out, got)
                act.wait_ge(s_full, turn + 1)
                act.activation(out, got, ACT.Copy).then_inc(done, 1)

            def to_phases(out, got):
                return out.rearrange("p (f i) -> p f i", f=DIL), got.rearrange("p (i f) -> p f i", f=DIL)

            def from_phases(out, got):
                return out.rearrange("p (i f) -> p f i", f=DIL), got.rearrange("p (f i) -> p f i", f=DIL)

            def proj(b, turn, side):
                if causal:
                    return
                if not (isinstance(b, int) and b == 0):
                    act.wait_ge(s_pt[side], NPT * b)
                lay(turn, QK[:, side, :], s_pj, None if side else to_phases)

            def part1(b, turn, side):
                if causal:
                    act.wait_ge(s_pt[side], NPT * b + 1)
                else:
                    act.wait_ge(s_pj, 2 * b + side + 1)
                if not (isinstance(b, int) and b == 0):
                    act.wait_ge(s_pw[side], 16 * SPLIT * SPLIT * b)
                act.activation(PT[:, side, 0, :], QK[:, side, :], ACT.Copy).then_inc(s_pa[side], 1)

            def part2(b, turn, side):
                act.wait_ge(s_pt[side], NPT * b + NPT - 1)
                act.activation(PT[:, side, 1, :], QR[:, side, :], ACT.Copy).then_inc(s_pa[side], 1)

            def values(b, turn, which):
                if not (isinstance(b, int) and b == 0):
                    act.wait_ge(s_vc, NG * b)
                lay(turn, VS[:, which, :, :].rearrange("p t d -> p (t d)"), s_vs)

            def scores(n, g, b, turn, i):
                act.wait_ge(s_st, U * n + i + 1)
                r = i // HG
                if not (isinstance(n, int) and U * n + i < NE):
                    act.wait_ge(s_pv, R * n + r - 1)
                width = (sum(c[2] for c in cols(r)) if causal else 2 * S)
                act.activation(E[:, e_slot(g, i), 0:width], ST[:, (U * g + i) % 2, 0:width], ACT.Exp, scale=SCALE
                               ).then_inc(s_ex, 1)

            def evac(n, g, b, turn):
                act.wait_ge(s_pv, R * n + R)
                if not (isinstance(n, int) and n < 2):
                    act.wait_ge(s_no, NNO * (n - 1))
                act.activation(OS[:, g % 2, :], OA[:, :], ACT.Copy).then_inc(s_ev, 1)

            def heads_T(b, turn):
                lay(turn, OT[:, :], s_ot, from_phases)

            walk(act, dict(xT=xT, proj=proj, part1=part1, part2=part2, values=values, scores=scores, evac=evac, heads_T=heads_T))

        @block.vector
        def _(dve):
            def norm_stats(b, turn):
                for t in range(NT):
                    dve.bn_stats(stats[:, t, :], X[:, b * NT + t, :]).then_inc(s_bn, 1)
                wait_apart(dve, s_bn, NT * (b + 1), passed)
                for t in range(NT):
                    m = dve.bn_aggr(mv[:, t, :], stats[:, t, :])
                m.then_inc(s_ln, 1)

            def norm_rows(b, turn):
                dve.wait_ge(s_pow, 2 * b + 2)
                if not (isinstance(b, int) and b == 0):
                    dve.wait_ge(s_xt, b)
                for t in range(NT):
                    m = dve.tensor_scalar(xn[:, t, :], X[:, b * NT + t, :], mv[:, t, 0:1], rstd[:, t:t + 1],
                                          ALU.subtract, ALU.mult)
                m.then_inc(s_ln, 1)

            def rotate(b, turn, side, second):
                dve.wait_ge(s_full, turn + 1)
                out = TQ[:, 0, :] if not second else TQ[:, 1, :]
                if side:
                    dve.wait_ge(s_pt[0], NPT * b + 1)
                elif not (isinstance(b, int) and b == 0):
                    dve.wait_ge(s_pt[1], NPT * (b - 1) + 1)
                dve.tensor_tensor(out, MI[:, :], const["sin"] if second else const["cos"], ALU.mult
                                  ).then_inc(s_rope, 1)

            def proj(b, turn, side):
                if causal:
                    rotate(b, turn, side, 0)

            def rot(b, turn, side):
                rotate(b, turn, side, 1)

            def smax(n, g, b, turn, j):
                hs, t = j // NT, j % NT
                dve.wait_ge(s_sm, SMU * n + j + 1)
                if causal and j == 0 and not (isinstance(n, int) and n == 0):
                    dve.wait_ge(s_ms, 4 * n)
                if causal:
                    dve.tensor_reduce(NM[:, hs, t:t + 1], SM[:, j % 2, 0:(t + 1) * P], AX.X, ALU.max, negate=True
                                      ).then_inc(s_mx, 1)
                else:
                    dve.tensor_reduce(M[:, hs, t, :].rearrange("p (w f) -> p w f", f=DIL),
                                      SM[:, j % 2, :].rearrange("p (w i f) -> p w f i", w=NT, f=DIL), AX.X, ALU.max
                                      ).then_inc(s_mx, 1)

            def maxima(n, g, b, turn):
                if causal:
                    return
                dve.wait_ge(s_mx, SMU * (n + 1))
                if not (isinstance(n, int) and n == 0):
                    dve.wait_ge(s_ms, 4 * n)
                flat = M[:, :, :, :].rearrange("p h t k -> p (h t) k")
                dve.tensor_reduce(NM[:, 0:HG, :].rearrange("p h t -> p (h t)"), flat, AX.X, ALU.max, negate=True
                                  ).then_inc(s_mp, 1)
                dve.tensor_tensor(MD[:, :, :, :].rearrange("p h t k -> p (h t) k"), flat,
                                  const["window"].rearrange("p (a k) -> p a k", a=1).broadcast_to([P, HG * NT, NT * DIL]),
                                  ALU.min).then_inc(s_mp, 1)
                step = NT * DIL
                own = bass.AP(M, 0, [[HG * NT * step, P], [NT * step, HG], [step + 1, DIL], [DIL, NT]])
                dve.tensor_reduce(NM[:, 2 * HG:3 * HG, :], own, AX.X, ALU.max, negate=True).then_inc(s_mp, 1)
                dve.wait_ge(s_mp, 4 * n + 3)
                dve.tensor_reduce(NM[:, HG:2 * HG, :].rearrange("p h t -> p (h t)"),
                                  MD[:, :, :, :].rearrange("p h t k -> p (h t) k"), AX.X, ALU.max, negate=True
                                  ).then_inc(s_mp, 1)

            def rows(n, g, b, turn):
                dve.wait_ge(s_full, turn + 1)
                if not (isinstance(n, int) and n == 0):
                    dve.wait_ge(s_mw, 16 * n)
                dve.tensor_copy(MR[:, :], MI[0:MROWS, 0:S // 2].bitcast(BF16)).then_inc(s_mr, 1)

            def sel(n, g, b, turn):
                dve.wait_ge(s_full, turn + 1)
                k = KINDS * HG
                got = MI[:, 0:NT * k * OC].rearrange("p (t k c) -> p t k c", t=NT, k=k)
                dve.reciprocal(RL[:, :, :, :], got[:, :, :, DH:OC]).then_inc(s_no, 1)
                dve.wait_ge(s_no, NNO * n + 1)
                if not (isinstance(b, int) and b == 0):
                    dve.wait_ge(s_ot, b)
                out = ON[:, :, g * HG * DH:(g + 1) * HG * DH]
                to = out.rearrange("p t (h c) -> p t h c", h=HG) if causal else PR[:, :, :, :]
                dve.tensor_tensor(to, got[:, :, :, 0:DH], RL[:, :, :, :].broadcast_to([P, NT, k, DH]), ALU.mult
                                  ).then_inc(s_no, 1)
                if causal:
                    return
                dve.wait_ge(s_no, NNO * n + 2)
                dve.tensor_reduce(out, PR[:, :, :, :].rearrange("p t (k h) c -> p t (h c) k", k=KINDS), AX.X,
                                  ALU.add).then_inc(s_no, 1)

            def out_proj(b, turn):
                dve.wait_ge(s_full, turn + 1)
                now = X[:, bass.ds(b * NT, NT), :].rearrange("p t d -> p (t d)")
                dve.tensor_tensor(now, now, MI[:, :], ALU.add).then_inc(s_res, 1)

            walk(dve, dict(norm_stats=norm_stats, norm_rows=norm_rows, proj=proj, rot=rot, smax=smax, maxima=maxima,
                           rows=rows, sel=sel, out_proj=out_proj))

        @block.gpsimd
        def _(pool):
            pool.memset(KS[:, :, :], 1.0).then_inc(s_zero, 1)
            pool.memset(QS[:, :, :], 0.0).then_inc(s_zero, 1)
            layouts = ((V, 2 * VC),) if causal else ((V, 2 * VC), (VP, KC))
            for val, _ in layouts:
                pool.memset(val[:, :, :, :], 0.0).then_inc(s_init, 1)
            pool.wait_ge(s_init, NV)
            for val, c in layouts:
                pool.memset(val[:, :, :, c + DH:c + OC], float(KINDS)).then_inc(s_init, 1)

            def norm_rows(b, turn):
                wait_apart(pool, s_ln, 2 * b + 1, passed)
                pool.tensor_scalar(rstd[:, :], mv[:, :, 1], EPS, None, ALU.add).then_inc(s_pow, 1)
                pool.wait_ge(s_pow, 2 * b + 1)
                pool.tensor_tensor(rstd[:, :], rstd[:, :], const["minus_half"][:, 0:NT], ALU.pow).then_inc(s_pow, 1)

            def parts_(b, turn, side):
                q, r, pt = QK[:, side, :], QR[:, side, :], PT[:, side, :, :]
                if causal:
                    pool.wait_ge(s_rope, 4 * b + 2 * side + 2)
                    pool.tensor_tensor(q, TQ[:, 0, :], TQ[:, 1, :], ALU.add).then_inc(s_pt[side], 1)
                pool.wait_ge(s_pa[side], 2 * b + 1)
                pool.tensor_tensor(r, q, pt[:, 0, :], ALU.subtract).then_inc(s_pt[side], 1)
                pool.wait_ge(s_pa[side], 2 * b + 2)
                pool.tensor_tensor(pt[:, 2, :], r, pt[:, 1, :], ALU.subtract).then_inc(s_pt[side], 1)

            def vcopy(b, turn, g):
                pool.wait_ge(s_vs, NV * (b + 1))
                if not (isinstance(b, int) and b == 0):
                    wait_apart(pool, s_pv, R * (NG * (b - 1) + g + 1), passed)
                for which, (val, c) in enumerate(layouts):
                    m = pool.tensor_copy(val[:, :, g * HG:(g + 1) * HG, c:c + DH],
                                         VS[:, which, :, g * HG * DH:(g + 1) * HG * DH].rearrange(
                                             "p t (h c) -> p t h c", h=HG))
                m.then_inc(s_vc, 1)

            def maxima(n, g, b, turn):
                if not (isinstance(n, int) and n == 0):
                    pool.wait_ge(s_mr, n)
                if causal:
                    wait_apart(pool, s_mx, SMU * (n + 1), passed)
                else:
                    wait_apart(pool, s_mp, 4 * n + 4, passed)
                part = MT[:, :, :].rearrange("p t (k s) -> p s k t", s=SPLIT)
                pool.tensor_copy(part[:, 0], NM[:, :, :]).then_inc(s_ms, 1)
                pool.wait_ge(s_ms, 4 * n + 1)
                pool.tensor_tensor(NR[:, :, :], NM[:, :, :], part[:, 0], ALU.subtract).then_inc(s_ms, 1)
                wait_apart(pool, s_ms, 4 * n + 2, passed)
                pool.tensor_copy(part[:, 1], NR[:, :, :]).then_inc(s_ms, 1)
                pool.wait_ge(s_ms, 4 * n + 3)
                pool.tensor_tensor(part[:, 2], NR[:, :, :], part[:, 1], ALU.subtract).then_inc(s_ms, 1)

            walk(pool, dict(norm_rows=norm_rows, parts=parts_, vcopy=vcopy, maxima=maxima))

        @block.sync
        def _(sp):
            sp.wait_ge(s_zero, 2)

            def parts_out(b, turn, side):
                wait_apart(sp, s_pt[side], NPT * (b + 1), passed)
                if side == 0 and not (isinstance(b, int) and b == 0):
                    for g in range(NG):
                        wait_apart(sp, s_rd[g], 32 * b, passed)
                for a in range(SPLIT):
                    for c in range(SPLIT):
                        r = (a * SPLIT + c) * DH
                        sp.dma_start(sdram[side, r:r + DH].rearrange("d h n -> h d n"),
                                     PT[:, side, (a, c)[side], :]).then_inc(s_pw[side], 16)

            def stacks(b, turn, g):
                if not (isinstance(b, int) and b == 0):
                    wait_apart(sp, s_st, U * (NG * (b - 1) + g + 1), passed)
                for side, dst in ((0, QS), (1, KS)):
                    wait_apart(sp, s_pw[side], 16 * SPLIT * SPLIT * (b + 1), passed)
                    sp.dma_start(dst[0:KR, g * HG:(g + 1) * HG, :], sdram[side, :, g * HG:(g + 1) * HG, :]
                                 ).then_inc(s_rd[g], 16)

            def rows(n, g, b, turn):
                wait_apart(sp, s_mr, n + 1, passed)
                if not (isinstance(n, int) and n == 0):
                    wait_apart(sp, s_ml, 16 * MRD * n, passed)
                sp.dma_start(mdram, MR[:, :]).then_inc(s_mw, 16)
                wait_apart(sp, s_mw, 16 * (n + 1), passed)
                if not (isinstance(n, int) and n < 2):
                    wait_apart(sp, s_st, U * (n - 1), passed)
                rows_ = mdram.rearrange("(k s) n -> s k n", s=SPLIT)
                sp.dma_start(QS[MR0:MR0 + SPLIT, g * HG:(g + 1) * HG, :], rows_[:, 0:HG, :]).then_inc(s_ml, 16)
                if not causal:
                    sp.dma_start(ML[:, g % 2, :, :], rows_[:, HG:3 * HG, :]).then_inc(s_ml, 16)

            walk(sp, dict(parts_out=parts_out, stacks=stacks, rows=rows))


def constants():
    import numpy as np
    p = np.arange(P)
    big = np.float32(1e30)
    freqs = (1.0 / np.float32(10000.0) ** (np.arange(0, DH, 2, dtype=np.float32) / DH)).astype(np.float32)
    angle = np.outer(freqs[(p % DH) // 2], np.arange(S, dtype=np.float32)).astype(np.float32)
    pick = np.zeros((P, 3, HG, OC), np.float32)
    for k in range(3):
        for h in range(HG):
            for c in range(OC):
                pick[h * VW + KC * k + c, k, h, c] = 1.0
    parts = {
        "ident": np.eye(P, dtype=np.float32),
        "mask_q": np.where(p[None, :] <= p[:, None], np.float32(0), -big),
        "mask_k": np.where(p[:, None] <= p[None, :], np.float32(0), -big),
        "window": np.where(p[:, None] // (P // NT) == np.arange(NT * DIL)[None, :] // DIL, np.float32(3e38), np.float32(-3e38)),
        "pick": pick.reshape(P, 3 * HG * OC),
        "minus_half": np.full((P, NT), -0.5, np.float32),
        "ones": np.ones((P, P), np.float32),
        "column": np.tile(np.arange(8, dtype=np.float32), (P, 1)),
        "cos": np.cos(angle),
        "sin": np.sin(angle),
    }
    at, n = {}, 0
    for name, a in parts.items():
        at[name] = (n, n + a.shape[1])
        n += a.shape[1]
    return np.concatenate([a.astype(np.float32) for a in parts.values()], axis=1), at


def setup(nc, ctx, c_dram, at, x_dram, X, w0qkv, w0out, w1qkv, w1out):
    def sb(name, shape, dt=F32):
        return ctx.enter_context(nc.sbuf_tensor(name, shape, dt))

    C = sb("const", [P, c_dram.shape[1]])
    CB = sb("const_b", [P, 4 * P], BF16)
    W0 = sb("w0", [P, 3 * D])
    WO0 = sb("wo0", [P, D])
    W1 = sb("w1t", [P, 3 * D])
    WR1 = sb("w1r", [P, 2 * D])
    WO1 = sb("wo1", [P, D])
    const = {name: C[:, a:b] for name, (a, b) in at.items()}
    for i, name in enumerate(("ident", "mask_q", "mask_k", "ones")):
        const[name + "_b"] = CB[:, i * P:(i + 1) * P]
    with ExitStack() as inner:
        raw = inner.enter_context(nc.sbuf_tensor("w1raw", [P, 4, D], F32))
        ps = inner.enter_context(nc.psum_tensor("w1ps", [P, 4 * D], F32))
        s_c, s_x, s_w, s_raw, s_cb, s_t, s_v = (inner.enter_context(nc.semaphore("su_" + n)) for n in
                                          ("c", "x", "w", "raw", "cb", "t", "v"))
        block = inner.enter_context(nc.Block())

        @block.sync
        def _(sp):
            sp.dma_start(C[:, :], c_dram).then_inc(s_c, 16)
            sp.dma_start(X[:, 0:NT, :], x_dram[0].rearrange("(t p) d -> p t d", p=P)).then_inc(s_x, 16)
            sp.dma_start(raw[:, 0:3, :], w1qkv.rearrange("(t p) i -> p t i", p=P)).then_inc(s_raw, 16)
            sp.dma_start(raw[:, 3, :], w1out).then_inc(s_raw, 16)
            sp.dma_start(W0[:, :], w0qkv).then_inc(s_w, 16)
            sp.dma_start(WO0[:, :], w0out).then_inc(s_w, 16)
            for b in range(1, B):
                sp.dma_start(X[:, b * NT:(b + 1) * NT, :], x_dram[b].rearrange("(t p) d -> p t d", p=P)
                             ).then_inc(s_x, 16)
            sp.wait_ge(s_w, 32)
            sp.wait_ge(s_x, 16 * B)

        @block.vector
        def _(dve):
            dve.wait_ge(s_c, 16)
            for i, name in enumerate(("ident", "mask_q", "mask_k", "ones")):
                dve.tensor_copy(CB[:, i * P:(i + 1) * P], const[name]).then_inc(s_cb, 1)
            dve.wait_ge(s_t, 1)
            dve.tensor_copy(W1[:, :], ps[:, 0:3 * D]).then_inc(s_v, 1)
            dve.tensor_copy(WO1[:, :], ps[:, 3 * D:4 * D]).then_inc(s_v, 1)
            pairs = ps[:, 0:2 * D].rearrange("p (f two) -> p f two", two=2)
            turned = WR1[:, :].rearrange("p (f two) -> p f two", two=2)
            dve.tensor_scalar(turned[:, :, 0], pairs[:, :, 1], -1.0, None, ALU.mult).then_inc(s_v, 1)
            dve.tensor_copy(turned[:, :, 1], pairs[:, :, 0]).then_inc(s_v, 1)

        @block.tensor
        def _(pe):
            pe.wait_ge(s_c, 16)
            pe.wait_ge(s_raw, 32)
            for t in range(4):
                m = pe.transpose(ps[:, t * P:(t + 1) * P], raw[:, t, :], const["ident"])
            m.then_inc(s_t, 1)

    return const, {"qkv": W0[:, :], "out": WO0[:, :]}, {"qkv": W1[:, :], "rot": WR1[:, :], "out": WO1[:, :]}


NE0 = 7
F0 = 512
NX0 = NE0 + 1
HB0 = F0 // P
NE1 = 8
F1 = 256
HB1 = F1 // P
ROUNDS = 2
BOOST = 0.5
TOP = 8


class Norm:

    def __init__(self, nc, ctx, name, minus_half, passed):
        self.passed = passed
        self.half = minus_half
        self.stats = ctx.enter_context(nc.sbuf_tensor(name + "stats", [P, NT, 6], F32))
        self.mv = ctx.enter_context(nc.sbuf_tensor(name + "mv", [P, NT, 2], F32))
        self.rstd = ctx.enter_context(nc.sbuf_tensor(name + "rstd", [P, NT], F32))
        self.s_bn, self.s_mv, self.s_pow, self.s_out = (ctx.enter_context(nc.semaphore(name + n))
                                                        for n in ("bn", "mv", "pow", "out"))

    def vector_stats(self, dve, k, tile):
        for t in range(NT):
            dve.bn_stats(self.stats[:, t, :], tile(t)).then_inc(self.s_bn, 1)
        wait_apart(dve, self.s_bn, NT * (k + 1), self.passed)
        for t in range(NT):
            m = dve.bn_aggr(self.mv[:, t, :], self.stats[:, t, :])
        m.then_inc(self.s_mv, 1)

    def pool(self, pool, k):
        if not (isinstance(k, int) and k == 0):
            pool.wait_ge(self.s_out, k)
        wait_apart(pool, self.s_mv, k + 1, self.passed)
        pool.tensor_scalar(self.rstd[:, :], self.mv[:, :, 1], EPS, None, ALU.add).then_inc(self.s_pow, 1)
        pool.wait_ge(self.s_pow, 2 * k + 1)
        pool.tensor_tensor(self.rstd[:, :], self.rstd[:, :], self.half, ALU.pow).then_inc(self.s_pow, 1)

    def vector_rows(self, dve, k, tile, out):
        dve.wait_ge(self.s_pow, 2 * k + 2)
        for t in range(NT):
            m = dve.tensor_scalar(out(t), tile(t), self.mv[:, t, 0:1], self.rstd[:, t:t + 1],
                                  ALU.subtract, ALU.mult)
        m.then_inc(self.s_out, 1)


def top_two(dve, passed, sem, start, values, top, index, column):
    wait_apart(dve, sem, start, passed)
    for t in range(NT):
        dve.max(top[:, t, :], values[:, t, :]).then_inc(sem, 1)
    for t in range(NT):
        wait_apart(dve, sem, start + t + 1, passed)
        dve.max_index(index[:, t, :], top[:, t, :], values[:, t, :]).then_inc(sem, 1)
    dve.wait_ge(sem, start + 2 * NT)
    dve.tensor_copy(column, index[:, :, 0:2]).then_inc(sem, 1)
    return 2 * NT + 1


def mixture0(nc, X, const, router, gate, up, down, sgate, sup, sdown):
    with ExitStack() as ctx:
        def sb(name, shape, dt=F32):
            return ctx.enter_context(nc.sbuf_tensor("a" + name, shape, dt))

        def sem(name):
            return ctx.enter_context(nc.semaphore("a" + name))

        def ps(name, shape):
            return ctx.enter_context(nc.psum_tensor("a" + name, shape, F32))

        WG = sb("wg", [P, NX0, F0])
        WU = sb("wu", [P, NX0, F0])
        WD = sb("wd", [P, NX0, HB0, D])
        RW = sb("rw", [TOP, D])
        RT = sb("rt", [P, TOP])
        xn = sb("xn", [P, NT, D])
        xnT = sb("xnT", [P, S])
        LG = sb("lg", [P, NT, TOP])
        TV = sb("tv", [P, NT, TOP])
        TI = sb("ti", [P, NT, TOP], mybir.dt.uint32)
        IC = sb("ic", [P, NT, 2])
        EV = sb("ev", [P, NT, 1])
        W12 = sb("w12", [P, NT, 2])
        HOT = sb("hot", [P, 2, NT, TOP])
        CW = sb("cw", [P, NT, TOP])
        SG = sb("sg", [P, 2, S])
        HT = sb("ht", [P, 2, S])
        G = ps("g", [P, 2, S])
        U = ps("u", [P, 2, S])
        Y = ps("y", [P, 2, NT * D])
        TP = ps("tp", [P, S])
        RB = ps("rb", [P, NT, TOP])
        s_w = [sem(f"w{i}") for i in range(3)]
        s_rw = sem("rw")
        s_rt = sem("rt")
        s_rtc = sem("rtc")
        s_tp = sem("tp")
        s_xt = sem("xt")
        s_rb = sem("rb")
        s_r = sem("r")
        s_e = sem("e")
        s_gu = sem("gu")
        s_sg = sem("sg")
        s_h = sem("h")
        s_y = sem("y")
        s_c = sem("c")
        passed = sem("passed")
        norm = Norm(nc, ctx, "a", const["minus_half"][:, 0:NT], passed)
        K = NX0 * HB0
        STEPS = 2 * NT + 1 + 7
        block = ctx.enter_context(nc.Block())

        def walk(eng, prep, body):
            prep(0)
            with eng.Fori(0, B - 1) as b:
                body(b, lambda: prep(b + 1))
            body(B - 1, lambda: None)

        @block.sync
        def _(sp):
            sp.dma_start(RW[0:NE0, :], router).then_inc(s_rw, 16)
            for i, (dst, routed, shared) in enumerate(((WG, gate, sgate), (WU, up, sup))):
                sp.dma_start(dst[:, 0:NE0, :], routed.rearrange("e d h -> d e h")).then_inc(s_w[i], 16)
                sp.dma_start(dst[:, NE0:NX0, :], shared.rearrange("e d h -> d e h")).then_inc(s_w[i], 16)
            for e in range(NX0):
                src = down[e] if e < NE0 else sdown[0]
                sp.dma_start(WD[:, e, :, :], src.rearrange("(c h) d -> h c d", h=P)).then_inc(s_w[2], 16)

        @block.tensor
        def _(pe):
            pe.wait_ge(s_rw, 16)
            pe.transpose(TP[:, 0:NE0], RW[0:NE0, :], const["ident"][0:NE0, 0:NE0]).then_inc(s_rt, 1)
            pe.wait_ge(s_rtc, 1)
            for s, n in zip(s_w, (32, 32, 16 * NX0)):
                pe.wait_ge(s, n)

            def prep(b):
                pe.wait_ge(norm.s_out, b + 1)
                for t in range(NT):
                    m = pe.transpose(TP[:, t * P:(t + 1) * P], xn[:, t, :], const["ident"])
                m.then_inc(s_tp, 1)

            def body(b, prepare):
                pe.wait_ge(s_xt, b + 1)
                for t in range(NT):
                    m = pe.matmul(RB[:, t, :], xnT[:, t * P:(t + 1) * P], RT[:, :], start=(t == 0), stop=True,
                                  skip_group_check=True)
                m.then_inc(s_rb, 1)

                def down_(k):
                    e, c = k // HB0, k % HB0
                    if c == 0:
                        pe.wait_ge(s_c, b * NX0 + e + 1)
                    pe.wait_ge(s_h, b * K + k + 3)
                    for t in range(NT):
                        m = pe.matmul(Y[:, e % 2, t * D:(t + 1) * D], HT[:, k % 2, t * P:(t + 1) * P],
                                      WD[:, e, c, :], start=(c == 0 and t == 0), stop=(c == HB0 - 1),
                                      skip_group_check=True)
                    if c == HB0 - 1:
                        m.then_inc(s_y, 1)

                for k in range(K):
                    e, c = k // HB0, k % HB0
                    pe.wait_ge(s_h, b * K + k + 1)
                    for dst, wt in ((G, WG), (U, WU)):
                        m = pe.matmul(dst[:, k % 2, :], wt[:, e, c * P:(c + 1) * P], xnT[:, :], start=True, stop=True)
                    m.then_inc(s_gu, 1)
                    if k == K // 2:
                        prepare()
                    if k:
                        down_(k - 1)
                down_(K - 1)

            walk(pe, prep, body)

        @block.scalar
        def _(act):
            def body(b, prepare):
                act.wait_ge(s_tp, b + 1)
                act.wait_ge(s_gu, b * K) if not (isinstance(b, int) and b == 0) else None
                act.copy(xnT[:, :], TP[:, :]).then_inc(s_xt, 1)
                for k in range(K):
                    act.wait_ge(s_gu, b * K + k + 1)
                    act.activation(SG[:, k % 2, :], G[:, k % 2, :], ACT.Silu).then_inc(s_sg, 1)
                    if k == 1:
                        act.wait_ge(s_r, STEPS * b + 2 * NT + 3)
                        act.activation(EV[:, :, :], EV[:, :, :], ACT.Exp).then_inc(s_e, 1)

            body(0, lambda: None)
            with act.Fori(1, B) as b:
                body(b, lambda: None)

        @block.gpsimd
        def _(pool):
            norm.pool(pool, 0)
            with pool.Fori(1, B) as b:
                norm.pool(pool, b)

        @block.vector
        def _(dve):
            dve.memset(LG[:, :, :], -3e38).then_inc(s_rtc, 1)
            dve.memset(RT[:, :], 0.0).then_inc(s_h, 2)
            dve.wait_ge(s_h, 2)
            dve.wait_ge(s_rt, 1)
            dve.wait_ge(s_rtc, 1)
            dve.tensor_copy(RT[:, 0:NE0], TP[:, 0:NE0]).then_inc(s_rtc, 1)
            dve.memset(CW[:, :, :], 1.0).then_inc(s_c, 2)

            def rows(b):
                return lambda t: X[:, b * NT + t, :]

            def prep(b):
                norm.vector_stats(dve, b, rows(b))
                norm.vector_rows(dve, b, rows(b), lambda t: xn[:, t, :])

            def body(b, prepare):
                r0 = STEPS * b

                def step(n):
                    dve.wait_ge(s_r, r0 + n)

                def hidden(k):
                    dve.wait_ge(s_sg, b * K + k + 1)
                    dve.tensor_tensor(HT[:, k % 2, :], SG[:, k % 2, :], U[:, k % 2, :], ALU.mult).then_inc(s_h, 1)

                def expert(e):
                    dve.wait_ge(s_y, b * NX0 + e + 1)
                    dve.wait_ge(s_c, b * NX0 + e + 2)
                    if e == NE0:
                        now = X[:, bass.ds(b * NT, NT), :].rearrange("p t d -> p (t d)")
                        m = dve.tensor_tensor(now, now, Y[:, e % 2, :], ALU.add)
                    else:
                        for t in range(NT):
                            now = X[:, b * NT + t, :]
                            m = dve.scalar_tensor_tensor(now, Y[:, e % 2, t * D:(t + 1) * D], CW[:, t, e:e + 1], now,
                                                         ALU.mult, ALU.add)
                    m.then_inc(s_c, 1)

                def route_first():
                    dve.wait_ge(s_rb, b + 1)
                    dve.tensor_copy(LG[:, :, 0:NE0], RB[:, :, 0:NE0]).then_inc(s_r, 1)
                    top_two(dve, passed, s_r, r0 + 1, LG, TV, TI, IC[:, :, :])
                    dve.tensor_tensor(EV[:, :, 0], TV[:, :, 1], TV[:, :, 0], ALU.subtract).then_inc(s_r, 1)

                def route_second():
                    n = 2 * NT + 3
                    dve.wait_ge(s_e, b + 1)
                    dve.tensor_scalar(W12[:, :, 0:1], EV[:, :, :], 1.0, None, ALU.add).then_inc(s_r, 1)
                    step(n + 1)
                    dve.reciprocal(W12[:, :, 0:1], W12[:, :, 0:1]).then_inc(s_r, 1)
                    step(n + 2)
                    dve.tensor_tensor(W12[:, :, 1:2], W12[:, :, 0:1], EV[:, :, :], ALU.mult).then_inc(s_r, 1)
                    step(n + 3)
                    for j in range(2):
                        for t in range(NT):
                            m = dve.tensor_scalar(HOT[:, j, t, :], const["column"], IC[:, t, j:j + 1],
                                                  W12[:, t, j:j + 1], ALU.is_equal, ALU.mult)
                    m.then_inc(s_r, 1)
                    step(n + 4)
                    dve.tensor_tensor(CW[:, :, 0:NE0], HOT[:, 0, :, 0:NE0], HOT[:, 1, :, 0:NE0], ALU.add
                                      ).then_inc(s_r, 1)
                    step(n + 5)

                for k in range(K):
                    hidden(k)
                    if k == 0:
                        route_first()
                    if k == 2:
                        route_second()
                    if k >= HB0 and k % HB0 == 1:
                        expert(k // HB0 - 1)
                    if k == K // 4:
                        prepare()
                expert(NX0 - 1)

            walk(dve, prep, body)


def mixture1(nc, X, const, out_dram, gate_w, gate_b, w1, b1, w2, b2, gamma, beta):
    with ExitStack() as ctx:
        def sb(name, shape, dt=F32):
            return ctx.enter_context(nc.sbuf_tensor("b" + name, shape, dt))

        def sem(name):
            return ctx.enter_context(nc.semaphore("b" + name))

        def ps(name, shape):
            return ctx.enter_context(nc.psum_tensor("b" + name, shape, F32))

        KH = NE1 * HB1
        W1 = sb("w1", [P, NE1, F1])
        W2 = sb("w2", [P, NE1, HB1, D])
        GW = sb("gw", [P, NE1])
        GB = sb("gb", [P, NE1])
        BR = sb("br", [KH, P])
        B1 = sb("b1", [P, KH])
        B2 = sb("b2", [P, NE1, D])
        GA = sb("ga", [P, D])
        BE = sb("be", [P, D])
        xn = sb("xn", [P, NT, D])
        xnT = sb("xnT", [P, S])
        LG = sb("lg", [P, NT, NE1])
        MX = sb("mx", [P, NT, 1])
        TV = sb("tv", [P, NT, TOP])
        TI = sb("ti", [P, NT, TOP], mybir.dt.uint32)
        IC = sb("ic", [P, NT, 2])
        HOT = sb("hot", [P, 2, NT, NE1])
        BS = sb("bs", [P, NT, D])
        OR = sb("or", [P, 2, NT, D])
        BO = sb("bo", [P, NT, D])
        HT = sb("ht", [P, 2, S])
        F = sb("f", [P, NT, D])
        HP = ps("hp", [P, 2, S])
        Y = ps("y", [P, 2, NT * D])
        TP = ps("tp", [P, S])
        RB = ps("rb", [P, NT, NE1])
        BP = ps("bp", [P, KH])
        s_w1, s_w2 = sem("w1"), sem("w2")
        s_small = sem("small")
        s_bt = sem("bt")
        s_b1 = sem("b1")
        s_tp = sem("tp")
        s_xt = sem("xt")
        s_rb = sem("rb")
        s_r = sem("r")
        s_e = sem("e")
        s_hp = sem("hp")
        s_h = sem("h")
        s_y = sem("y")
        s_c = sem("c")
        s_bs = sem("bs")
        s_bo = sem("bo")
        s_f = sem("f")
        s_out = sem("dr")
        STEPS = 7 + 2 * NT + 1 + 1
        passed = sem("passed")
        norm = Norm(nc, ctx, "b", const["minus_half"][:, 0:NT], passed)
        block = ctx.enter_context(nc.Block())

        @block.sync
        def _(sp):
            sp.dma_start(GW[:, :], gate_w).then_inc(s_small, 16)
            sp.dma_start(GB[:, :], gate_b.partition_broadcast(P)).then_inc(s_small, 16)
            sp.dma_start(BR[:, :], b1.rearrange("e (c h) -> (e c) h", h=P)).then_inc(s_small, 16)
            sp.dma_start(B2[:, :, :], b2.rearrange("e d -> (e d)").partition_broadcast(P)).then_inc(s_small, 16)
            sp.dma_start(GA[:, :], gamma.partition_broadcast(P)).then_inc(s_small, 16)
            sp.dma_start(BE[:, :], beta.partition_broadcast(P)).then_inc(s_small, 16)
            sp.dma_start(W1[:, :, :], w1.rearrange("e d h -> d e h")).then_inc(s_w1, 16)
            sp.dma_start(W2[:, :, :, :], w2.rearrange("e (c h) d -> h e c d", h=P)).then_inc(s_w2, 16)
            for b in range(B):
                sp.wait_ge(s_f, 5 * b + 5)
                sp.dma_start(out_dram[b].rearrange("(t p) d -> p t d", p=P), X[:, b * NT:(b + 1) * NT, :]
                             ).then_inc(s_out, 16)
            sp.wait_ge(s_out, 16 * B)

        @block.tensor
        def _(pe):
            pe.wait_ge(s_small, 96)
            pe.transpose(BP[:, :], BR[:, :], const["ident"][0:KH, 0:KH]).then_inc(s_bt, 1)
            pe.wait_ge(s_b1, 1)
            pe.wait_ge(s_w1, 16)
            pe.wait_ge(s_w2, 16)

            with pe.Fori(0, B) as b:
                for r in range(ROUNDS):
                    u = b * ROUNDS + r
                    if r == 0:
                        pe.wait_ge(norm.s_out, 2 * b + 1)
                    else:
                        pe.wait_ge(s_bo, b + 1)
                    src = (xn, BO)[r]
                    for t in range(NT):
                        m = pe.transpose(TP[:, t * P:(t + 1) * P], src[:, t, :], const["ident"])
                    m.then_inc(s_tp, 1)
                    pe.wait_ge(s_xt, u + 1)
                    if r == 0:
                        for t in range(NT):
                            m = pe.matmul(RB[:, t, :], xnT[:, t * P:(t + 1) * P], GW[:, :], start=(t == 0), stop=True,
                                          skip_group_check=True)
                        m.then_inc(s_rb, 1)

                    def down_(k):
                        e, c = k // HB1, k % HB1
                        if c == 0:
                            pe.wait_ge(s_c, u * NE1 + e + 1)
                        pe.wait_ge(s_h, u * KH + k + 3)
                        for t in range(NT):
                            m = pe.matmul(Y[:, e % 2, t * D:(t + 1) * D], HT[:, k % 2, t * P:(t + 1) * P],
                                          W2[:, e, c, :], start=(c == 0 and t == 0), stop=(c == HB1 - 1),
                                          skip_group_check=True)
                        if c == HB1 - 1:
                            m.then_inc(s_y, 1)

                    for k in range(KH):
                        pe.wait_ge(s_h, u * KH + k + 1)
                        pe.matmul(HP[:, k % 2, :], W1[:, k // HB1, (k % HB1) * P:(k % HB1 + 1) * P], xnT[:, :],
                                  start=True, stop=True).then_inc(s_hp, 1)
                        if k:
                            down_(k - 1)
                    down_(KH - 1)

        @block.scalar
        def _(act):
            act.wait_ge(s_b1, 1)

            with act.Fori(0, B) as b:
                for r in range(ROUNDS):
                    u = b * ROUNDS + r
                    act.wait_ge(s_tp, u + 1)
                    act.copy(xnT[:, :], TP[:, :]).then_inc(s_xt, 1)
                    if r == 0:
                        act.wait_ge(s_r, STEPS * b + 3)
                        act.activation(LG[:, :, :], LG[:, :, :], ACT.Exp).then_inc(s_e, 1)
                    for k in range(KH):
                        act.wait_ge(s_hp, u * KH + k + 1)
                        act.activation(HT[:, k % 2, :], HP[:, k % 2, :], ACT.Relu, bias=B1[:, k:k + 1]).then_inc(s_h, 1)

        @block.gpsimd
        def _(pool):
            norm.pool(pool, 0)
            with pool.Fori(1, 2 * B) as k:
                norm.pool(pool, k)

        @block.vector
        def _(dve):
            dve.memset(TV[:, :, :], 0.0).then_inc(s_h, 2)
            dve.memset(MX[:, :, :], 0.0).then_inc(s_c, 2)
            dve.wait_ge(s_bt, 1)
            dve.tensor_copy(B1[:, :], BP[:, :]).then_inc(s_b1, 1)
            dve.wait_ge(s_small, 96)

            with dve.Fori(0, B) as b:
                def rows(t):
                    return X[:, b * NT + t, :]

                r0 = STEPS * b
                norm.vector_stats(dve, 2 * b, rows)
                norm.vector_rows(dve, 2 * b, rows, lambda t: xn[:, t, :])
                dve.wait_ge(s_rb, b + 1)
                dve.tensor_tensor(LG[:, :, :], RB[:, :, :], GB[:, :].rearrange("p (a e) -> p a e", a=1).broadcast_to(
                    [P, NT, NE1]), ALU.add).then_inc(s_r, 1)
                dve.wait_ge(s_r, r0 + 1)
                dve.tensor_reduce(MX[:, :, 0], LG[:, :, :], AX.X, ALU.max).then_inc(s_r, 1)
                dve.wait_ge(s_r, r0 + 2)
                dve.tensor_tensor(LG[:, :, :], LG[:, :, :], MX[:, :, :].broadcast_to([P, NT, NE1]), ALU.subtract
                                  ).then_inc(s_r, 1)
                dve.wait_ge(s_e, b + 1)
                dve.tensor_reduce(MX[:, :, 0], LG[:, :, :], AX.X, ALU.add).then_inc(s_r, 1)
                dve.wait_ge(s_r, r0 + 4)
                dve.reciprocal(MX[:, :, :], MX[:, :, :]).then_inc(s_r, 1)
                dve.wait_ge(s_r, r0 + 5)
                dve.tensor_tensor(LG[:, :, :], LG[:, :, :], MX[:, :, :].broadcast_to([P, NT, NE1]), ALU.mult
                                  ).then_inc(s_r, 1)
                top_two(dve, passed, s_r, r0 + 6, LG, TV, TI, IC[:, :, :])
                dve.wait_ge(s_r, r0 + 7 + 2 * NT)
                for j in range(2):
                    for t in range(NT):
                        m = dve.tensor_scalar(HOT[:, j, t, :], const["column"], IC[:, t, j:j + 1], None, ALU.is_equal)
                m.then_inc(s_r, 1)
                dve.memset(BS[:, 0, 0:1], 0.0).then_inc(s_r, 1)
                dve.wait_ge(s_r, r0 + STEPS)

                for r in range(ROUNDS):
                    u = b * ROUNDS + r
                    for e in range(NE1):
                        dve.wait_ge(s_c, u * NE1 + e + 2)
                        for t in range(NT):
                            hot = HOT[:, r, t, e:e + 1]
                            if e == 0:
                                m = dve.tensor_scalar(BS[:, t, :], B2[:, e, :], hot, None, ALU.mult)
                            else:
                                m = dve.scalar_tensor_tensor(BS[:, t, :], B2[:, e, :], hot, OR[:, r, t, :], ALU.mult,
                                                             ALU.add)
                        m.then_inc(s_bs, 1)
                        dve.wait_ge(s_bs, u * NE1 + e + 1)
                        dve.wait_ge(s_y, u * NE1 + e + 1)
                        for t in range(NT):
                            m = dve.scalar_tensor_tensor(OR[:, r, t, :], Y[:, e % 2, t * D:(t + 1) * D],
                                                         HOT[:, r, t, e:e + 1], BS[:, t, :], ALU.mult, ALU.add)
                        m.then_inc(s_c, 1)
                    dve.wait_ge(s_c, u * NE1 + NE1 + 2)
                    if r == 0:
                        dve.scalar_tensor_tensor(BO[:, :, :], OR[:, 0, :, :], BOOST, xn[:, :, :], ALU.mult, ALU.add
                                                 ).then_inc(s_bo, 1)
                for r in range(ROUNDS):
                    for t in range(NT):
                        m = dve.scalar_tensor_tensor(F[:, t, :], OR[:, r, t, :], TV[:, t, r:r + 1],
                                                     (xn, F)[r][:, t, :], ALU.mult, ALU.add)
                    m.then_inc(s_f, 1)
                    dve.wait_ge(s_f, 5 * b + r + 1)
                norm.vector_stats(dve, 2 * b + 1, lambda t: F[:, t, :])
                norm.vector_rows(dve, 2 * b + 1, lambda t: F[:, t, :], lambda t: F[:, t, :])
                dve.wait_ge(norm.s_out, 2 * b + 2)
                for i, (row, op) in enumerate(((GA, ALU.mult), (BE, ALU.add))):
                    wide = row[:, :].rearrange("p (a d) -> p a d", a=1).broadcast_to([P, NT, D])
                    dve.tensor_tensor(F[:, :, :], F[:, :, :], wide, op).then_inc(s_f, 1)
                    dve.wait_ge(s_f, 5 * b + 3 + i)
                now = X[:, bass.ds(b * NT, NT), :]
                dve.tensor_tensor(now, now, F[:, :, :], ALU.add).then_inc(s_f, 1)


def build(nc, c, x, w0qkv, w0out, router, gate, up, down, sgate, sup, sdown, w1qkv, w1out, gate_w, gate_b, w1, b1, w2, b2,
          gamma, beta, out):
    at = constants()[1]
    with ExitStack() as ctx:
        X = ctx.enter_context(nc.sbuf_tensor("X", [P, B * NT, D], F32))
        const, attn0, attn1 = setup(nc, ctx, c, at, x, X, w0qkv, w0out, w1qkv, w1out)
        parts = nc.dram_tensor("parts", [2, KR, H, S], BF16).ap()
        rows0 = nc.dram_tensor("rows0", [3 * HG * SPLIT, S], BF16).ap()
        rows1 = nc.dram_tensor("rows1", [HG * SPLIT, S], BF16).ap()
        attention(nc, X, const, attn0, (parts, rows0), False)
        mixture0(nc, X, const, router, gate, up, down, sgate, sup, sdown)
        attention(nc, X, const, attn1, (parts, rows1), True)
        mixture1(nc, X, const, out, gate_w, gate_b, w1, b1, w2, b2, gamma, beta)


INPUTS = ["L0_attn_x", "L0_attn_w_qkv", "L0_attn_w_out", "L0_ffn_router_w", "L0_ffn_w_gate", "L0_ffn_w_up",
          "L0_ffn_w_down", "L0_ffn_sw_gate", "L0_ffn_sw_up", "L0_ffn_sw_down", "L1_attn_W_qkv", "L1_attn_W_out",
          "L1_ffn_gate_W", "L1_ffn_gate_b", "L1_ffn_W1", "L1_ffn_b1", "L1_ffn_W2", "L1_ffn_b2", "L1_ffn_ln_gamma",
          "L1_ffn_ln_beta"]


def kernel(**inputs):
    import numpy as np
    import concourse.bacc as bacc
    from concourse.bass_utils import run_bass_kernel_spmd

    nc = bacc.Bacc("TRN2", target_bir_lowering=False, num_devices=1)
    arrays = {"constants": constants()[0]}
    for name in INPUTS:
        arrays[name] = np.ascontiguousarray(inputs[name])
    args = [nc.dram_tensor(name, a.shape, mybir.dt.from_np(a.dtype), kind="ExternalInput").ap()
            for name, a in arrays.items()]
    out = nc.dram_tensor("out", (B, S, D), F32, kind="ExternalOutput").ap()
    build(nc, *args, out)
    result = run_bass_kernel_spmd(nc, [arrays], core_ids=[0])
    return result.results[0]["out"]
```

```python
from contextlib import ExitStack

import concourse.bass as bass
from concourse import mybir

F32 = mybir.dt.float32
BF16 = mybir.dt.bfloat16
U32 = mybir.dt.uint32
I32 = mybir.dt.int32
ALU = mybir.AluOpType
ACT = mybir.ActivationFunctionType
AX = mybir.AxisListType

P = 128
D = 128
S = 512
B = 8
NT = S // P
H = 16
DH = D // H
HG = 4
NG = H // HG
DIL = 4
SPLIT = 3
KR = SPLIT * SPLIT * DH
MR0 = 96
SCALE = float(DH) ** -0.5
VW = 32
OC = DH + 1
KC = 10
EPS = 1e-5


def wait_apart(eng, sem, value, passed):
    eng.wait_ge(sem, value)
    if not isinstance(value, int):
        eng.sem_inc(passed, 1)


class Turns:

    def __init__(self, prologue, first, middle, last, tail):
        self.order = {"prologue": prologue, "first": first, "middle": middle, "last": last, "tail": tail}
        self.before = {}
        n = 0
        for part, uses in self.order.items():
            self.before[part] = n
            n += len(uses) * (B - 2 if part == "middle" else 1)

    def number(self, part, b, use):
        n = self.before[part] + self.order[part].index(use)
        return n + (b - 1) * len(self.order["middle"]) if part == "middle" else n

    def previous(self, part, b, use):
        at = self.order[part].index(use)
        if at:
            return part, b, self.order[part][at - 1]
        if part == "prologue":
            return None
        names = list(self.order)
        before = names[names.index(part) - 1]
        last = self.order[before][-1]
        assert part != "middle" or last == self.order["middle"][-1]
        return before, b if part == "first" else b - 1, last


def attention(nc, X, const, w, scratch, causal):
    L = "c" if causal else "w"
    KINDS = 1 if causal else 3
    U = 8 if causal else 12
    R = U // HG
    SMU = HG * NT
    MROWS = KINDS * HG * SPLIT
    NE = 2 * HG
    VC = 0 if causal else KC

    with nc.cleanup_on_exit(), ExitStack() as ctx:
        def sb(name, shape, dt=F32):
            return ctx.enter_context(nc.sbuf_tensor(L + name, shape, dt))

        def sem(name):
            return nc.alloc_semaphore(name=L + name)

        QS = sb("qs", [P, H, S], BF16)
        KS = sb("ks", [P, H, S], BF16)
        ML = sb("ml", [SPLIT, 2, 2 * HG, S], BF16)
        E = sb("e", [P, NE, 2 * S])
        V = sb("v", [P, NT, H, 2 * VC + VW])
        VP = V if causal else sb("vp", [P, DIL, H, VW])
        VS = sb("vs", [P, 2, NT, D])
        stats = sb("stats", [P, NT, 6])
        mv = sb("mv", [P, NT, 2])
        rstd = sb("rstd", [P, NT])
        xn = sb("xn", [P, NT, D])
        xnT = sb("xnT", [P, S])
        QK = sb("qk", [P, 2, S])
        QR = sb("qr", [P, 2, S])
        PT = sb("pt", [P, 2, SPLIT, S], BF16)
        TQ = sb("tq", [P, 2, S])
        M = sb("m", [P, HG, NT, NT * DIL])
        MD = sb("md", [P, HG, NT, NT * DIL])
        NM = sb("nm", [P, KINDS * HG, NT])
        NR = sb("nr", [P, KINDS * HG, NT])
        MT = sb("mt", [P, NT, MROWS], BF16)
        MR = sb("mr", [MROWS, S], BF16)
        OS = sb("os", [P, 2, S])
        RL = sb("rl", [P, NT, KINDS * HG, 1])
        PR = sb("pr", [P, NT, KINDS * HG, DH])
        ON = sb("on", [P, NT, D])
        OT = sb("ot", [P, S])

        ST = ctx.enter_context(nc.psum_tensor(L + "st", [P, 2, 2 * S], F32))
        SM = ctx.enter_context(nc.psum_tensor(L + "sm", [P, 2, S], F32))
        OA = ctx.enter_context(nc.psum_tensor(L + "oa", [P, S], F32))
        MI = ctx.enter_context(nc.psum_tensor(L + "mi", [P, S], F32))

        s_zero = sem("zero")
        s_init = sem("init")
        s_ln = sem("ln")
        s_bn = sem("bn")
        s_pow = sem("pow")
        s_pj = sem("pj")
        s_vs = sem("vs")
        s_rope = sem("rope")
        s_xt = sem("xt")
        s_pa = [sem("paq"), sem("pak")]
        s_pt = [sem("ptq"), sem("ptk")]
        s_pw = [sem("pwq"), sem("pwk")]
        s_rd = [sem(f"rd{g}") for g in range(NG)]
        s_vc = sem("vc")
        s_sm = sem("sm")
        s_mx = sem("mx")
        s_mp = sem("mp")
        s_ms = sem("ms")
        s_mr = sem("mr")
        s_mw = sem("mw")
        s_ml = sem("ml")
        s_st = sem("st")
        s_ex = sem("ex")
        s_pv = sem("pv")
        s_ev = sem("ev")
        s_no = sem("no")
        s_ot = sem("ot")
        s_res = sem("res")
        s_full = sem("full")
        MRD = 1 if causal else 2
        NNO = 2 if causal else 3
        NV = 1 if causal else 2
        NPT = 3 if causal else 2

        passed = sem("passed")
        sdram, mdram = scratch

        def slot(part, g):
            ev = []
            has_prev = not (part == "first" and g == 0)
            has1 = not (part == "last" and g == NG - 1)
            has2 = not (part == "last" and g >= NG - 2)
            has_next = part != "last"
            half = U // 2
            cuts = [round(i * (SMU // 2) / half) for i in range(half + 1)]
            at = {}

            def put(i, *steps):
                at.setdefault(i, []).extend(steps)

            if g == 0:
                put(-1, ("stacks", 0, 3))
            if has_next and g == 2:
                put(0, ("stacks", 1, 0), ("stacks", 1, 1))
            if has_next and g == 3:
                put(0, ("stacks", 1, 2))
            if has_prev:
                put(1, ("pv", -1, R - 1))
                put(3 if not causal else 2, ("evac", -1))
                put(4 if not causal else 3, ("sel", -1))
            put(5, ("pv", 0, 0))
            if not causal:
                put(9, ("pv", 0, 1))
            if has1:
                put(half - 1, ("maxima", 1))
                put(7 if not causal else 5, ("rows", 1))
            if g == 0 and part != "first":
                put(8 if not causal else 6, ("heads_T", -1))
                put(10 if not causal else 7, ("out_proj", -1))
            if has_next:
                if g == 0:
                    put(9 if not causal else 6, ("norm_stats", 1))
                    put(11 if not causal else 7, ("norm_rows", 1))
                if g == 1:
                    if causal:
                        put(0, ("xT", 1))
                        put(1, ("proj", 1, 0))
                        put(2, ("rot", 1, 0))
                        put(2, ("parts", 1, 0))
                        put(3, ("part1", 1, 0))
                        put(4, ("proj", 1, 1), ("rot", 1, 1), ("parts", 1, 1))
                        put(4, ("part2", 1, 0))
                        put(5, ("part1", 1, 1), ("parts_out", 1, 0))
                        put(6, ("part2", 1, 1))
                        put(7, ("parts_out", 1, 1))
                    else:
                        put(0, ("xT", 1))
                        put(2, ("proj", 1, 0))
                        put(3, ("part1", 1, 0), ("parts", 1, 0))
                        put(4, ("part2", 1, 0))
                        put(5, ("proj", 1, 1))
                        put(6, ("part1", 1, 1), ("parts", 1, 1), ("parts_out", 1, 0))
                        put(8, ("part2", 1, 1))
                        put(9, ("parts_out", 1, 1))
                if g == 2:
                    put(1, ("values", 1, 0))
                    if not causal:
                        put(9, ("values", 1, 1))
                if g == 3:
                    put(0, ("vcopy", 1, 0), ("vcopy", 1, 1))
            if g == 0:
                put(half, ("vcopy", 0, 2))
            if g == 1:
                put(half, ("vcopy", 0, 3))
            ev += at.get(-1, [])
            for i in range(U):
                ev.append(("scores", 0, i))
                if i < half and has1:
                    ev += [("smax", 1, SMU // 2 + j) for j in range(cuts[i], cuts[i + 1])]
                if i >= half and has2:
                    ev += [("smax", 2, j) for j in range(cuts[i - half], cuts[i - half + 1])]
                ev += at.get(i, [])
            return ev

        prep = [("norm_stats", 0), ("norm_rows", 0), ("xT", 0)]
        for side in range(2):
            prep.append(("proj", 0, side))
            if causal:
                prep.append(("rot", 0, side))
            prep += [("part1", 0, side), ("parts", 0, side), ("part2", 0, side), ("parts_out", 0, side)]
        prep += [("stacks", 0, 0), ("stacks", 0, 1), ("stacks", 0, 2), ("values", 0, 0)]
        if not causal:
            prep.append(("values", 0, 1))
        prep += [("vcopy", 0, 0), ("vcopy", 0, 1)]
        prep += [("smax", 0, j) for j in range(SMU)]
        prep += [("maxima", 0), ("rows", 0)]
        prep += [("smax", 1, j) for j in range(SMU // 2)]
        parts = {
            "prologue": [(0, e) for e in prep],
            "tail": [(NG, e) for e in [("pv", -1, R - 1), ("evac", -1), ("sel", -1), ("heads_T", -1),
                                      ("out_proj", -1)]],
        }
        for part in ("first", "middle", "last"):
            parts[part] = [(g, e) for g in range(NG) for e in slot(part, g)]

        SEQ = {"norm_stats", "norm_rows", "xT", "proj", "rot", "part1", "part2", "parts", "parts_out", "stacks", "values",
               "vcopy", "heads_T", "out_proj"}
        BANK = {"xT", "proj", "rot", "values", "rows", "sel", "heads_T", "out_proj"}
        turns = Turns(*[[(g, e) for g, e in parts[p] if e[0] in BANK] for p in
                        ("prologue", "first", "middle", "last", "tail")])

        def place(g, e, b, part):
            name, off = e[0], e[1]
            if name in SEQ:
                return (b + off,)
            gg = (0 if part == "tail" else g) + off
            return b * NG + gg, gg % NG, b + gg // NG

        def emptied(part, b, use):
            found = turns.previous(part, b, use)
            if found is None:
                return None
            part, b, (g, e) = found
            n = place(g, e, b, part)[0]
            return {
                "xT": lambda: (s_xt, n + 1),
                "proj": lambda: (s_rope, 4 * n + 2 * e[2] + 1) if causal else (s_pj, 2 * n + e[2] + 1),
                "rot": lambda: (s_rope, 4 * n + 2 * e[2] + 2),
                "values": lambda: (s_vs, NV * n + e[2] + 1),
                "rows": lambda: (s_mr, n + 1),
                "sel": lambda: (s_no, NNO * n + 2),
                "heads_T": lambda: (s_ot, n + 1),
                "out_proj": lambda: (s_res, n + 1),
            }[e[0]]()

        def walk(eng, handlers):
            def run(part, b):
                for g, e in parts[part]:
                    if e[0] not in handlers:
                        continue
                    turn = None
                    if e[0] in BANK and eng is nc.tensor:
                        free = emptied(part, b, (g, e))
                        if free:
                            eng.wait_ge(*free)
                    elif e[0] in BANK:
                        turn = turns.number(part, b, (g, e))
                    handlers[e[0]](*place(g, e, b, part), turn, *e[2:])

            run("prologue", 0)
            run("first", 0)
            with eng.Fori(1, B - 1) as b:
                run("middle", b)
            run("last", B - 1)
            run("tail", B)

        def window(x, t):
            n = P // DIL
            return x.rearrange("p (f i) -> p f i", f=DIL)[:, :, t * n:(t + 1) * n]

        def e_slot(g, i):
            return (U * g + i) % NE

        def cols(r):
            a, c = 2 * r, 2 * r + 1
            return [(a, 0, S - a * P), (c, S - a * P, S - c * P)]

        block = ctx.enter_context(nc.Block())

        @block.tensor
        def _(pe):
            pe.wait_ge(s_init, 2 * NV)

            def xT(b, turn):
                pe.wait_ge(s_ln, 2 * b + 2)
                for t in range(NT):
                    m = pe.transpose(MI[:, t * P:(t + 1) * P], xn[:, t, :], const["ident"])
                m.then_inc(s_full, 1)

            def proj(b, turn, side):
                pe.wait_ge(s_xt, b + 1)
                pe.matmul(MI[:, :], w["qkv"][:, side * D:(side + 1) * D], xnT[:, :], start=True, stop=True
                          ).then_inc(s_full, 1)

            def rot(b, turn, side):
                pe.matmul(MI[:, :], w["rot"][:, side * D:(side + 1) * D], xnT[:, :], start=True, stop=True
                          ).then_inc(s_full, 1)

            def values(b, turn, which):
                for t in range(NT):
                    tok = xnT[:, t * P:(t + 1) * P] if which == 0 else xnT[:, t::DIL]
                    m = pe.matmul(MI[:, t * P:(t + 1) * P], tok, w["qkv"][:, 2 * D:3 * D], start=True, stop=True)
                m.then_inc(s_full, 1)

            def smax(n, g, b, turn, j):
                h, t = g * HG + j // NT, j % NT
                if j == 0:
                    pe.wait_ge(s_rd[g], 32 * b + 32)
                if not (isinstance(n, int) and n == 0 and j < 2):
                    pe.wait_ge(s_mx, SMU * n + j - 1)
                keys = (t + 1) * P if causal else S
                m = pe.matmul(SM[:, j % 2, 0:keys], QS[0:MR0, h, t * P:(t + 1) * P], KS[0:MR0, h, 0:keys],
                              start=True, stop=not causal, skip_group_check=True)
                if causal:
                    m = pe.matmul(SM[:, j % 2, t * P:keys], const["ident_b"], const["mask_q_b"], start=False, stop=True,
                                  skip_group_check=True)
                m.then_inc(s_sm, 1)

            def rows(n, g, b, turn):
                wait_apart(pe, s_ms, 4 * n + 4, passed)
                out = MI[0:MROWS, 0:S // 2].bitcast(BF16)
                for t in range(NT):
                    m = pe.transpose(out[:, t * P:(t + 1) * P], MT[:, t, :], const["ident_b"])
                m.then_inc(s_full, 1)

            def scores(n, g, b, turn, i):
                hs = i % HG
                h = g * HG + hs
                u = U * g + i
                if i == 0:
                    pe.wait_ge(s_ml, 16 * MRD * (n + 1))
                if not (isinstance(n, int) and n == 0 and i < 2):
                    pe.wait_ge(s_ex, U * n + i - 1)
                st = ST[:, u % 2, :]
                if causal:
                    for kb, at, width in cols(i // HG):
                        pe.matmul(st[:, at:at + width], KS[:, h, kb * P:(kb + 1) * P], QS[:, h, kb * P:S],
                                  start=True, stop=False, skip_group_check=True)
                        m = pe.matmul(st[:, at:at + P], const["ident_b"], const["mask_k_b"], start=False, stop=True,
                                      skip_group_check=True)
                elif i < HG:
                    for kind in range(2):
                        at = kind * S
                        pe.matmul(st[:, at:at + S], const["ones_b"][0:SPLIT, :], ML[:, g % 2, kind * HG + hs, :],
                                  start=True, stop=False, skip_group_check=True)
                        for t in range(NT):
                            q, k, out = QS[0:MR0, h, :], KS[0:MR0, h, :], st[:, at:at + S]
                            if kind == 0:
                                q, k, out = window(q, t), k[:, t * P:(t + 1) * P], window(out, t)
                            else:
                                q, k, out = q[:, t * P:(t + 1) * P], k[:, t::DIL], out[:, t * P:(t + 1) * P]
                            m = pe.matmul(out, k, q, start=False, stop=(t == NT - 1), skip_group_check=True)
                else:
                    for c in range(2):
                        kb = 2 * (i // HG - 1) + c
                        m = pe.matmul(st[:, c * S:(c + 1) * S], KS[:, h, kb * P:(kb + 1) * P], QS[:, h, :],
                                      start=True, stop=True)
                m.then_inc(s_st, 1)

            def pv(n, g, b, turn, r):
                pe.wait_ge(s_ex, U * n + HG * (r + 1))
                if r == 0:
                    pe.wait_ge(s_vc, n + 1)
                    if not (isinstance(n, int) and n == 0):
                        pe.wait_ge(s_ev, n)
                if not causal and r == 0:
                    for kind in range(2):
                        for t in range(NT):
                            for hs in range(HG):
                                out = OA[VW * hs:VW * (hs + 1), :]
                                e = E[:, e_slot(g, hs), kind * S:(kind + 1) * S]
                                if kind == 0:
                                    out, e = window(out, t), window(e, t)
                                    val = V[:, t, g * HG + hs, 2 * VC:2 * VC + VW]
                                else:
                                    out, e = out[:, t * P:(t + 1) * P], e[:, t * P:(t + 1) * P]
                                    val = VP[:, t, g * HG + hs, :]
                                m = pe.matmul(out, val, e, start=(kind == 0 and t == 0), stop=False,
                                              skip_group_check=True)
                else:
                    blocks = cols(r) if causal else [(2 * (r - 1) + c, c * S, S) for c in range(2)]
                    for kb, at, width in blocks:
                        for hs in range(HG):
                            m = pe.matmul(OA[VW * hs:VW * (hs + 1), S - width:S], V[:, kb, g * HG + hs, 0:VW],
                                          E[:, e_slot(g, HG * r + hs), at:at + width],
                                          start=(causal and kb == 0), stop=(kb == NT - 1), skip_group_check=True)
                m.then_inc(s_pv, 1)

            def sel(n, g, b, turn):
                pe.wait_ge(s_ev, n + 1)
                c = KINDS * HG * OC
                for t in range(NT):
                    m = pe.matmul(MI[:, c * t:c * (t + 1)], OS[:, g % 2, t * P:(t + 1) * P], const["pick"][:, 0:c],
                                  start=True, stop=True, skip_group_check=True)
                m.then_inc(s_full, 1)

            def heads_T(b, turn):
                pe.wait_ge(s_no, NNO * NG * (b + 1))
                for t in range(NT):
                    m = pe.transpose(MI[:, t * P:(t + 1) * P], ON[:, t, :], const["ident"])
                m.then_inc(s_full, 1)

            def out_proj(b, turn):
                pe.wait_ge(s_ot, b + 1)
                for t in range(NT):
                    m = pe.matmul(MI[:, t * P:(t + 1) * P], OT[:, t * P:(t + 1) * P], w["out"], start=True, stop=True)
                m.then_inc(s_full, 1)

            walk(pe, dict(xT=xT, proj=proj, rot=rot, values=values, smax=smax, rows=rows, scores=scores, pv=pv,
                          sel=sel, heads_T=heads_T, out_proj=out_proj))

        @block.scalar
        def _(act):
            def xT(b, turn):
                if not (isinstance(b, int) and b == 0):
                    act.wait_ge(s_vs, NV * b)
                lay(turn, xnT[:, :], s_xt)

            def lay(turn, out, done, order=None):
                got = MI[:, :]
                if order and not causal:
                    out, got = order(out, got)
                act.wait_ge(s_full, turn + 1)
                act.activation(out, got, ACT.Copy).then_inc(done, 1)

            def to_phases(out, got):
                return out.rearrange("p (f i) -> p f i", f=DIL), got.rearrange("p (i f) -> p f i", f=DIL)

            def from_phases(out, got):
                return out.rearrange("p (i f) -> p f i", f=DIL), got.rearrange("p (f i) -> p f i", f=DIL)

            def proj(b, turn, side):
                if causal:
                    return
                if not (isinstance(b, int) and b == 0):
                    act.wait_ge(s_pt[side], NPT * b)
                lay(turn, QK[:, side, :], s_pj, None if side else to_phases)

            def part1(b, turn, side):
                if causal:
                    act.wait_ge(s_pt[side], NPT * b + 1)
                else:
                    act.wait_ge(s_pj, 2 * b + side + 1)
                if not (isinstance(b, int) and b == 0):
                    act.wait_ge(s_pw[side], 16 * SPLIT * SPLIT * b)
                act.activation(PT[:, side, 0, :], QK[:, side, :], ACT.Copy).then_inc(s_pa[side], 1)

            def part2(b, turn, side):
                act.wait_ge(s_pt[side], NPT * b + NPT - 1)
                act.activation(PT[:, side, 1, :], QR[:, side, :], ACT.Copy).then_inc(s_pa[side], 1)

            def values(b, turn, which):
                if not (isinstance(b, int) and b == 0):
                    act.wait_ge(s_vc, NG * b)
                lay(turn, VS[:, which, :, :].rearrange("p t d -> p (t d)"), s_vs)

            def scores(n, g, b, turn, i):
                act.wait_ge(s_st, U * n + i + 1)
                r = i // HG
                if not (isinstance(n, int) and U * n + i < NE):
                    act.wait_ge(s_pv, R * n + r - 1)
                width = (sum(c[2] for c in cols(r)) if causal else 2 * S)
                act.activation(E[:, e_slot(g, i), 0:width], ST[:, (U * g + i) % 2, 0:width], ACT.Exp, scale=SCALE
                               ).then_inc(s_ex, 1)

            def evac(n, g, b, turn):
                act.wait_ge(s_pv, R * n + R)
                if not (isinstance(n, int) and n < 2):
                    act.wait_ge(s_no, NNO * (n - 1))
                act.activation(OS[:, g % 2, :], OA[:, :], ACT.Copy).then_inc(s_ev, 1)

            def heads_T(b, turn):
                lay(turn, OT[:, :], s_ot, from_phases)

            walk(act, dict(xT=xT, proj=proj, part1=part1, part2=part2, values=values, scores=scores, evac=evac, heads_T=heads_T))

        @block.vector
        def _(dve):
            def norm_stats(b, turn):
                for t in range(NT):
                    dve.bn_stats(stats[:, t, :], X[:, b * NT + t, :]).then_inc(s_bn, 1)
                wait_apart(dve, s_bn, NT * (b + 1), passed)
                for t in range(NT):
                    m = dve.bn_aggr(mv[:, t, :], stats[:, t, :])
                m.then_inc(s_ln, 1)

            def norm_rows(b, turn):
                dve.wait_ge(s_pow, 2 * b + 2)
                if not (isinstance(b, int) and b == 0):
                    dve.wait_ge(s_xt, b)
                for t in range(NT):
                    m = dve.tensor_scalar(xn[:, t, :], X[:, b * NT + t, :], mv[:, t, 0:1], rstd[:, t:t + 1],
                                          ALU.subtract, ALU.mult)
                m.then_inc(s_ln, 1)

            def rotate(b, turn, side, second):
                dve.wait_ge(s_full, turn + 1)
                out = TQ[:, 0, :] if not second else TQ[:, 1, :]
                if side:
                    dve.wait_ge(s_pt[0], NPT * b + 1)
                elif not (isinstance(b, int) and b == 0):
                    dve.wait_ge(s_pt[1], NPT * (b - 1) + 1)
                dve.tensor_tensor(out, MI[:, :], const["sin"] if second else const["cos"], ALU.mult
                                  ).then_inc(s_rope, 1)

            def proj(b, turn, side):
                if causal:
                    rotate(b, turn, side, 0)

            def rot(b, turn, side):
                rotate(b, turn, side, 1)

            def smax(n, g, b, turn, j):
                hs, t = j // NT, j % NT
                dve.wait_ge(s_sm, SMU * n + j + 1)
                if causal and j == 0 and not (isinstance(n, int) and n == 0):
                    dve.wait_ge(s_ms, 4 * n)
                if causal:
                    dve.tensor_reduce(NM[:, hs, t:t + 1], SM[:, j % 2, 0:(t + 1) * P], AX.X, ALU.max, negate=True
                                      ).then_inc(s_mx, 1)
                else:
                    dve.tensor_reduce(M[:, hs, t, :].rearrange("p (w f) -> p w f", f=DIL),
                                      SM[:, j % 2, :].rearrange("p (w i f) -> p w f i", w=NT, f=DIL), AX.X, ALU.max
                                      ).then_inc(s_mx, 1)

            def maxima(n, g, b, turn):
                if causal:
                    return
                dve.wait_ge(s_mx, SMU * (n + 1))
                if not (isinstance(n, int) and n == 0):
                    dve.wait_ge(s_ms, 4 * n)
                flat = M[:, :, :, :].rearrange("p h t k -> p (h t) k")
                dve.tensor_reduce(NM[:, 0:HG, :].rearrange("p h t -> p (h t)"), flat, AX.X, ALU.max, negate=True
                                  ).then_inc(s_mp, 1)
                dve.tensor_tensor(MD[:, :, :, :].rearrange("p h t k -> p (h t) k"), flat,
                                  const["window"].rearrange("p (a k) -> p a k", a=1).broadcast_to([P, HG * NT, NT * DIL]),
                                  ALU.min).then_inc(s_mp, 1)
                step = NT * DIL
                own = bass.AP(M, 0, [[HG * NT * step, P], [NT * step, HG], [step + 1, DIL], [DIL, NT]])
                dve.tensor_reduce(NM[:, 2 * HG:3 * HG, :], own, AX.X, ALU.max, negate=True).then_inc(s_mp, 1)
                dve.wait_ge(s_mp, 4 * n + 3)
                dve.tensor_reduce(NM[:, HG:2 * HG, :].rearrange("p h t -> p (h t)"),
                                  MD[:, :, :, :].rearrange("p h t k -> p (h t) k"), AX.X, ALU.max, negate=True
                                  ).then_inc(s_mp, 1)

            def rows(n, g, b, turn):
                dve.wait_ge(s_full, turn + 1)
                if not (isinstance(n, int) and n == 0):
                    dve.wait_ge(s_mw, 16 * n)
                dve.tensor_copy(MR[:, :], MI[0:MROWS, 0:S // 2].bitcast(BF16)).then_inc(s_mr, 1)

            def sel(n, g, b, turn):
                dve.wait_ge(s_full, turn + 1)
                k = KINDS * HG
                got = MI[:, 0:NT * k * OC].rearrange("p (t k c) -> p t k c", t=NT, k=k)
                dve.reciprocal(RL[:, :, :, :], got[:, :, :, DH:OC]).then_inc(s_no, 1)
                dve.wait_ge(s_no, NNO * n + 1)
                if not (isinstance(b, int) and b == 0):
                    dve.wait_ge(s_ot, b)
                out = ON[:, :, g * HG * DH:(g + 1) * HG * DH]
                to = out.rearrange("p t (h c) -> p t h c", h=HG) if causal else PR[:, :, :, :]
                dve.tensor_tensor(to, got[:, :, :, 0:DH], RL[:, :, :, :].broadcast_to([P, NT, k, DH]), ALU.mult
                                  ).then_inc(s_no, 1)
                if causal:
                    return
                dve.wait_ge(s_no, NNO * n + 2)
                dve.tensor_reduce(out, PR[:, :, :, :].rearrange("p t (k h) c -> p t (h c) k", k=KINDS), AX.X,
                                  ALU.add).then_inc(s_no, 1)

            def out_proj(b, turn):
                dve.wait_ge(s_full, turn + 1)
                now = X[:, bass.ds(b * NT, NT), :].rearrange("p t d -> p (t d)")
                dve.tensor_tensor(now, now, MI[:, :], ALU.add).then_inc(s_res, 1)

            walk(dve, dict(norm_stats=norm_stats, norm_rows=norm_rows, proj=proj, rot=rot, smax=smax, maxima=maxima,
                           rows=rows, sel=sel, out_proj=out_proj))

        @block.gpsimd
        def _(pool):
            pool.memset(KS[:, :, :], 1.0).then_inc(s_zero, 1)
            pool.memset(QS[:, :, :], 0.0).then_inc(s_zero, 1)
            layouts = ((V, 2 * VC),) if causal else ((V, 2 * VC), (VP, KC))
            for val, _ in layouts:
                pool.memset(val[:, :, :, :], 0.0).then_inc(s_init, 1)
            pool.wait_ge(s_init, NV)
            for val, c in layouts:
                pool.memset(val[:, :, :, c + DH:c + OC], float(KINDS)).then_inc(s_init, 1)

            def norm_rows(b, turn):
                wait_apart(pool, s_ln, 2 * b + 1, passed)
                pool.tensor_scalar(rstd[:, :], mv[:, :, 1], EPS, None, ALU.add).then_inc(s_pow, 1)
                pool.wait_ge(s_pow, 2 * b + 1)
                pool.tensor_tensor(rstd[:, :], rstd[:, :], const["minus_half"][:, 0:NT], ALU.pow).then_inc(s_pow, 1)

            def parts_(b, turn, side):
                q, r, pt = QK[:, side, :], QR[:, side, :], PT[:, side, :, :]
                if causal:
                    pool.wait_ge(s_rope, 4 * b + 2 * side + 2)
                    pool.tensor_tensor(q, TQ[:, 0, :], TQ[:, 1, :], ALU.add).then_inc(s_pt[side], 1)
                pool.wait_ge(s_pa[side], 2 * b + 1)
                pool.tensor_tensor(r, q, pt[:, 0, :], ALU.subtract).then_inc(s_pt[side], 1)
                pool.wait_ge(s_pa[side], 2 * b + 2)
                pool.tensor_tensor(pt[:, 2, :], r, pt[:, 1, :], ALU.subtract).then_inc(s_pt[side], 1)

            def vcopy(b, turn, g):
                pool.wait_ge(s_vs, NV * (b + 1))
                if not (isinstance(b, int) and b == 0):
                    wait_apart(pool, s_pv, R * (NG * (b - 1) + g + 1), passed)
                for which, (val, c) in enumerate(layouts):
                    m = pool.tensor_copy(val[:, :, g * HG:(g + 1) * HG, c:c + DH],
                                         VS[:, which, :, g * HG * DH:(g + 1) * HG * DH].rearrange(
                                             "p t (h c) -> p t h c", h=HG))
                m.then_inc(s_vc, 1)

            def maxima(n, g, b, turn):
                if not (isinstance(n, int) and n == 0):
                    pool.wait_ge(s_mr, n)
                if causal:
                    wait_apart(pool, s_mx, SMU * (n + 1), passed)
                else:
                    wait_apart(pool, s_mp, 4 * n + 4, passed)
                part = MT[:, :, :].rearrange("p t (k s) -> p s k t", s=SPLIT)
                pool.tensor_copy(part[:, 0], NM[:, :, :]).then_inc(s_ms, 1)
                pool.wait_ge(s_ms, 4 * n + 1)
                pool.tensor_tensor(NR[:, :, :], NM[:, :, :], part[:, 0], ALU.subtract).then_inc(s_ms, 1)
                wait_apart(pool, s_ms, 4 * n + 2, passed)
                pool.tensor_copy(part[:, 1], NR[:, :, :]).then_inc(s_ms, 1)
                pool.wait_ge(s_ms, 4 * n + 3)
                pool.tensor_tensor(part[:, 2], NR[:, :, :], part[:, 1], ALU.subtract).then_inc(s_ms, 1)

            walk(pool, dict(norm_rows=norm_rows, parts=parts_, vcopy=vcopy, maxima=maxima))

        @block.sync
        def _(sp):
            sp.wait_ge(s_zero, 2)

            def parts_out(b, turn, side):
                wait_apart(sp, s_pt[side], NPT * (b + 1), passed)
                if side == 0 and not (isinstance(b, int) and b == 0):
                    for g in range(NG):
                        wait_apart(sp, s_rd[g], 32 * b, passed)
                for a in range(SPLIT):
                    for c in range(SPLIT):
                        r = (a * SPLIT + c) * DH
                        sp.dma_start(sdram[side, r:r + DH].rearrange("d h n -> h d n"),
                                     PT[:, side, (a, c)[side], :]).then_inc(s_pw[side], 16)

            def stacks(b, turn, g):
                if not (isinstance(b, int) and b == 0):
                    wait_apart(sp, s_st, U * (NG * (b - 1) + g + 1), passed)
                for side, dst in ((0, QS), (1, KS)):
                    wait_apart(sp, s_pw[side], 16 * SPLIT * SPLIT * (b + 1), passed)
                    sp.dma_start(dst[0:KR, g * HG:(g + 1) * HG, :], sdram[side, :, g * HG:(g + 1) * HG, :]
                                 ).then_inc(s_rd[g], 16)

            def rows(n, g, b, turn):
                wait_apart(sp, s_mr, n + 1, passed)
                if not (isinstance(n, int) and n == 0):
                    wait_apart(sp, s_ml, 16 * MRD * n, passed)
                sp.dma_start(mdram, MR[:, :]).then_inc(s_mw, 16)
                wait_apart(sp, s_mw, 16 * (n + 1), passed)
                if not (isinstance(n, int) and n < 2):
                    wait_apart(sp, s_st, U * (n - 1), passed)
                rows_ = mdram.rearrange("(k s) n -> s k n", s=SPLIT)
                sp.dma_start(QS[MR0:MR0 + SPLIT, g * HG:(g + 1) * HG, :], rows_[:, 0:HG, :]).then_inc(s_ml, 16)
                if not causal:
                    sp.dma_start(ML[:, g % 2, :, :], rows_[:, HG:3 * HG, :]).then_inc(s_ml, 16)

            walk(sp, dict(parts_out=parts_out, stacks=stacks, rows=rows))


def constants():
    import numpy as np
    p = np.arange(P)
    big = np.float32(1e30)
    freqs = (1.0 / np.float32(10000.0) ** (np.arange(0, DH, 2, dtype=np.float32) / DH)).astype(np.float32)
    angle = np.outer(freqs[(p % DH) // 2], np.arange(S, dtype=np.float32)).astype(np.float32)
    pick = np.zeros((P, 3, HG, OC), np.float32)
    for k in range(3):
        for h in range(HG):
            for c in range(OC):
                pick[h * VW + KC * k + c, k, h, c] = 1.0
    parts = {
        "ident": np.eye(P, dtype=np.float32),
        "mask_q": np.where(p[None, :] <= p[:, None], np.float32(0), -big),
        "mask_k": np.where(p[:, None] <= p[None, :], np.float32(0), -big),
        "window": np.where(p[:, None] // (P // NT) == np.arange(NT * DIL)[None, :] // DIL, np.float32(3e38), np.float32(-3e38)),
        "pick": pick.reshape(P, 3 * HG * OC),
        "minus_half": np.full((P, B * NT), -0.5, np.float32),
        "before": np.where(p[:, None] < p[None, :], np.float32(1), np.float32(0)),
        "column_less": np.tile(np.arange(8, dtype=np.float32) - 8, (P, 1)),
        "base": np.tile((B * S + P) * np.arange(8, dtype=np.float32), (P, 1)),
        "row": p[:, None].astype(np.float32),
        "steps": np.tile(P * np.arange(B * NT, dtype=np.float32), (P, 1)),
        "upto": np.tile((np.arange(8)[None, :] <= np.arange(8)[:, None]).astype(np.float32).reshape(1, 64), (P, 1)),
        "block": np.tile(np.arange(72, dtype=np.float32), (P, 1)),
        "block_row": np.tile(P * np.arange(72, dtype=np.float32), (P, 1)),
        "ones": np.ones((P, P), np.float32),
        "column": np.tile(np.arange(8, dtype=np.float32), (P, 1)),
        "cos": np.cos(angle),
        "sin": np.sin(angle),
    }
    at, n = {}, 0
    for name, a in parts.items():
        at[name] = (n, n + a.shape[1])
        n += a.shape[1]
    return np.concatenate([a.astype(np.float32) for a in parts.values()], axis=1), at


def setup(nc, ctx, c_dram, at, x_dram, X, w0qkv, w0out, w1qkv, w1out):
    def sb(name, shape, dt=F32):
        return ctx.enter_context(nc.sbuf_tensor(name, shape, dt))

    C = sb("const", [P, c_dram.shape[1]])
    CB = sb("const_b", [P, 5 * P], BF16)
    W0 = sb("w0", [P, 3 * D])
    WO0 = sb("wo0", [P, D])
    W1 = sb("w1t", [P, 3 * D])
    WR1 = sb("w1r", [P, 2 * D])
    WO1 = sb("wo1", [P, D])
    const = {name: C[:, a:b] for name, (a, b) in at.items()}
    for i, name in enumerate(("ident", "mask_q", "mask_k", "ones", "before")):
        const[name + "_b"] = CB[:, i * P:(i + 1) * P]
    with nc.cleanup_on_exit(), ExitStack() as inner:
        raw = inner.enter_context(nc.sbuf_tensor("w1raw", [P, 4, D], F32))
        ps = inner.enter_context(nc.psum_tensor("w1ps", [P, 4 * D], F32))
        s_c, s_x, s_w, s_raw, s_cb, s_t, s_v = (nc.alloc_semaphore(name="su_" + n) for n in
                                          ("c", "x", "w", "raw", "cb", "t", "v"))
        block = inner.enter_context(nc.Block())

        @block.sync
        def _(sp):
            sp.dma_start(C[:, :], c_dram).then_inc(s_c, 16)
            sp.dma_start(X[:, 0:NT, :], x_dram[0].rearrange("(t p) d -> p t d", p=P)).then_inc(s_x, 16)
            sp.dma_start(raw[:, 0:3, :], w1qkv.rearrange("(t p) i -> p t i", p=P)).then_inc(s_raw, 16)
            sp.dma_start(raw[:, 3, :], w1out).then_inc(s_raw, 16)
            sp.dma_start(W0[:, :], w0qkv).then_inc(s_w, 16)
            sp.dma_start(WO0[:, :], w0out).then_inc(s_w, 16)
            for b in range(1, B):
                sp.dma_start(X[:, b * NT:(b + 1) * NT, :], x_dram[b].rearrange("(t p) d -> p t d", p=P)
                             ).then_inc(s_x, 16)
            sp.wait_ge(s_w, 32)
            sp.wait_ge(s_x, 16 * B)

        @block.vector
        def _(dve):
            dve.wait_ge(s_c, 16)
            for i, name in enumerate(("ident", "mask_q", "mask_k", "ones", "before")):
                dve.tensor_copy(CB[:, i * P:(i + 1) * P], const[name]).then_inc(s_cb, 1)
            dve.wait_ge(s_t, 1)
            dve.tensor_copy(W1[:, :], ps[:, 0:3 * D]).then_inc(s_v, 1)
            dve.tensor_copy(WO1[:, :], ps[:, 3 * D:4 * D]).then_inc(s_v, 1)
            pairs = ps[:, 0:2 * D].rearrange("p (f two) -> p f two", two=2)
            turned = WR1[:, :].rearrange("p (f two) -> p f two", two=2)
            dve.tensor_scalar(turned[:, :, 0], pairs[:, :, 1], -1.0, None, ALU.mult).then_inc(s_v, 1)
            dve.tensor_copy(turned[:, :, 1], pairs[:, :, 0]).then_inc(s_v, 1)

        @block.tensor
        def _(pe):
            pe.wait_ge(s_c, 16)
            pe.wait_ge(s_raw, 32)
            for t in range(4):
                m = pe.transpose(ps[:, t * P:(t + 1) * P], raw[:, t, :], const["ident"])
            m.then_inc(s_t, 1)

    return const, {"qkv": W0[:, :], "out": WO0[:, :]}, {"qkv": W1[:, :], "rot": WR1[:, :], "out": WO1[:, :]}


NE0 = 7
F0 = 512
NX0 = NE0 + 1
HB0 = F0 // P
NE1 = 8
F1 = 256
HB1 = F1 // P
ROUNDS = 2
BOOST = 0.5
TOP = 8
BLOCKS0 = 72
BLOCKS1 = 40


class Norm:

    def __init__(self, nc, ctx, name, minus_half, passed):
        self.passed = passed
        self.half = minus_half
        self.stats = ctx.enter_context(nc.sbuf_tensor(name + "stats", [P, NT, 6], F32))
        self.mv = ctx.enter_context(nc.sbuf_tensor(name + "mv", [P, NT, 2], F32))
        self.rstd = ctx.enter_context(nc.sbuf_tensor(name + "rstd", [P, NT], F32))
        self.s_bn, self.s_mv, self.s_pow, self.s_out = (nc.alloc_semaphore(name=name + n)
                                                        for n in ("bn", "mv", "pow", "out"))

    def vector_stats(self, dve, k, tile):
        for t in range(NT):
            dve.bn_stats(self.stats[:, t, :], tile(t)).then_inc(self.s_bn, 1)
        wait_apart(dve, self.s_bn, NT * (k + 1), self.passed)
        for t in range(NT):
            m = dve.bn_aggr(self.mv[:, t, :], self.stats[:, t, :])
        m.then_inc(self.s_mv, 1)

    def pool(self, pool, k):
        if not (isinstance(k, int) and k == 0):
            pool.wait_ge(self.s_out, k)
        wait_apart(pool, self.s_mv, k + 1, self.passed)
        pool.tensor_scalar(self.rstd[:, :], self.mv[:, :, 1], EPS, None, ALU.add).then_inc(self.s_pow, 1)
        pool.wait_ge(self.s_pow, 2 * k + 1)
        pool.tensor_tensor(self.rstd[:, :], self.rstd[:, :], self.half, ALU.pow).then_inc(self.s_pow, 1)

    def vector_rows(self, dve, k, tile, out):
        dve.wait_ge(self.s_pow, 2 * k + 2)
        for t in range(NT):
            m = dve.tensor_scalar(out(t), tile(t), self.mv[:, t, 0:1], self.rstd[:, t:t + 1],
                                  ALU.subtract, ALU.mult)
        m.then_inc(self.s_out, 1)


def norm_all(dve, norm, X, xn, s_tp, s_cp):
    def sequence(b):
        def rows(t):
            return X[:, b * NT + t, :]
        norm.vector_stats(dve, b, rows)
        if not isinstance(b, int):
            dve.wait_ge(s_tp, b)
            dve.wait_ge(s_cp, b)
        norm.vector_rows(dve, b, rows, lambda t: xn[:, t, :])

    sequence(0)
    with dve.Fori(1, B) as b:
        sequence(b)


TT = B * NT
CAP = B * S + P
UN = 4


class Steps:

    def __init__(self, eng, sem):
        self.eng, self.sem, self.n = eng, sem, 0

    def wait(self):
        if self.n:
            self.eng.wait_ge(self.sem, self.n)

    def __call__(self, op, *args, **kw):
        self.wait()
        return self.did(op(*args, **kw))

    def did(self, instruction):
        instruction.then_inc(self.sem, 1)
        self.n += 1
        return self.n


def across(x, shape):
    return x.rearrange("p (a e) -> p a e", a=1).broadcast_to(shape)


class Routing:

    def __init__(self, nc, ctx, name, const, experts, together, blocks):
        def sb(n, shape, dt=F32):
            return ctx.enter_context(nc.sbuf_tensor(name + n, shape, dt))
        self.const, self.E, self.together, self.N = const, experts, together, blocks
        self.sets = 1 if together else 2
        self.V = sb("V", [P, TT, TOP])
        self.EQ = sb("EQ", [P, TT, TOP])
        self.BEST = sb("BEST", [P, 2, TT])
        self.LOW = sb("LOW", [P, TT])
        self.HOT = sb("HOT", [P, 2, TT, TOP])
        self.HB = sb("HB", [P, self.sets, TT, TOP], BF16)
        self.AT = sb("AT", [P, TT, TOP])
        self.DEST = sb("DEST", [P, 2, TT])
        self.IDX = sb("IDX", [P, 2, TT], U32)
        self.SLOT = sb("SLOT", [P, 2, TT], U32)
        self.PAD = sb("PAD", [P, self.sets, TOP], U32)
        self.PF = sb("PF", [P, TOP])
        self.CNT = sb("CNT", [P, TOP])
        self.GT = sb("GT", [P, TOP, TT])
        self.NB = sb("NB", [P, TOP])
        self.SQ = sb("SQ", [P, TOP, TOP])
        self.END = sb("END", [P, TOP])
        self.BEG = sb("BEG", [P, TOP])
        self.K = sb("K", [P, TOP])
        self.GE = sb("GE", [P, blocks, TOP])
        self.ON = sb("ON", [P, blocks, TOP])
        self.RJ = sb("RJ", [P, blocks, TOP])
        self.TF = sb("TF", [P, 2, blocks])
        self.TAB = sb("TAB", [P, self.sets, 2, blocks], I32)

    def choose(self, st, dve):
        wide = [P, TT, TOP]
        V, EQ, LOW = self.V[:, :, :], self.EQ[:, :, :], self.LOW
        for j in range(2):
            best = self.BEST[:, j, :]
            st(dve.tensor_reduce, best, V, AX.X, ALU.max)
            st(dve.tensor_tensor, EQ, V, best.rearrange("p (t a) -> p t a", a=1).broadcast_to(wide), ALU.is_equal)
            st(dve.tensor_tensor, EQ, EQ, across(self.const["column_less"], wide), ALU.mult)
            st(dve.tensor_reduce, LOW[:, :], EQ, AX.X, ALU.min)
            st(dve.tensor_tensor, self.HOT[:, j, :, :], EQ,
               LOW[:, :].rearrange("p (t a) -> p t a", a=1).broadcast_to(wide), ALU.is_equal)
            if j == 0:
                st(dve.tensor_scalar, EQ, self.HOT[:, 0, :, :], 0.5, -3e38, ALU.subtract, ALU.mult)
                st(dve.tensor_tensor, V, V, EQ, ALU.min)
        if self.together:
            return st(dve.tensor_tensor, self.HB[:, 0, :, :], self.HOT[:, 0, :, :], self.HOT[:, 1, :, :], ALU.add)
        return st(dve.tensor_copy, self.HB[:, :, :, :], self.HOT[:, :, :, :])

    def count(self, pe, PO, sem):
        for i in range(self.sets):
            pe.matmul(PO[:, i, 0:TT, :], self.const["before_b"], self.HB[:, i, :, :], start=True, stop=False,
                      skip_group_check=True)
            for t in range(TT):
                m = pe.matmul(PO[:, i, t + 1:TT + 1, :], self.const["ones_b"],
                              self.HB[:, i, t:t + 1, :].broadcast_to([P, TT - t, TOP]), start=False,
                              stop=(t == TT - 1), skip_group_check=True)
        m.then_inc(sem, 1)

    def place(self, st, dve, PO):
        wide = [P, TT, TOP]
        base = self.const["base"]
        for j in range(2):
            if j < self.sets:
                st(dve.tensor_tensor, self.AT[:, :, :], PO[:, j, 0:TT, :], across(base, wide), ALU.add)
            st(dve.tensor_tensor, self.EQ[:, :, :], self.AT[:, :, :], self.HOT[:, j, :, :], ALU.mult)
            st(dve.tensor_reduce, self.DEST[:, j, :], self.EQ[:, :, :], AX.X, ALU.add)
        st(dve.tensor_copy, self.IDX[:, :, :], self.DEST[:, :, :])
        for i in range(self.sets):
            st(dve.tensor_tensor, self.PF[:, :], PO[:, i, TT, :], base, ALU.add)
            n = st(dve.tensor_scalar, self.PAD[:, i, :], self.PF[:, :], self.const["row"], None, ALU.add)
        return n

    def table(self, st, dve, PO):
        E, N, const = self.E, self.N, self.const
        for i in range(self.sets):
            st(dve.tensor_copy, self.CNT[:, :], PO[:, i, TT, :])
            st(dve.tensor_tensor, self.GT[:, :, :], self.CNT[:, :].rearrange("p (e a) -> p e a", a=1).broadcast_to(
                [P, TOP, TT]), across(const["steps"], [P, TOP, TT]), ALU.is_gt)
            st(dve.tensor_reduce, self.NB[:, :], self.GT[:, :, :], AX.X, ALU.add)
            st(dve.tensor_tensor, self.SQ[:, :, :], across(self.NB[:, :], [P, TOP, TOP]),
               const["upto"].rearrange("p (a e) -> p a e", a=TOP), ALU.mult)
            st(dve.tensor_reduce, self.END[:, :], self.SQ[:, :, :], AX.X, ALU.add)
            st(dve.tensor_tensor, self.BEG[:, :], self.END[:, :], self.NB[:, :], ALU.subtract)
            st(dve.scalar_tensor_tensor, self.K[:, :], self.BEG[:, :], float(-P), const["base"], ALU.mult, ALU.add)
            shape = [P, N, E]
            block = const["block"][:, 0:N].rearrange("p (j a) -> p j a", a=1).broadcast_to(shape)
            row = const["block_row"][:, 0:N].rearrange("p (j a) -> p j a", a=1).broadcast_to(shape)
            GE, ON, RJ = (x[:, :, 0:E] for x in (self.GE, self.ON, self.RJ))
            st(dve.tensor_tensor, GE, block, across(self.END[:, 0:E], shape), ALU.is_ge)
            st(dve.tensor_tensor, ON, block, across(self.BEG[:, 0:E], shape), ALU.is_ge)
            st(dve.tensor_tensor, ON, ON, GE, ALU.subtract)
            st(dve.tensor_tensor, RJ, row, across(self.K[:, 0:E], shape), ALU.add)
            st(dve.tensor_tensor, RJ, RJ, ON, ALU.mult)
            st(dve.tensor_reduce, self.TF[:, 0, :], GE, AX.X, ALU.add)
            st(dve.tensor_scalar, self.TF[:, 0, :], self.TF[:, 0, :], float(TOP - 1), None, ALU.min)
            st(dve.tensor_reduce, self.TF[:, 1, :], RJ, AX.X, ALU.add)
            n = st(dve.tensor_copy, self.TAB[:, i, :, :], self.TF[:, :, :])
            for j in range(2) if self.together else (i,):
                st(dve.tensor_tensor, self.EQ[:, :, :], self.HOT[:, j, :, :], across(self.K[:, :], [P, TT, TOP]),
                   ALU.mult)
                st(dve.tensor_reduce, self.LOW[:, :], self.EQ[:, :, :], AX.X, ALU.add)
                n = st(dve.tensor_tensor, self.SLOT[:, j, :], self.DEST[:, j, :], self.LOW[:, :], ALU.subtract)
        return n

    def scatter(self, pool, x, zeros, rows, sem, choices, i):
        n = 0
        for t in range(TT):
            for j in choices:
                pool.indirect_dma_start(rows, bass.IndirectOffsetOnAxis(ap=self.IDX[:, j, t:t + 1], axis=0), x(t), None
                                        ).then_inc(sem, 16)
                n += 16
        for e in range(self.E):
            pool.indirect_dma_start(rows, bass.IndirectOffsetOnAxis(ap=self.PAD[:, i, e:e + 1], axis=0), zeros, None
                                    ).then_inc(sem, 16)
            n += 16
        return n


def block_pass(nc, L, const, table, rows, results, blocks, weights, down, width, bias=None):
    F = width
    HB = F // P
    N = blocks
    gated = bias is None
    with nc.cleanup_on_exit(), ExitStack() as ctx:
        def sb(name, shape, dt=F32):
            return ctx.enter_context(nc.sbuf_tensor(L + name, shape, dt))

        def sem(name):
            return nc.alloc_semaphore(name=L + name)

        def ps(name, shape):
            return ctx.enter_context(nc.psum_tensor(L + name, shape, F32))

        XB = sb("xb", [P, UN, D])
        XT = sb("xt", [P, 2, P])
        SG = sb("sg", [P, 2, F])
        HH = sb("hh", [P, 2, F])
        HT = sb("ht", [P, 2, F])
        YS = sb("ys", [P, UN, D])
        UP = ps("up", [P, 2, len(weights), S])
        TX = ps("tx", [P, S])
        TH = ps("th", [P, S])
        Y = ps("y", [P, 2, S])
        s_in = [sem(f"in{i}") for i in range(UN)]
        s_out = [sem(f"ot{i}") for i in range(UN)]
        s_tx = sem("stx")
        s_xt = sem("sxt")
        s_up = sem("sup")
        s_sg = sem("ssg")
        s_h = sem("sh")
        s_th = sem("sth")
        s_ht = sem("sht")
        s_y = sem("sy")
        s_ys = sem("sys")
        passed = sem("passed")
        block = ctx.enter_context(nc.Block())

        def walk(eng, step, lag, first=1, last=0):
            def run(steps):
                for i in steps:
                    step(i // UN, i % UN, lambda d: 0 <= i - d < N)

            run(range(first * UN))
            with eng.Fori(first, N // UN - last) as k:
                for u in range(UN):
                    step(k, u, lambda d: True)
            run(range(N - last * UN, N + lag))

        def nth(k, u, d):
            return k * UN + u - d, (u - d) % UN, k + (u - d) // UN

        def wait_if(eng, sem, value, apart=False):
            if isinstance(value, int) and value <= 0:
                return
            if apart:
                wait_apart(eng, sem, value, passed)
            else:
                eng.wait_ge(sem, value)

        @block.sync
        def _(sp):
            def step(k, u, has):
                if has(0):
                    i, q, n = nth(k, u, 0)
                    row = sp.value_load(table[0:1, 1, bass.ds(i, 1)], min_val=0, max_val=rows.shape[0] - P)
                    wait_if(sp, s_tx, i - UN + 1, True)
                    sp.dma_start(XB[:, q, :], rows[bass.ds(row, P)]).then_inc(s_in[q], 16)
                if has(UN + 2):
                    i, q, n = nth(k, u, UN + 2)
                    wait_if(sp, s_ys, i + 1, True)
                    sp.dma_start(results[bass.ds(i * P, P)], YS[:, q, :]).then_inc(s_out[q], 16)

            walk(sp, step, UN + 2, first=2)
            for q in range(UN):
                sp.wait_ge(s_out[q], 16 * (N // UN))

        @block.tensor
        def _(pe):
            pe.wait_ge(s_in[0], 16)
            pe.transpose(TX[:, 0:P], XB[:, 0, :], const["ident"]).then_inc(s_tx, 1)

            def turn_rows(k, u):
                i, q, n = nth(k, u, -1)
                pe.wait_ge(s_in[q], 16 * n + 16)
                pe.transpose(TX[:, 0:P], XB[:, q, :], const["ident"]).then_inc(s_tx, 1)

            def step(k, u, has):
                if has(0):
                    i = nth(k, u, 0)[0]
                    e = pe.value_load(table[0:1, 0, bass.ds(i, 1)], min_val=0, max_val=TOP - 1)
                    pe.wait_ge(s_xt, i + 1)
                    wait_if(pe, s_h, i - 1)
                    for w, weight in enumerate(weights):
                        m = pe.matmul(UP[:, u % 2, w, 0:F], XT[:, u % 2, :], weight[:, bass.ds(e * F, F)], start=True,
                                      stop=True)
                    m.then_inc(s_up, 1)
                if has(-1):
                    turn_rows(k, u)
                if has(1):
                    i = nth(k, u, 1)[0]
                    pe.wait_ge(s_h, i + 1)
                    wait_if(pe, s_ht, i)
                    for c in range(HB):
                        m = pe.transpose(TH[:, c * P:(c + 1) * P], HH[:, (u - 1) % 2, c * P:(c + 1) * P],
                                         const["ident"])
                    m.then_inc(s_th, 1)
                if has(2):
                    i = nth(k, u, 2)[0]
                    e = pe.value_load(table[0:1, 0, bass.ds(i, 1)], min_val=0, max_val=TOP - 1)
                    pe.wait_ge(s_ht, i + 1)
                    wait_if(pe, s_ys, i - 1)
                    for c in range(HB):
                        m = pe.matmul(Y[:, u % 2, 0:D], HT[:, u % 2, c * P:(c + 1) * P],
                                      down[:, bass.ds(e * HB * D + c * D, D)], start=(c == 0), stop=(c == HB - 1))
                    m.then_inc(s_y, 1)

            walk(pe, step, 2, last=1)

        @block.scalar
        def _(act):
            act.wait_ge(s_tx, 1)
            act.copy(XT[:, 0, :], TX[:, 0:P]).then_inc(s_xt, 1)

            def step(k, u, has):
                if has(0) and gated:
                    i = nth(k, u, 0)[0]
                    act.wait_ge(s_up, i + 1)
                    act.activation(SG[:, u % 2, :], UP[:, u % 2, 0, 0:F], ACT.Silu).then_inc(s_sg, 1)
                if has(-1):
                    i = nth(k, u, -1)[0]
                    act.wait_ge(s_tx, i + 1)
                    act.copy(XT[:, (u + 1) % 2, :], TX[:, 0:P]).then_inc(s_xt, 1)
                if has(1):
                    i = nth(k, u, 1)[0]
                    act.wait_ge(s_th, i + 1)
                    act.activation(HT[:, (u - 1) % 2, :], TH[:, 0:F], ACT.Copy if gated else ACT.Relu).then_inc(s_ht, 1)

            walk(act, step, 2, last=1)

        @block.vector
        def _(dve):
            def step(k, u, has):
                if has(0):
                    i = nth(k, u, 0)[0]
                    if gated:
                        dve.wait_ge(s_sg, i + 1)
                        one, two, op = SG[:, u % 2, :], UP[:, u % 2, 1, 0:F], ALU.mult
                    else:
                        e = dve.value_load(table[0:1, 0, bass.ds(i, 1)], min_val=0, max_val=TOP - 1)
                        dve.wait_ge(s_up, i + 1)
                        one, two, op = UP[:, u % 2, 0, 0:F], bias[0][:, bass.ds(e * F, F)], ALU.add
                    dve.tensor_tensor(HH[:, u % 2, :], one, two, op).then_inc(s_h, 1)
                if has(2):
                    i, q, n = nth(k, u, 2)
                    if not gated:
                        e = dve.value_load(table[0:1, 0, bass.ds(i, 1)], min_val=0, max_val=TOP - 1)
                    dve.wait_ge(s_y, i + 1)
                    wait_if(dve, s_out[q], 16 * n)
                    if gated:
                        m = dve.tensor_copy(YS[:, q, :], Y[:, u % 2, 0:D])
                    else:
                        m = dve.tensor_tensor(YS[:, q, :], Y[:, u % 2, 0:D], bias[1][:, bass.ds(e * D, D)], ALU.add)
                    m.then_inc(s_ys, 1)

            walk(dve, step, 2, first=2)


def mixture0(nc, X, const, scratch, router, gate, up, down, sgate, sup, sdown):
    rows_dram, results_dram = scratch
    with nc.cleanup_on_exit(), ExitStack() as ctx:
        def sb(name, shape, dt=F32):
            return ctx.enter_context(nc.sbuf_tensor("a" + name, shape, dt))

        WG = sb("wg", [P, NX0, F0])
        WU = sb("wu", [P, NX0, F0])
        WD = sb("wd", [P, NX0, HB0, D])
        W12 = sb("w12", [P, 2, TT])
        route = Routing(nc, ctx, "a", const, NE0, True, BLOCKS0)
        route_and_share(nc, X, const, route, W12, (WG, WU, WD), rows_dram, router, gate, up, down, sgate, sup, sdown)
        flat = [w[:, :, :].rearrange("p e f -> p (e f)") for w in (WG, WU)]
        block_pass(nc, "ab", const, route.TAB[0:1, 0, :, :], rows_dram, results_dram, BLOCKS0, flat,
                   WD[:, :, :, :].rearrange("p e c d -> p (e c d)"), F0)
        take_weighted(nc, X, route, W12, results_dram)


def route_and_share(nc, X, const, route, W12, weights, rows_dram, router, gate, up, down, sgate, sup, sdown):
    WG, WU, WD = weights
    with nc.cleanup_on_exit(), ExitStack() as ctx:
        def sb(name, shape, dt=F32):
            return ctx.enter_context(nc.sbuf_tensor("a" + name, shape, dt))

        def sem(name):
            return nc.alloc_semaphore(name="a" + name)

        def ps(name, shape):
            return ctx.enter_context(nc.psum_tensor("a" + name, shape, F32))

        RW = sb("rw", [TOP, D])
        RT = sb("rt", [P, TOP])
        XN = sb("xn", [P, TT, D])
        XS = sb("xs", [P, S])
        XT = sb("xT", [P, B * S])
        ZE = sb("ze", [P, D])
        xn = sb("xN", [P, NT, D])
        SG = sb("sg", [P, 2, S])
        HT = sb("ht", [P, 2, S])
        G = ps("g", [P, 2, S])
        U = ps("u", [P, 2, S])
        Y = ps("y", [P, 2, NT * D])
        TP = ps("tp", [P, S])
        RB = ps("rb", [P, TT, TOP])
        PO = TP[:, 0:(TT + 1) * TOP].rearrange("p (a t e) -> p a t e", a=1, e=TOP)
        passed = sem("passed")
        norm = Norm(nc, ctx, "a", const["minus_half"][:, 0:NT], passed)
        s_rw = sem("rw")
        s_sw = sem("sw")
        s_w = sem("w")
        s_rt = sem("rt")
        s_rtc = sem("rtc")
        s_ze = sem("ze")
        s_tp = sem("tp")
        s_cp = sem("cp")
        s_xs = sem("xs")
        s_xt = sem("xt")
        s_rb = sem("rb")
        s_r = sem("r")
        s_e = sem("e")
        s_po = sem("po")
        s_sc = sem("sc")
        s_gu = sem("gu")
        s_sg = sem("sg")
        s_h = sem("h")
        s_y = sem("y")
        s_c = sem("c")
        K, SH = HB0, NE0
        marks = {}
        block = ctx.enter_context(nc.Block())

        @block.vector
        def _(dve):
            st = Steps(dve, s_r)
            st(dve.memset, RT[:, :], 0.0)
            st(dve.memset, route.V[:, :, :], -3e38)
            dve.wait_ge(s_rt, 1)
            st.wait()
            dve.tensor_copy(RT[:, 0:NE0], TP[:, 0:NE0]).then_inc(s_rtc, 1)

            norm_all(dve, norm, X, xn, s_tp, s_cp)
            dve.wait_ge(s_rb, B)
            st(dve.tensor_copy, route.V[:, :, 0:NE0], RB[:, :, 0:NE0])
            marks["chosen"] = route.choose(st, dve)
            marks["apart"] = st(dve.tensor_tensor, W12[:, 1, :], route.BEST[:, 1, :], route.BEST[:, 0, :], ALU.subtract)
            dve.wait_ge(s_po, 1)
            marks["placed"] = route.place(st, dve, PO)

            def body(b):
                for k in range(K):
                    dve.wait_ge(s_sg, b * K + k + 1)
                    dve.tensor_tensor(HT[:, k % 2, :], SG[:, k % 2, :], U[:, k % 2, :], ALU.mult).then_inc(s_h, 1)
                now = X[:, bass.ds(b * NT, NT), :].rearrange("p t d -> p (t d)")
                dve.wait_ge(s_y, b + 1)
                dve.tensor_tensor(now, now, Y[:, 0, :], ALU.add).then_inc(s_c, 1)

            body(0)
            dve.wait_ge(s_e, 1)
            st(dve.tensor_scalar, W12[:, 0, :], W12[:, 1, :], 1.0, None, ALU.add)
            st(dve.reciprocal, W12[:, 0, :], W12[:, 0, :])
            st(dve.tensor_tensor, W12[:, 1, :], W12[:, 0, :], W12[:, 1, :], ALU.mult)
            route.table(st, dve, PO)
            with dve.Fori(1, B) as b:
                body(b)

        @block.sync
        def _(sp):
            sp.dma_start(RW[0:NE0, :], router).then_inc(s_rw, 16)
            for dst, shared in ((WG, sgate), (WU, sup)):
                sp.dma_start(dst[:, SH, :], shared[0]).then_inc(s_sw, 16)
            sp.dma_start(WD[:, SH, :, :], sdown[0].rearrange("(c h) d -> h c d", h=P)).then_inc(s_sw, 16)
            for dst, routed in ((WG, gate), (WU, up)):
                sp.dma_start(dst[:, 0:NE0, :], routed.rearrange("e d h -> d e h")).then_inc(s_w, 16)
            for e in range(NE0):
                sp.dma_start(WD[:, e, :, :], down[e].rearrange("(c h) d -> h c d", h=P)).then_inc(s_w, 16)
            sp.wait_ge(s_w, 16 * (2 + NE0))

        @block.tensor
        def _(pe):
            pe.wait_ge(s_rw, 16)
            pe.transpose(TP[:, 0:NE0], RW[0:NE0, :], const["ident"][0:NE0, 0:NE0]).then_inc(s_rt, 1)
            pe.wait_ge(s_rtc, 1)

            def turn(b):
                pe.wait_ge(norm.s_out, b + 1)
                for t in range(NT):
                    m = pe.transpose(TP[:, t * P:(t + 1) * P], xn[:, t, :], const["ident"])
                m.then_inc(s_tp, 1)
                pe.wait_ge(s_xs, b + 1)
                for t in range(NT):
                    m = pe.matmul(RB[:, b * NT + t, :], XS[:, t * P:(t + 1) * P], RT[:, :], start=True, stop=True,
                                  skip_group_check=True)
                m.then_inc(s_rb, 1)
                pe.wait_ge(s_xt, b + 1)

            with pe.Fori(0, B) as b:
                turn(b)
            pe.wait_ge(s_r, marks["chosen"])
            route.count(pe, PO, s_po)
            pe.wait_ge(s_sw, 48)

            def down_(b, k):
                pe.wait_ge(s_h, b * K + k + 1)
                for t in range(NT):
                    m = pe.matmul(Y[:, 0, t * D:(t + 1) * D], HT[:, k % 2, t * P:(t + 1) * P],
                                  WD[:, SH, k, :], start=(k == 0 and t == 0), stop=(k == K - 1),
                                  skip_group_check=True)
                if k == K - 1:
                    m.then_inc(s_y, 1)

            def body(b, first):
                for k in range(K):
                    if not first or k > 1:
                        pe.wait_ge(s_h, b * K + k - 1)
                    for dst, wt in ((G, WG), (U, WU)):
                        m = pe.matmul(dst[:, k % 2, :], wt[:, SH, k * P:(k + 1) * P], XT[:, bass.ds(b * S, S)],
                                      start=True, stop=True)
                    m.then_inc(s_gu, 1)
                    if k == 0 and not first:
                        down_(b - 1, K - 1)
                    if k == 1 and not first:
                        pe.wait_ge(s_c, b)
                    if k:
                        down_(b, k - 1)

            body(0, True)
            with pe.Fori(1, B) as b:
                body(b, False)
            down_(B - 1, K - 1)

        @block.scalar
        def _(act):
            with act.Fori(0, B) as b:
                act.wait_ge(s_tp, b + 1)
                act.copy(XS[:, :], TP[:, :]).then_inc(s_xs, 1)
                act.copy(XT[:, bass.ds(b * S, S)], TP[:, :]).then_inc(s_xt, 1)
            act.wait_ge(s_r, marks["apart"])
            act.activation(W12[:, 1, :], W12[:, 1, :], ACT.Exp).then_inc(s_e, 1)
            with act.Fori(0, B) as b:
                for k in range(K):
                    act.wait_ge(s_gu, b * K + k + 1)
                    act.activation(SG[:, k % 2, :], G[:, k % 2, :], ACT.Silu).then_inc(s_sg, 1)

        @block.gpsimd
        def _(pool):
            def sequence(b):
                norm.pool(pool, b)
                wait_apart(pool, norm.s_out, b + 1, passed)
                pool.tensor_copy(XN[:, bass.ds(b * NT, NT), :], xn[:, :, :]).then_inc(s_cp, 1)

            sequence(0)
            with pool.Fori(1, B) as b:
                sequence(b)
            pool.memset(ZE[:, :], 0.0).then_inc(s_ze, 1)
            pool.wait_ge(s_ze, 1)
            pool.wait_ge(s_cp, B)
            pool.wait_ge(s_r, marks["placed"])
            n = route.scatter(pool, lambda t: XN[:, t, :], ZE[:, :], rows_dram, s_sc, (0, 1), 0)
            pool.wait_ge(s_sc, n)


def gather(pool, route, YG, results_dram, sems, choices, place=0):
    n = 16 * NT * len(choices)
    for b in range(B):
        if b > 1:
            pool.wait_ge(sems[b % 2], n * (b // 2))
        for t in range(b * NT, (b + 1) * NT):
            for at, j in enumerate(choices):
                pool.indirect_dma_start(YG[:, place + at, t, :], None, results_dram,
                                        bass.IndirectOffsetOnAxis(ap=route.SLOT[:, j, t:t + 1], axis=0)
                                        ).then_inc(sems[b % 2], 16)


def gathered(dve, sems, n, sequence):
    with dve.Fori(0, B // 2) as k:
        for odd in range(2):
            dve.wait_ge(sems[odd], 16 * n * (k + 1))
            sequence(2 * k + odd)


def take_weighted(nc, X, route, W12, results_dram):
    with nc.cleanup_on_exit(), ExitStack() as ctx:
        YG = ctx.enter_context(nc.sbuf_tensor("cyg", [P, 2, TT, D], F32))
        s_g = [nc.alloc_semaphore(name=f"cg{i}") for i in range(2)]
        s_c = nc.alloc_semaphore(name="cc")
        block = ctx.enter_context(nc.Block())

        @block.gpsimd
        def _(pool):
            gather(pool, route, YG, results_dram, s_g, (0, 1))

        @block.vector
        def _(dve):
            def sequence(b):
                for j in range(2):
                    if j:
                        dve.wait_ge(s_c, 2 * b + 1)
                    for t in range(NT):
                        t = b * NT + t
                        m = dve.scalar_tensor_tensor(X[:, t, :], YG[:, j, t, :], W12[:, j, bass.ds(t, 1)], X[:, t, :],
                                                     ALU.mult, ALU.add)
                    m.then_inc(s_c, 1)

            gathered(dve, s_g, 2 * NT, sequence)


def mixture1(nc, X, const, scratch, out_dram, gate_w, gate_b, w1, b1, w2, b2, gamma, beta):
    rows_dram, results_dram = scratch
    with nc.cleanup_on_exit(), ExitStack() as ctx:
        def sb(name, shape, dt=F32):
            return ctx.enter_context(nc.sbuf_tensor("b" + name, shape, dt))

        W1 = sb("w1", [P, NE1, F1])
        W2 = sb("w2", [P, NE1, HB1, D])
        B1 = sb("b1", [P, NE1, F1])
        B2 = sb("b2", [P, NE1, D])
        GA = sb("ga", [P, D])
        BE = sb("be", [P, D])
        XN = sb("xn", [P, TT, D])
        OR = sb("or", [P, 2, TT, D])
        route = Routing(nc, ctx, "b", const, NE1, False, BLOCKS1)
        route_gate(nc, X, XN, const, route, (W1, W2, B1, B2, GA, BE), rows_dram[0], gate_w, gate_b, w1, b1, w2, b2,
                   gamma, beta)
        flat = W1[:, :, :].rearrange("p e f -> p (e f)")
        for r in range(ROUNDS):
            block_pass(nc, f"b{r}", const, route.TAB[0:1, r, :, :], rows_dram[r], results_dram[r], BLOCKS1, [flat],
                       W2[:, :, :, :].rearrange("p e c d -> p (e c d)"), F1,
                       bias=(B1[:, :, :].rearrange("p e f -> p (e f)"), B2[:, :, :].rearrange("p e d -> p (e d)")))
            if r == 0:
                boost(nc, XN, OR, route, rows_dram[1], results_dram[0])
        finish(nc, X, XN, OR, const, route, GA, BE, results_dram[1], out_dram)


def route_gate(nc, X, XN, const, route, weights, rows_dram, gate_w, gate_b, w1, b1, w2, b2, gamma, beta):
    W1, W2, B1, B2, GA, BE = weights
    with nc.cleanup_on_exit(), ExitStack() as ctx:
        def sb(name, shape, dt=F32):
            return ctx.enter_context(nc.sbuf_tensor("b" + name, shape, dt))

        def sem(name):
            return nc.alloc_semaphore(name="b" + name)

        def ps(name, shape):
            return ctx.enter_context(nc.psum_tensor("b" + name, shape, F32))

        GW = sb("gw", [P, NE1])
        GB = sb("gb", [P, NE1])
        XS = sb("xs", [P, S])
        ZE = sb("ze", [P, D])
        xn = sb("xN", [P, NT, D])
        MX = sb("mx", [P, TT, 1])
        TP = ps("tp", [P, S])
        RB = ps("rb", [P, TT, TOP])
        PO = ps("po", [P, 2, S])
        PO = PO[:, :, 0:(TT + 1) * TOP].rearrange("p a (t e) -> p a t e", e=TOP)
        passed = sem("passed")
        norm = Norm(nc, ctx, "b", const["minus_half"][:, 0:NT], passed)
        s_gate = sem("gate")
        s_w = sem("w")
        s_ze = sem("ze")
        s_tp = sem("tp")
        s_cp = sem("cp")
        s_xs = sem("xs")
        s_rb = sem("rb")
        s_r = sem("r")
        s_e = sem("e")
        s_po = sem("po")
        s_sc = sem("sc")
        marks = {}
        block = ctx.enter_context(nc.Block())

        @block.vector
        def _(dve):
            norm_all(dve, norm, X, xn, s_tp, s_cp)
            st = Steps(dve, s_r)
            wide = [P, TT, TOP]
            V = route.V[:, :, :]
            dve.wait_ge(s_gate, 32)
            dve.wait_ge(s_rb, B)
            st(dve.tensor_tensor, V, RB[:, :, :], across(GB[:, :], wide), ALU.add)
            st(dve.tensor_reduce, MX[:, :, 0], V, AX.X, ALU.max)
            marks["less"] = st(dve.tensor_tensor, V, V, MX[:, :, :].broadcast_to(wide), ALU.subtract)
            dve.wait_ge(s_e, 1)
            st(dve.tensor_reduce, MX[:, :, 0], V, AX.X, ALU.add)
            st(dve.reciprocal, MX[:, :, :], MX[:, :, :])
            st(dve.tensor_tensor, V, V, MX[:, :, :].broadcast_to(wide), ALU.mult)
            marks["chosen"] = route.choose(st, dve)
            dve.wait_ge(s_po, 1)
            marks["placed"] = route.place(st, dve, PO)
            route.table(st, dve, PO)

        @block.sync
        def _(sp):
            sp.dma_start(GW[:, :], gate_w).then_inc(s_gate, 16)
            sp.dma_start(GB[:, :], gate_b.partition_broadcast(P)).then_inc(s_gate, 16)
            sp.dma_start(W1[:, :, :], w1.rearrange("e d h -> d e h")).then_inc(s_w, 16)
            sp.dma_start(W2[:, :, :, :], w2.rearrange("e (c h) d -> h e c d", h=P)).then_inc(s_w, 16)
            sp.dma_start(B1[:, :, :], b1.rearrange("e h -> (e h)").partition_broadcast(P)).then_inc(s_w, 16)
            sp.dma_start(B2[:, :, :], b2.rearrange("e d -> (e d)").partition_broadcast(P)).then_inc(s_w, 16)
            sp.dma_start(GA[:, :], gamma.partition_broadcast(P)).then_inc(s_w, 16)
            sp.dma_start(BE[:, :], beta.partition_broadcast(P)).then_inc(s_w, 16)
            sp.wait_ge(s_w, 96)

        @block.tensor
        def _(pe):
            pe.wait_ge(s_gate, 32)
            with pe.Fori(0, B) as b:
                pe.wait_ge(norm.s_out, b + 1)
                for t in range(NT):
                    m = pe.transpose(TP[:, t * P:(t + 1) * P], xn[:, t, :], const["ident"])
                m.then_inc(s_tp, 1)
                pe.wait_ge(s_xs, b + 1)
                for t in range(NT):
                    m = pe.matmul(RB[:, b * NT + t, :], XS[:, t * P:(t + 1) * P], GW[:, :], start=True, stop=True,
                                  skip_group_check=True)
                m.then_inc(s_rb, 1)
            pe.wait_ge(s_r, marks["chosen"])
            route.count(pe, PO, s_po)

        @block.scalar
        def _(act):
            with act.Fori(0, B) as b:
                act.wait_ge(s_tp, b + 1)
                act.copy(XS[:, :], TP[:, :]).then_inc(s_xs, 1)
            act.wait_ge(s_r, marks["less"])
            act.activation(route.V[:, :, :], route.V[:, :, :], ACT.Exp).then_inc(s_e, 1)

        @block.gpsimd
        def _(pool):
            def sequence(b):
                norm.pool(pool, b)
                wait_apart(pool, norm.s_out, b + 1, passed)
                pool.tensor_copy(XN[:, bass.ds(b * NT, NT), :], xn[:, :, :]).then_inc(s_cp, 1)

            sequence(0)
            with pool.Fori(1, B) as b:
                sequence(b)
            pool.memset(ZE[:, :], 0.0).then_inc(s_ze, 1)
            pool.wait_ge(s_ze, 1)
            pool.wait_ge(s_cp, B)
            pool.wait_ge(s_r, marks["placed"])
            n = route.scatter(pool, lambda t: XN[:, t, :], ZE[:, :], rows_dram, s_sc, (0,), 0)
            pool.wait_ge(s_sc, n)


def boost(nc, XN, OR, route, rows_dram, results_dram):
    with nc.cleanup_on_exit(), ExitStack() as ctx:
        BO = ctx.enter_context(nc.sbuf_tensor("dbo", [P, TT, D], F32))
        ZE = ctx.enter_context(nc.sbuf_tensor("dze", [P, D], F32))
        s_g = [nc.alloc_semaphore(name=f"dg{i}") for i in range(2)]
        s_ze = nc.alloc_semaphore(name="dz")
        s_b = nc.alloc_semaphore(name="db")
        s_sc = nc.alloc_semaphore(name="ds")
        block = ctx.enter_context(nc.Block())

        @block.gpsimd
        def _(pool):
            pool.memset(ZE[:, :], 0.0).then_inc(s_ze, 1)
            gather(pool, route, OR, results_dram, s_g, (0,))
            pool.wait_ge(s_ze, 1)
            pool.wait_ge(s_b, B)
            n = route.scatter(pool, lambda t: BO[:, t, :], ZE[:, :], rows_dram, s_sc, (1,), 1)
            pool.wait_ge(s_sc, n)

        @block.vector
        def _(dve):
            def sequence(b):
                t = bass.ds(b * NT, NT)
                dve.scalar_tensor_tensor(BO[:, t, :], OR[:, 0, t, :], BOOST, XN[:, t, :], ALU.mult, ALU.add
                                         ).then_inc(s_b, 1)

            gathered(dve, s_g, NT, sequence)


def finish(nc, X, XN, OR, const, route, GA, BE, results_dram, out_dram):
    with nc.cleanup_on_exit(), ExitStack() as ctx:
        F = ctx.enter_context(nc.sbuf_tensor("ef", [P, NT, D], F32))
        s_g = [nc.alloc_semaphore(name=f"eg{i}") for i in range(2)]
        s_f = nc.alloc_semaphore(name="ef")
        s_out = ctx.enter_context(nc.semaphore("eo"))
        passed = nc.alloc_semaphore(name="ep")
        norm = Norm(nc, ctx, "e", const["minus_half"][:, 0:NT], passed)
        block = ctx.enter_context(nc.Block())

        @block.gpsimd
        def _(pool):
            gather(pool, route, OR, results_dram, s_g, (1,), 1)
            norm.pool(pool, 0)
            with pool.Fori(1, B) as b:
                norm.pool(pool, b)

        @block.sync
        def _(sp):
            for b in range(B):
                sp.wait_ge(s_f, 5 * b + 5)
                sp.dma_start(out_dram[b].rearrange("(t p) d -> p t d", p=P), X[:, b * NT:(b + 1) * NT, :]
                             ).then_inc(s_out, 16)
            sp.wait_ge(s_out, 16 * B)

        @block.vector
        def _(dve):
            def sequence(b):
                if not isinstance(b, int):
                    dve.wait_ge(s_f, 5 * b)
                for r in range(ROUNDS):
                    for t in range(NT):
                        x = XN[:, b * NT + t, :] if r == 0 else F[:, t, :]
                        m = dve.scalar_tensor_tensor(F[:, t, :], OR[:, r, b * NT + t, :],
                                                     route.BEST[:, r, bass.ds(b * NT + t, 1)], x, ALU.mult, ALU.add)
                    m.then_inc(s_f, 1)
                    dve.wait_ge(s_f, 5 * b + r + 1)
                norm.vector_stats(dve, b, lambda t: F[:, t, :])
                norm.vector_rows(dve, b, lambda t: F[:, t, :], lambda t: F[:, t, :])
                dve.wait_ge(norm.s_out, b + 1)
                for i, (row, op) in enumerate(((GA, ALU.mult), (BE, ALU.add))):
                    dve.tensor_tensor(F[:, :, :], F[:, :, :], across(row[:, :], [P, NT, D]), op).then_inc(s_f, 1)
                    dve.wait_ge(s_f, 5 * b + 3 + i)
                now = X[:, bass.ds(b * NT, NT), :]
                dve.tensor_tensor(now, now, F[:, :, :], ALU.add).then_inc(s_f, 1)

            gathered(dve, s_g, NT, sequence)


def build(nc, c, x, w0qkv, w0out, router, gate, up, down, sgate, sup, sdown, w1qkv, w1out, gate_w, gate_b, w1, b1, w2, b2,
          gamma, beta, out):
    at = constants()[1]
    with ExitStack() as ctx:
        X = ctx.enter_context(nc.sbuf_tensor("X", [P, B * NT, D], F32))
        const, attn0, attn1 = setup(nc, ctx, c, at, x, X, w0qkv, w0out, w1qkv, w1out)
        parts = nc.dram_tensor("qk_parts", [2, KR, H, S], BF16).ap()
        rows0 = nc.dram_tensor("maxima_0", [3 * HG * SPLIT, S], BF16).ap()
        rows1 = nc.dram_tensor("maxima_1", [HG * SPLIT, S], BF16).ap()
        attention(nc, X, const, attn0, (parts, rows0), False)
        rows = [nc.dram_tensor(f"rows_{i}", [TOP * CAP, D], F32).ap() for i in range(3)]
        results = [nc.dram_tensor(f"results_{i}", [n * P, D], F32).ap() for i, n in enumerate(
            (BLOCKS0, BLOCKS1, BLOCKS1))]
        mixture0(nc, X, const, (rows[0], results[0]), router, gate, up, down, sgate, sup, sdown)
        attention(nc, X, const, attn1, (parts, rows1), True)
        mixture1(nc, X, const, (rows[1:], results[1:]), out, gate_w, gate_b, w1, b1, w2, b2, gamma, beta)


INPUTS = ["L0_attn_x", "L0_attn_w_qkv", "L0_attn_w_out", "L0_ffn_router_w", "L0_ffn_w_gate", "L0_ffn_w_up",
          "L0_ffn_w_down", "L0_ffn_sw_gate", "L0_ffn_sw_up", "L0_ffn_sw_down", "L1_attn_W_qkv", "L1_attn_W_out",
          "L1_ffn_gate_W", "L1_ffn_gate_b", "L1_ffn_W1", "L1_ffn_b1", "L1_ffn_W2", "L1_ffn_b2", "L1_ffn_ln_gamma",
          "L1_ffn_ln_beta"]


def kernel(**inputs):
    import numpy as np
    import concourse.bacc as bacc
    from concourse.bass_utils import run_bass_kernel_spmd

    nc = bacc.Bacc("TRN2", target_bir_lowering=False, num_devices=1)
    arrays = {"constants": constants()[0]}
    for name in INPUTS:
        arrays[name] = np.ascontiguousarray(inputs[name])
    args = [nc.dram_tensor(name, a.shape, mybir.dt.from_np(a.dtype), kind="ExternalInput").ap()
            for name, a in arrays.items()]
    out = nc.dram_tensor("out", (B, S, D), F32, kind="ExternalOutput").ap()
    build(nc, *args, out)
    result = run_bass_kernel_spmd(nc, [arrays], core_ids=[0])
    return result.results[0]["out"]
```

```python
from contextlib import ExitStack

import concourse.bass as bass
from concourse import mybir

F32 = mybir.dt.float32
BF16 = mybir.dt.bfloat16
U32 = mybir.dt.uint32
I32 = mybir.dt.int32
ALU = mybir.AluOpType
ACT = mybir.ActivationFunctionType
AX = mybir.AxisListType

P = 128
D = 128
S = 512
B = 8
NT = S // P
H = 16
DH = D // H
HG = 4
NG = H // HG
DIL = 4
SPLIT = 3
KR = SPLIT * SPLIT * DH
MR0 = 96
SCALE = float(DH) ** -0.5
VW = 32
OC = DH + 1
KC = 10
EPS = 1e-5


def wait_apart(eng, sem, value, passed):
    eng.wait_ge(sem, value)
    if not isinstance(value, int):
        eng.sem_inc(passed, 1)


class Turns:

    def __init__(self, prologue, first, middle, last, tail):
        self.order = {"prologue": prologue, "first": first, "middle": middle, "last": last, "tail": tail}
        self.before = {}
        n = 0
        for part, uses in self.order.items():
            self.before[part] = n
            n += len(uses) * (B - 2 if part == "middle" else 1)

    def number(self, part, b, use):
        n = self.before[part] + self.order[part].index(use)
        return n + (b - 1) * len(self.order["middle"]) if part == "middle" else n

    def previous(self, part, b, use):
        at = self.order[part].index(use)
        if at:
            return part, b, self.order[part][at - 1]
        if part == "prologue":
            return None
        names = list(self.order)
        before = names[names.index(part) - 1]
        last = self.order[before][-1]
        assert part != "middle" or last == self.order["middle"][-1]
        return before, b if part == "first" else b - 1, last


def attention(nc, X, const, w, scratch, causal, due=None):
    L = "c" if causal else "w"
    KINDS = 1 if causal else 3
    U = 8 if causal else 12
    R = U // HG
    SMU = HG * NT
    MROWS = KINDS * HG * SPLIT
    CUT = 2 if causal else 4
    AHEAD = SMU * (U - CUT) // U
    NE = 2 * HG
    VC = 0 if causal else KC

    with nc.cleanup_on_exit(), ExitStack() as ctx:
        def sb(name, shape, dt=F32):
            return ctx.enter_context(nc.sbuf_tensor(L + name, shape, dt))

        def sem(name):
            return nc.alloc_semaphore(name=L + name)

        QS = sb("qs", [P, H, S], BF16)
        KS = sb("ks", [P, H, S], BF16)
        ML = sb("ml", [SPLIT, 2, 2 * HG, S], BF16)
        E = sb("e", [P, NE, 2 * S])
        V = sb("v", [P, NT, H, 2 * VC + VW])
        VP = V if causal else sb("vp", [P, DIL, H, VW])
        VS = sb("vs", [P, 2, NT, D])
        stats = sb("stats", [P, NT, 6])
        mv = sb("mv", [P, NT, 2])
        rstd = sb("rstd", [P, NT])
        xn = sb("xn", [P, NT, D])
        xnT = sb("xnT", [P, S])
        QK = sb("qk", [P, 2, S])
        QR = sb("qr", [P, 2, S])
        PT = sb("pt", [P, 2, SPLIT, S], BF16)
        TQ = sb("tq", [P, 2, S])
        M = sb("m", [P, HG, NT, NT * DIL])
        MD = sb("md", [P, HG, NT, NT * DIL])
        NM = sb("nm", [P, KINDS * HG, NT])
        NR = sb("nr", [P, KINDS * HG, NT])
        MT = sb("mt", [P, NT, MROWS], BF16)
        MR = sb("mr", [MROWS, S], BF16)
        OS = sb("os", [P, 2, S])
        RL = sb("rl", [P, NT, KINDS * HG, 1])
        PR = sb("pr", [P, NT, KINDS * HG, DH])
        ON = sb("on", [P, NT, D])
        OT = sb("ot", [P, S])

        ST = ctx.enter_context(nc.psum_tensor(L + "st", [P, 2, 2 * S], F32))
        SM = ctx.enter_context(nc.psum_tensor(L + "sm", [P, 2, S], F32))
        OA = ctx.enter_context(nc.psum_tensor(L + "oa", [P, S], F32))
        MI = ctx.enter_context(nc.psum_tensor(L + "mi", [P, S], F32))

        s_zero = sem("zero")
        s_init = sem("init")
        s_ln = sem("ln")
        s_bn = sem("bn")
        s_pow = sem("pow")
        s_pj = sem("pj")
        s_vs = sem("vs")
        s_rope = sem("rope")
        s_xt = sem("xt")
        s_pa = [sem("paq"), sem("pak")]
        s_pt = [sem("ptq"), sem("ptk")]
        s_pw = [sem("pwq"), sem("pwk")]
        s_rd = [sem(f"rd{g}") for g in range(NG)]
        s_vc = sem("vc")
        s_sm = sem("sm")
        s_mx = sem("mx")
        s_mp = sem("mp")
        s_ms = sem("ms")
        s_mr = sem("mr")
        s_mw = sem("mw")
        s_ml = sem("ml")
        s_st = sem("st")
        s_ex = sem("ex")
        s_pv = sem("pv")
        s_ev = sem("ev")
        s_no = sem("no")
        s_ot = sem("ot")
        s_res = sem("res")
        s_full = sem("full")
        MRD = 1 if causal else 2
        NNO = 2 if causal else 3
        NV = 1 if causal else 2
        NPT = 3 if causal else 2

        passed = sem("passed")
        if due:
            SL = sb("sl", [P, 2 * NT], U32)
            YG = sb("yg", [P, 2, NT, D])
            s_sl = sem("sl")
            s_yg = sem("yg")
            s_in = sem("in")
        sdram, mdram = scratch

        def slot(part, g):
            ev = []
            has_prev = not (part == "first" and g == 0)
            has1 = not (part == "last" and g == NG - 1)
            has2 = not (part == "last" and g >= NG - 2)
            has_next = part != "last"
            half = U // 2
            late = [round(i * (SMU - AHEAD) / CUT) for i in range(CUT + 1)]
            early = [round(i * AHEAD / (U - CUT)) for i in range(U - CUT + 1)]
            at = {}

            def put(i, *steps):
                at.setdefault(i, []).extend(steps)

            if due and has_next and g == 2:
                put(2, ("results", 2))
            if g == 0:
                put(-1, ("stacks", 0, 3))
            if has_next and g == 2:
                put(0, ("stacks", 1, 0), ("stacks", 1, 1))
            if has_next and g == 3:
                put(0, ("stacks", 1, 2))
            if has_prev:
                put(1, ("pv", -1, R - 1))
                put(3 if not causal else 2, ("evac", -1))
                put(4 if not causal else 3, ("sel", -1))
            put(5, ("pv", 0, 0))
            if not causal:
                put(9, ("pv", 0, 1))
            if has1:
                put(CUT - 1, ("maxima", 1))
                put(CUT + (0 if causal else 1), ("rows", 1))
            if g == 0 and part != "first":
                put(8 if not causal else 6, ("heads_T", -1))
                put(10 if not causal else 7, ("out_proj", -1))
            if has_next:
                if g == 0:
                    put(1 if causal else 0, ("norm_stats", 1))
                    put(3 if causal else 1, ("norm_rows", 1))
                if causal:
                    if g == 0:
                        put(4, ("xT", 1))
                        put(5, ("proj", 1, 0))
                        put(6, ("rot", 1, 0), ("parts", 1, 0))
                        put(7, ("part1", 1, 0))
                    if g == 1:
                        put(0, ("proj", 1, 1), ("rot", 1, 1), ("parts", 1, 1), ("part2", 1, 0))
                        put(1, ("part1", 1, 1), ("parts_out", 1, 0))
                        put(2, ("part2", 1, 1))
                        put(3, ("parts_out", 1, 1))
                else:
                    if g == 0:
                        put(6, ("xT", 1))
                        put(7, ("proj", 1, 0))
                        put(9, ("part1", 1, 0), ("parts", 1, 0))
                        put(11, ("part2", 1, 0))
                    if g == 1:
                        put(0, ("proj", 1, 1), ("parts_out", 1, 0))
                        put(1, ("part1", 1, 1))
                        put(2, ("parts", 1, 1))
                        put(7, ("parts_out", 1, 1))
                        put(8, ("part2", 1, 1))
                if g == 2:
                    put(1, ("values", 1, 0))
                    if not causal:
                        put(9, ("values", 1, 1))
                if g == 3:
                    put(0, ("vcopy", 1, 0), ("vcopy", 1, 1))
            if g == 0:
                put(half, ("vcopy", 0, 2))
            if g == 1:
                put(half, ("vcopy", 0, 3))
            ev += at.get(-1, [])
            for i in range(U):
                ev.append(("scores", 0, i))
                if i < CUT and has1:
                    ev += [("smax", 1, AHEAD + j) for j in range(late[i], late[i + 1])]
                if i >= CUT and has2:
                    ev += [("smax", 2, j) for j in range(early[i - CUT], early[i - CUT + 1])]
                ev += at.get(i, [])
            return ev

        prep = [("norm_stats", 0)] + ([("results", 1)] if due else []) + [("norm_rows", 0), ("xT", 0)]
        for side in range(2):
            prep.append(("proj", 0, side))
            if causal:
                prep.append(("rot", 0, side))
            prep += [("part1", 0, side), ("parts", 0, side), ("part2", 0, side), ("parts_out", 0, side)]
        prep += [("stacks", 0, 0), ("stacks", 0, 1), ("stacks", 0, 2), ("values", 0, 0)]
        if not causal:
            prep.append(("values", 0, 1))
        prep += [("vcopy", 0, 0), ("vcopy", 0, 1)]
        prep += [("smax", 0, j) for j in range(SMU)]
        prep += [("maxima", 0), ("rows", 0)]
        prep += [("smax", 1, j) for j in range(AHEAD)]
        parts = {
            "prologue": [(0, e) for e in prep],
            "tail": [(NG, e) for e in [("pv", -1, R - 1), ("evac", -1), ("sel", -1), ("heads_T", -1),
                                      ("out_proj", -1)]],
        }
        for part in ("first", "middle", "last"):
            parts[part] = [(g, e) for g in range(NG) for e in slot(part, g)]

        SEQ = {"results", "norm_stats", "norm_rows", "xT", "proj", "rot", "part1", "part2", "parts", "parts_out", "stacks",
               "values", "vcopy", "heads_T", "out_proj"}
        BANK = {"xT", "proj", "rot", "values", "rows", "sel", "heads_T", "out_proj"}
        turns = Turns(*[[(g, e) for g, e in parts[p] if e[0] in BANK] for p in
                        ("prologue", "first", "middle", "last", "tail")])

        def place(g, e, b, part):
            name, off = e[0], e[1]
            if name in SEQ:
                return (b + off,)
            gg = (0 if part == "tail" else g) + off
            return b * NG + gg, gg % NG, b + gg // NG

        def emptied(part, b, use):
            found = turns.previous(part, b, use)
            if found is None:
                return None
            part, b, (g, e) = found
            n = place(g, e, b, part)[0]
            return {
                "xT": lambda: (s_xt, n + 1),
                "proj": lambda: (s_rope, 4 * n + 2 * e[2] + 1) if causal else (s_pj, 2 * n + e[2] + 1),
                "rot": lambda: (s_rope, 4 * n + 2 * e[2] + 2),
                "values": lambda: (s_vs, NV * n + e[2] + 1),
                "rows": lambda: (s_mr, n + 1),
                "sel": lambda: (s_no, NNO * n + 2),
                "heads_T": lambda: (s_ot, n + 1),
                "out_proj": lambda: (s_res, n + 1),
            }[e[0]]()

        def walk(eng, handlers):
            def run(part, b):
                for g, e in parts[part]:
                    if e[0] not in handlers:
                        continue
                    turn = None
                    if e[0] in BANK and eng is nc.tensor:
                        free = emptied(part, b, (g, e))
                        if free:
                            eng.wait_ge(*free)
                    elif e[0] in BANK:
                        turn = turns.number(part, b, (g, e))
                    handlers[e[0]](*place(g, e, b, part), turn, *e[2:])

            run("prologue", 0)
            if eng is nc.tensor:
                eng.wait_ge(s_init, 2 * NV)
            run("first", 0)
            with eng.Fori(1, B - 1) as b:
                run("middle", b)
            run("last", B - 1)
            run("tail", B)

        def window(x, t):
            n = P // DIL
            return x.rearrange("p (f i) -> p f i", f=DIL)[:, :, t * n:(t + 1) * n]

        def e_slot(g, i):
            return (U * g + i) % NE

        def cols(r):
            a, c = 2 * r, 2 * r + 1
            return [(a, 0, S - a * P), (c, S - a * P, S - c * P)]

        block = ctx.enter_context(nc.Block())

        @block.tensor
        def _(pe):
            def xT(b, turn):
                pe.wait_ge(s_ln, 2 * b + 2)
                for t in range(NT):
                    m = pe.transpose(MI[:, t * P:(t + 1) * P], xn[:, t, :], const["ident"])
                m.then_inc(s_full, 1)

            def proj(b, turn, side):
                pe.wait_ge(s_xt, b + 1)
                pe.matmul(MI[:, :], w["qkv"][:, side * D:(side + 1) * D], xnT[:, :], start=True, stop=True
                          ).then_inc(s_full, 1)

            def rot(b, turn, side):
                pe.matmul(MI[:, :], w["rot"][:, side * D:(side + 1) * D], xnT[:, :], start=True, stop=True
                          ).then_inc(s_full, 1)

            def values(b, turn, which):
                for t in range(NT):
                    tok = xnT[:, t * P:(t + 1) * P] if which == 0 else xnT[:, t::DIL]
                    m = pe.matmul(MI[:, t * P:(t + 1) * P], tok, w["qkv"][:, 2 * D:3 * D], start=True, stop=True)
                m.then_inc(s_full, 1)

            def smax(n, g, b, turn, j):
                h, t = g * HG + j // NT, j % NT
                if j == 0:
                    pe.wait_ge(s_rd[g], 32 * b + 32)
                if not (isinstance(n, int) and n == 0 and j < 2):
                    pe.wait_ge(s_mx, SMU * n + j - 1)
                keys = (t + 1) * P if causal else S
                m = pe.matmul(SM[:, j % 2, 0:keys], QS[0:MR0, h, t * P:(t + 1) * P], KS[0:MR0, h, 0:keys],
                              start=True, stop=not causal, skip_group_check=True)
                if causal:
                    m = pe.matmul(SM[:, j % 2, t * P:keys], const["ident_b"], const["mask_q_b"], start=False, stop=True,
                                  skip_group_check=True)
                m.then_inc(s_sm, 1)

            def rows(n, g, b, turn):
                wait_apart(pe, s_ms, 4 * n + 4, passed)
                out = MI[0:MROWS, 0:S // 2].bitcast(BF16)
                for t in range(NT):
                    m = pe.transpose(out[:, t * P:(t + 1) * P], MT[:, t, :], const["ident_b"])
                m.then_inc(s_full, 1)

            def scores(n, g, b, turn, i):
                hs = i % HG
                h = g * HG + hs
                u = U * g + i
                if i == 0:
                    pe.wait_ge(s_ml, 16 * MRD * (n + 1))
                if not (isinstance(n, int) and n == 0 and i < 2):
                    pe.wait_ge(s_ex, U * n + i - 1)
                st = ST[:, u % 2, :]
                if causal:
                    for kb, at, width in cols(i // HG):
                        pe.matmul(st[:, at:at + width], KS[:, h, kb * P:(kb + 1) * P], QS[:, h, kb * P:S],
                                  start=True, stop=False, skip_group_check=True)
                        m = pe.matmul(st[:, at:at + P], const["ident_b"], const["mask_k_b"], start=False, stop=True,
                                      skip_group_check=True)
                elif i < HG:
                    for kind in range(2):
                        at = kind * S
                        pe.matmul(st[:, at:at + S], const["ones_b"][0:SPLIT, :], ML[:, g % 2, kind * HG + hs, :],
                                  start=True, stop=False, skip_group_check=True)
                        for t in range(NT):
                            q, k, out = QS[0:MR0, h, :], KS[0:MR0, h, :], st[:, at:at + S]
                            if kind == 0:
                                q, k, out = window(q, t), k[:, t * P:(t + 1) * P], window(out, t)
                            else:
                                q, k, out = q[:, t * P:(t + 1) * P], k[:, t::DIL], out[:, t * P:(t + 1) * P]
                            m = pe.matmul(out, k, q, start=False, stop=(t == NT - 1), skip_group_check=True)
                else:
                    for c in range(2):
                        kb = 2 * (i // HG - 1) + c
                        m = pe.matmul(st[:, c * S:(c + 1) * S], KS[:, h, kb * P:(kb + 1) * P], QS[:, h, :],
                                      start=True, stop=True)
                m.then_inc(s_st, 1)

            def pv(n, g, b, turn, r):
                pe.wait_ge(s_ex, U * n + HG * (r + 1))
                if r == 0:
                    pe.wait_ge(s_vc, n + 1)
                    if not (isinstance(n, int) and n == 0):
                        pe.wait_ge(s_ev, n)
                if not causal and r == 0:
                    for kind in range(2):
                        for t in range(NT):
                            for hs in range(HG):
                                out = OA[VW * hs:VW * (hs + 1), :]
                                e = E[:, e_slot(g, hs), kind * S:(kind + 1) * S]
                                if kind == 0:
                                    out, e = window(out, t), window(e, t)
                                    val = V[:, t, g * HG + hs, 2 * VC:2 * VC + VW]
                                else:
                                    out, e = out[:, t * P:(t + 1) * P], e[:, t * P:(t + 1) * P]
                                    val = VP[:, t, g * HG + hs, :]
                                m = pe.matmul(out, val, e, start=(kind == 0 and t == 0), stop=False,
                                              skip_group_check=True)
                else:
                    blocks = cols(r) if causal else [(2 * (r - 1) + c, c * S, S) for c in range(2)]
                    for kb, at, width in blocks:
                        for hs in range(HG):
                            m = pe.matmul(OA[VW * hs:VW * (hs + 1), S - width:S], V[:, kb, g * HG + hs, 0:VW],
                                          E[:, e_slot(g, HG * r + hs), at:at + width],
                                          start=(causal and kb == 0), stop=(kb == NT - 1), skip_group_check=True)
                m.then_inc(s_pv, 1)

            def sel(n, g, b, turn):
                pe.wait_ge(s_ev, n + 1)
                c = KINDS * HG * OC
                for t in range(NT):
                    m = pe.matmul(MI[:, c * t:c * (t + 1)], OS[:, g % 2, t * P:(t + 1) * P], const["pick"][:, 0:c],
                                  start=True, stop=True, skip_group_check=True)
                m.then_inc(s_full, 1)

            def heads_T(b, turn):
                pe.wait_ge(s_no, NNO * NG * (b + 1))
                for t in range(NT):
                    m = pe.transpose(MI[:, t * P:(t + 1) * P], ON[:, t, :], const["ident"])
                m.then_inc(s_full, 1)

            def out_proj(b, turn):
                pe.wait_ge(s_ot, b + 1)
                for t in range(NT):
                    m = pe.matmul(MI[:, t * P:(t + 1) * P], OT[:, t * P:(t + 1) * P], w["out"], start=True, stop=True)
                m.then_inc(s_full, 1)

            walk(pe, dict(xT=xT, proj=proj, rot=rot, values=values, smax=smax, rows=rows, scores=scores, pv=pv,
                          sel=sel, heads_T=heads_T, out_proj=out_proj))

        @block.scalar
        def _(act):
            def xT(b, turn):
                if not (isinstance(b, int) and b == 0):
                    act.wait_ge(s_vs, NV * b)
                lay(turn, xnT[:, :], s_xt)

            def lay(turn, out, done, order=None):
                got = MI[:, :]
                if order and not causal:
                    out, got = order(out, got)
                act.wait_ge(s_full, turn + 1)
                act.activation(out, got, ACT.Copy).then_inc(done, 1)

            def to_phases(out, got):
                return out.rearrange("p (f i) -> p f i", f=DIL), got.rearrange("p (i f) -> p f i", f=DIL)

            def from_phases(out, got):
                return out.rearrange("p (i f) -> p f i", f=DIL), got.rearrange("p (f i) -> p f i", f=DIL)

            def proj(b, turn, side):
                if causal:
                    return
                if not (isinstance(b, int) and b == 0):
                    act.wait_ge(s_pt[side], NPT * b)
                lay(turn, QK[:, side, :], s_pj, None if side else to_phases)

            def part1(b, turn, side):
                if causal:
                    act.wait_ge(s_pt[side], NPT * b + 1)
                else:
                    act.wait_ge(s_pj, 2 * b + side + 1)
                if not (isinstance(b, int) and b == 0):
                    act.wait_ge(s_pw[side], 16 * SPLIT * SPLIT * b)
                act.activation(PT[:, side, 0, :], QK[:, side, :], ACT.Copy).then_inc(s_pa[side], 1)

            def part2(b, turn, side):
                act.wait_ge(s_pt[side], NPT * b + NPT - 1)
                act.activation(PT[:, side, 1, :], QR[:, side, :], ACT.Copy).then_inc(s_pa[side], 1)

            def values(b, turn, which):
                if not (isinstance(b, int) and b == 0):
                    act.wait_ge(s_vc, NG * b)
                lay(turn, VS[:, which, :, :].rearrange("p t d -> p (t d)"), s_vs)

            def scores(n, g, b, turn, i):
                act.wait_ge(s_st, U * n + i + 1)
                r = i // HG
                if not (isinstance(n, int) and U * n + i < NE):
                    act.wait_ge(s_pv, R * n + r - 1)
                width = (sum(c[2] for c in cols(r)) if causal else 2 * S)
                act.activation(E[:, e_slot(g, i), 0:width], ST[:, (U * g + i) % 2, 0:width], ACT.Exp, scale=SCALE
                               ).then_inc(s_ex, 1)

            def evac(n, g, b, turn):
                act.wait_ge(s_pv, R * n + R)
                if not (isinstance(n, int) and n < 2):
                    act.wait_ge(s_no, NNO * (n - 1))
                act.activation(OS[:, g % 2, :], OA[:, :], ACT.Copy).then_inc(s_ev, 1)

            def heads_T(b, turn):
                lay(turn, OT[:, :], s_ot, from_phases)

            walk(act, dict(xT=xT, proj=proj, part1=part1, part2=part2, values=values, scores=scores, evac=evac,
                           heads_T=heads_T))

        @block.vector
        def _(dve):
            def results(b, turn):
                dve.tensor_copy(SL[:, :].rearrange("p (j t) -> p j t", j=2), due[0][:, :, bass.ds(b * NT, NT)]
                                ).then_inc(s_sl, 1)

            def norm_stats(b, turn):
                for j in range(2) if due else ():
                    if j == 0:
                        dve.wait_ge(s_yg, 16 * 2 * NT * (b + 1))
                    else:
                        dve.wait_ge(s_in, 2 * b + 1)
                    for t in range(NT):
                        now = X[:, b * NT + t, :]
                        m = dve.scalar_tensor_tensor(now, YG[:, j, t, :], due[1][:, j, bass.ds(b * NT + t, 1)], now,
                                                     ALU.mult, ALU.add)
                    m.then_inc(s_in, 1)
                if due:
                    wait_apart(dve, s_in, 2 * b + 2, passed)
                for t in range(NT):
                    dve.bn_stats(stats[:, t, :], X[:, b * NT + t, :]).then_inc(s_bn, 1)
                wait_apart(dve, s_bn, NT * (b + 1), passed)
                for t in range(NT):
                    m = dve.bn_aggr(mv[:, t, :], stats[:, t, :])
                m.then_inc(s_ln, 1)

            def norm_rows(b, turn):
                dve.wait_ge(s_pow, 2 * b + 2)
                if not (isinstance(b, int) and b == 0):
                    dve.wait_ge(s_xt, b)
                for t in range(NT):
                    m = dve.tensor_scalar(xn[:, t, :], X[:, b * NT + t, :], mv[:, t, 0:1], rstd[:, t:t + 1],
                                          ALU.subtract, ALU.mult)
                m.then_inc(s_ln, 1)

            def rotate(b, turn, side, second):
                dve.wait_ge(s_full, turn + 1)
                out = TQ[:, 0, :] if not second else TQ[:, 1, :]
                if side:
                    dve.wait_ge(s_pt[0], NPT * b + 1)
                elif not (isinstance(b, int) and b == 0):
                    dve.wait_ge(s_pt[1], NPT * (b - 1) + 1)
                dve.tensor_tensor(out, MI[:, :], const["sin"] if second else const["cos"], ALU.mult
                                  ).then_inc(s_rope, 1)

            def proj(b, turn, side):
                if causal:
                    rotate(b, turn, side, 0)

            def rot(b, turn, side):
                rotate(b, turn, side, 1)

            def smax(n, g, b, turn, j):
                hs, t = j // NT, j % NT
                dve.wait_ge(s_sm, SMU * n + j + 1)
                if causal and j == 0 and not (isinstance(n, int) and n == 0):
                    dve.wait_ge(s_ms, 4 * n)
                if causal:
                    dve.tensor_reduce(NM[:, hs, t:t + 1], SM[:, j % 2, 0:(t + 1) * P], AX.X, ALU.max, negate=True
                                      ).then_inc(s_mx, 1)
                else:
                    dve.tensor_reduce(M[:, hs, t, :].rearrange("p (w f) -> p w f", f=DIL),
                                      SM[:, j % 2, :].rearrange("p (w i f) -> p w f i", w=NT, f=DIL), AX.X, ALU.max
                                      ).then_inc(s_mx, 1)

            def maxima(n, g, b, turn):
                dve.wait_ge(s_mx, SMU * (n + 1))
                if causal:
                    return maxima_parts(n)
                if not (isinstance(n, int) and n == 0):
                    dve.wait_ge(s_ms, 4 * n)
                flat = M[:, :, :, :].rearrange("p h t k -> p (h t) k")
                dve.tensor_reduce(NM[:, 0:HG, :].rearrange("p h t -> p (h t)"), flat, AX.X, ALU.max, negate=True
                                  ).then_inc(s_mp, 1)
                dve.tensor_tensor(MD[:, :, :, :].rearrange("p h t k -> p (h t) k"), flat,
                                  const["window"].rearrange("p (a k) -> p a k", a=1).broadcast_to(
                                      [P, HG * NT, NT * DIL]),
                                  ALU.min).then_inc(s_mp, 1)
                step = NT * DIL
                own = bass.AP(M, 0, [[HG * NT * step, P], [NT * step, HG], [step + 1, DIL], [DIL, NT]])
                dve.tensor_reduce(NM[:, 2 * HG:3 * HG, :], own, AX.X, ALU.max, negate=True).then_inc(s_mp, 1)
                dve.wait_ge(s_mp, 4 * n + 3)
                dve.tensor_reduce(NM[:, HG:2 * HG, :].rearrange("p h t -> p (h t)"),
                                  MD[:, :, :, :].rearrange("p h t k -> p (h t) k"), AX.X, ALU.max, negate=True
                                  ).then_inc(s_mp, 1)
                dve.wait_ge(s_mp, 4 * n + 4)
                maxima_parts(n)

            def maxima_parts(n):
                if not (isinstance(n, int) and n == 0):
                    dve.wait_ge(s_mr, n)
                part = MT[:, :, :].rearrange("p t (k s) -> p s k t", s=SPLIT)
                for i in range(SPLIT):
                    last = NM if i == 0 else NR
                    if i < SPLIT - 1:
                        dve.tensor_copy(part[:, i], last[:, :, :]).then_inc(s_ms, 1)
                        dve.wait_ge(s_ms, 4 * n + 2 * i + 1)
                    to = NR[:, :, :] if i == 0 else part[:, SPLIT - 1]
                    if i < SPLIT - 1:
                        dve.tensor_tensor(to, last[:, :, :], part[:, i], ALU.subtract).then_inc(s_ms, 1)
                    if i == 0:
                        dve.wait_ge(s_ms, 4 * n + 2)

            def rows(n, g, b, turn):
                dve.wait_ge(s_full, turn + 1)
                if not (isinstance(n, int) and n == 0):
                    dve.wait_ge(s_mw, 16 * n)
                dve.tensor_copy(MR[:, :], MI[0:MROWS, 0:S // 2].bitcast(BF16)).then_inc(s_mr, 1)

            def sel(n, g, b, turn):
                dve.wait_ge(s_full, turn + 1)
                k = KINDS * HG
                got = MI[:, 0:NT * k * OC].rearrange("p (t k c) -> p t k c", t=NT, k=k)
                dve.reciprocal(RL[:, :, :, :], got[:, :, :, DH:OC]).then_inc(s_no, 1)
                dve.wait_ge(s_no, NNO * n + 1)
                if not (isinstance(b, int) and b == 0):
                    dve.wait_ge(s_ot, b)
                out = ON[:, :, g * HG * DH:(g + 1) * HG * DH]
                to = out.rearrange("p t (h c) -> p t h c", h=HG) if causal else PR[:, :, :, :]
                dve.tensor_tensor(to, got[:, :, :, 0:DH], RL[:, :, :, :].broadcast_to([P, NT, k, DH]), ALU.mult
                                  ).then_inc(s_no, 1)
                if causal:
                    return
                dve.wait_ge(s_no, NNO * n + 2)
                dve.tensor_reduce(out, PR[:, :, :, :].rearrange("p t (k h) c -> p t (h c) k", k=KINDS), AX.X,
                                  ALU.add).then_inc(s_no, 1)

            def out_proj(b, turn):
                dve.wait_ge(s_full, turn + 1)
                now = X[:, bass.ds(b * NT, NT), :].rearrange("p t d -> p (t d)")
                dve.tensor_tensor(now, now, MI[:, :], ALU.add).then_inc(s_res, 1)

            if due:
                results(0, None)
            dve.memset(QS[:, :, :], 0.0).then_inc(s_zero, 1)
            walk(dve, dict(results=results, norm_stats=norm_stats, norm_rows=norm_rows, proj=proj, rot=rot,
                           smax=smax, maxima=maxima, rows=rows, sel=sel, out_proj=out_proj))
            if due:
                dve.wait_ge(s_yg, 16 * 2 * NT * (B + 1))

        @block.gpsimd
        def _(pool):
            def results(b, turn):
                wait_apart(pool, s_sl, b + 1, passed)
                for j in range(2):
                    for t in range(NT):
                        at = bass.IndirectOffsetOnAxis(ap=SL[:, j * NT + t:j * NT + t + 1], axis=0)
                        pool.indirect_dma_start(YG[:, j, t, :], None, due[2], at).then_inc(s_yg, 16)

            if due:
                results(0, None)
            def norm_rows(b, turn):
                wait_apart(pool, s_ln, 2 * b + 1, passed)
                pool.tensor_scalar(rstd[:, :], mv[:, :, 1], EPS, None, ALU.add).then_inc(s_pow, 1)
                pool.wait_ge(s_pow, 2 * b + 1)
                pool.tensor_tensor(rstd[:, :], rstd[:, :], const["minus_half"][:, 0:NT], ALU.pow).then_inc(s_pow, 1)

            norm_rows(0, None)
            pool.memset(KS[:, :, :], 1.0).then_inc(s_zero, 1)
            layouts = ((V, 2 * VC),) if causal else ((V, 2 * VC), (VP, KC))
            for val, _ in layouts:
                pool.memset(val[:, :, :, :], 0.0).then_inc(s_init, 1)
            pool.wait_ge(s_init, NV)
            for val, c in layouts:
                pool.memset(val[:, :, :, c + DH:c + OC], float(KINDS)).then_inc(s_init, 1)

            def parts_(b, turn, side):
                q, r, pt = QK[:, side, :], QR[:, side, :], PT[:, side, :, :]
                if causal:
                    pool.wait_ge(s_rope, 4 * b + 2 * side + 2)
                    pool.tensor_tensor(q, TQ[:, 0, :], TQ[:, 1, :], ALU.add).then_inc(s_pt[side], 1)
                pool.wait_ge(s_pa[side], 2 * b + 1)
                pool.tensor_tensor(r, q, pt[:, 0, :], ALU.subtract).then_inc(s_pt[side], 1)
                pool.wait_ge(s_pa[side], 2 * b + 2)
                pool.tensor_tensor(pt[:, 2, :], r, pt[:, 1, :], ALU.subtract).then_inc(s_pt[side], 1)

            def vcopy(b, turn, g):
                pool.wait_ge(s_vs, NV * (b + 1))
                if not (isinstance(b, int) and b == 0):
                    wait_apart(pool, s_pv, R * (NG * (b - 1) + g + 1), passed)
                for which, (val, c) in enumerate(layouts):
                    m = pool.tensor_copy(val[:, :, g * HG:(g + 1) * HG, c:c + DH],
                                         VS[:, which, :, g * HG * DH:(g + 1) * HG * DH].rearrange(
                                             "p t (h c) -> p t h c", h=HG))
                m.then_inc(s_vc, 1)

            def later_rows(b, turn):
                if not (isinstance(b, int) and b == 0):
                    norm_rows(b, turn)

            walk(pool, dict(results=results, norm_rows=later_rows, parts=parts_, vcopy=vcopy))

        @block.sync
        def _(sp):
            sp.wait_ge(s_zero, 2)

            def parts_out(b, turn, side):
                wait_apart(sp, s_pt[side], NPT * (b + 1), passed)
                if side == 0 and not (isinstance(b, int) and b == 0):
                    for g in range(NG):
                        wait_apart(sp, s_rd[g], 32 * b, passed)
                for a in range(SPLIT):
                    for c in range(SPLIT):
                        r = (a * SPLIT + c) * DH
                        sp.dma_start(sdram[side, r:r + DH].rearrange("d h n -> h d n"),
                                     PT[:, side, (a, c)[side], :]).then_inc(s_pw[side], 16)

            def stacks(b, turn, g):
                if not (isinstance(b, int) and b == 0):
                    wait_apart(sp, s_st, U * (NG * (b - 1) + g + 1), passed)
                for side, dst in ((0, QS), (1, KS)):
                    wait_apart(sp, s_pw[side], 16 * SPLIT * SPLIT * (b + 1), passed)
                    sp.dma_start(dst[0:KR, g * HG:(g + 1) * HG, :], sdram[side, :, g * HG:(g + 1) * HG, :]
                                 ).then_inc(s_rd[g], 16)

            def rows(n, g, b, turn):
                wait_apart(sp, s_mr, n + 1, passed)
                if not (isinstance(n, int) and n == 0):
                    wait_apart(sp, s_ml, 16 * MRD * n, passed)
                sp.dma_start(mdram, MR[:, :]).then_inc(s_mw, 16)
                wait_apart(sp, s_mw, 16 * (n + 1), passed)
                if not (isinstance(n, int) and n < 2):
                    wait_apart(sp, s_st, U * (n - 1), passed)
                rows_ = mdram.rearrange("(k s) n -> s k n", s=SPLIT)
                sp.dma_start(QS[MR0:MR0 + SPLIT, g * HG:(g + 1) * HG, :], rows_[:, 0:HG, :]).then_inc(s_ml, 16)
                if not causal:
                    sp.dma_start(ML[:, g % 2, :, :], rows_[:, HG:3 * HG, :]).then_inc(s_ml, 16)

            walk(sp, dict(parts_out=parts_out, stacks=stacks, rows=rows))


def constants():
    import numpy as np
    p = np.arange(P)
    big = np.float32(1e30)
    freqs = (1.0 / np.float32(10000.0) ** (np.arange(0, DH, 2, dtype=np.float32) / DH)).astype(np.float32)
    angle = np.outer(freqs[(p % DH) // 2], np.arange(S, dtype=np.float32)).astype(np.float32)
    pick = np.zeros((P, 3, HG, OC), np.float32)
    for k in range(3):
        for h in range(HG):
            for c in range(OC):
                pick[h * VW + KC * k + c, k, h, c] = 1.0
    parts = {
        "ident": np.eye(P, dtype=np.float32),
        "mask_q": np.where(p[None, :] <= p[:, None], np.float32(0), -big),
        "mask_k": np.where(p[:, None] <= p[None, :], np.float32(0), -big),
        "window": np.where(p[:, None] // (P // NT) == np.arange(NT * DIL)[None, :] // DIL, np.float32(3e38),
                           np.float32(-3e38)),
        "pick": pick.reshape(P, 3 * HG * OC),
        "minus_half": np.full((P, B * NT), -0.5, np.float32),
        "before": np.where(p[:, None] < p[None, :], np.float32(1), np.float32(0)),
        "column_less": np.tile(np.arange(8, dtype=np.float32) - 8, (P, 1)),
        "base": np.tile((B * S + P) * np.arange(8, dtype=np.float32), (P, 1)),
        "row": p[:, None].astype(np.float32),
        "steps": np.tile(P * np.arange(B * NT, dtype=np.float32), (P, 1)),
        "upto": np.tile((np.arange(8)[None, :] <= np.arange(8)[:, None]).astype(np.float32).reshape(1, 64), (P, 1)),
        "block": np.tile(np.arange(72, dtype=np.float32), (P, 1)),
        "base_block": np.tile((B * S + P) // P * np.arange(8, dtype=np.float32), (P, 1)),
        "powers": np.tile(8.0 ** np.arange(6, dtype=np.float32), (P, 1)),
        "ones": np.ones((P, P), np.float32),
        "column": np.tile(np.arange(8, dtype=np.float32), (P, 1)),
        "cos": np.cos(angle),
        "sin": np.sin(angle),
    }
    at, n = {}, 0
    for name, a in parts.items():
        at[name] = (n, n + a.shape[1])
        n += a.shape[1]
    return np.concatenate([a.astype(np.float32) for a in parts.values()], axis=1), at


def setup(nc, ctx, c_dram, at, x_dram, X, w0qkv, w0out, w1qkv, w1out):
    def sb(name, shape, dt=F32):
        return ctx.enter_context(nc.sbuf_tensor(name, shape, dt))

    C = sb("const", [P, c_dram.shape[1]])
    CB = sb("const_b", [P, 5 * P], BF16)
    W0 = sb("w0", [P, 3 * D])
    WO0 = sb("wo0", [P, D])
    W1 = sb("w1t", [P, 3 * D])
    WR1 = sb("w1r", [P, 2 * D])
    WO1 = sb("wo1", [P, D])
    const = {name: C[:, a:b] for name, (a, b) in at.items()}
    for i, name in enumerate(("ident", "mask_q", "mask_k", "ones", "before")):
        const[name + "_b"] = CB[:, i * P:(i + 1) * P]
    with nc.cleanup_on_exit(), ExitStack() as inner:
        raw = inner.enter_context(nc.sbuf_tensor("w1raw", [P, 4, D], F32))
        ps = inner.enter_context(nc.psum_tensor("w1ps", [P, 4 * D], F32))
        s_c, s_x, s_w, s_raw, s_cb, s_t, s_v = (nc.alloc_semaphore(name="su_" + n) for n in
                                          ("c", "x", "w", "raw", "cb", "t", "v"))
        block = inner.enter_context(nc.Block())

        @block.sync
        def _(sp):
            sp.dma_start(C[:, :], c_dram).then_inc(s_c, 16)
            sp.dma_start(X[:, 0:NT, :], x_dram[0].rearrange("(t p) d -> p t d", p=P)).then_inc(s_x, 16)
            sp.dma_start(raw[:, 0:3, :], w1qkv.rearrange("(t p) i -> p t i", p=P)).then_inc(s_raw, 16)
            sp.dma_start(raw[:, 3, :], w1out).then_inc(s_raw, 16)
            sp.dma_start(W0[:, :], w0qkv).then_inc(s_w, 16)
            sp.dma_start(WO0[:, :], w0out).then_inc(s_w, 16)
            for b in range(1, B):
                sp.dma_start(X[:, b * NT:(b + 1) * NT, :], x_dram[b].rearrange("(t p) d -> p t d", p=P)
                             ).then_inc(s_x, 16)
            sp.wait_ge(s_w, 32)
            sp.wait_ge(s_x, 16 * B)

        @block.vector
        def _(dve):
            dve.wait_ge(s_c, 16)
            for i, name in enumerate(("ident", "mask_q", "mask_k", "ones", "before")):
                dve.tensor_copy(CB[:, i * P:(i + 1) * P], const[name]).then_inc(s_cb, 1)
            dve.wait_ge(s_t, 1)
            dve.tensor_copy(W1[:, :], ps[:, 0:3 * D]).then_inc(s_v, 1)
            dve.tensor_copy(WO1[:, :], ps[:, 3 * D:4 * D]).then_inc(s_v, 1)
            pairs = ps[:, 0:2 * D].rearrange("p (f two) -> p f two", two=2)
            turned = WR1[:, :].rearrange("p (f two) -> p f two", two=2)
            dve.tensor_scalar(turned[:, :, 0], pairs[:, :, 1], -1.0, None, ALU.mult).then_inc(s_v, 1)
            dve.tensor_copy(turned[:, :, 1], pairs[:, :, 0]).then_inc(s_v, 1)

        @block.tensor
        def _(pe):
            pe.wait_ge(s_c, 16)
            pe.wait_ge(s_raw, 32)
            for t in range(4):
                m = pe.transpose(ps[:, t * P:(t + 1) * P], raw[:, t, :], const["ident"])
            m.then_inc(s_t, 1)

    return const, {"qkv": W0[:, :], "out": WO0[:, :]}, {"qkv": W1[:, :], "rot": WR1[:, :], "out": WO1[:, :]}


NE0 = 7
F0 = 512
NX0 = NE0 + 1
HB0 = F0 // P
NE1 = 8
F1 = 256
HB1 = F1 // P
ROUNDS = 2
BOOST = 0.5
TOP = 8
BLOCKS0 = 72
BLOCKS1 = 40


class Norm:

    def __init__(self, nc, ctx, name, minus_half, passed):
        self.passed = passed
        self.half = minus_half
        self.stats = ctx.enter_context(nc.sbuf_tensor(name + "stats", [P, NT, 6], F32))
        self.mv = ctx.enter_context(nc.sbuf_tensor(name + "mv", [P, NT, 2], F32))
        self.rstd = ctx.enter_context(nc.sbuf_tensor(name + "rstd", [P, NT], F32))
        self.s_bn, self.s_mv, self.s_pow, self.s_out = (nc.alloc_semaphore(name=name + n)
                                                        for n in ("bn", "mv", "pow", "out"))

    def vector_stats(self, dve, k, tile):
        for t in range(NT):
            dve.bn_stats(self.stats[:, t, :], tile(t)).then_inc(self.s_bn, 1)
        wait_apart(dve, self.s_bn, NT * (k + 1), self.passed)
        for t in range(NT):
            m = dve.bn_aggr(self.mv[:, t, :], self.stats[:, t, :])
        m.then_inc(self.s_mv, 1)

    def pool(self, pool, k):
        if not (isinstance(k, int) and k == 0):
            pool.wait_ge(self.s_out, k)
        wait_apart(pool, self.s_mv, k + 1, self.passed)
        pool.tensor_scalar(self.rstd[:, :], self.mv[:, :, 1], EPS, None, ALU.add).then_inc(self.s_pow, 1)
        pool.wait_ge(self.s_pow, 2 * k + 1)
        pool.tensor_tensor(self.rstd[:, :], self.rstd[:, :], self.half, ALU.pow).then_inc(self.s_pow, 1)

    def vector_rows(self, dve, k, tile, out):
        dve.wait_ge(self.s_pow, 2 * k + 2)
        for t in range(NT):
            m = dve.tensor_scalar(out(t), tile(t), self.mv[:, t, 0:1], self.rstd[:, t:t + 1],
                                  ALU.subtract, ALU.mult)
        m.then_inc(self.s_out, 1)


def norm_all(dve, norm, X, xn, s_tp, s_cp):
    def sequence(b):
        def rows(t):
            return X[:, b * NT + t, :]
        norm.vector_stats(dve, b, rows)
        if not isinstance(b, int):
            dve.wait_ge(s_tp, b)
            dve.wait_ge(s_cp, b)
        norm.vector_rows(dve, b, rows, lambda t: xn[:, t, :])

    sequence(0)
    with dve.Fori(1, B) as b:
        sequence(b)


TT = B * NT
CAP = B * S + P
UN = 4
EBITS = 3
RBITS = 9


class Steps:

    def __init__(self, eng, sem):
        self.eng, self.sem, self.n = eng, sem, 0

    def wait(self):
        if self.n:
            self.eng.wait_ge(self.sem, self.n)

    def __call__(self, op, *args, **kw):
        self.wait()
        return self.did(op(*args, **kw))

    def did(self, instruction):
        instruction.then_inc(self.sem, 1)
        self.n += 1
        return self.n


def across(x, shape):
    return x.rearrange("p (a e) -> p a e", a=1).broadcast_to(shape)


class Routing:

    def __init__(self, nc, ctx, name, const, experts, together, blocks, slots=None):
        def sb(n, shape, dt=F32):
            return ctx.enter_context(nc.sbuf_tensor(name + n, shape, dt))
        self.const, self.E, self.together, self.N = const, experts, together, blocks
        self.sets = 1 if together else 2
        self.V = sb("V", [P, TT, TOP])
        self.EQ = sb("EQ", [P, TT, TOP])
        self.BEST = sb("BEST", [P, 2, TT])
        self.LOW = sb("LOW", [P, TT])
        self.HOT = sb("HOT", [P, 2, TT, TOP])
        self.HB = sb("HB", [P, self.sets, TT, TOP], BF16)
        self.AT = sb("AT", [P, TT, TOP])
        self.DEST = sb("DEST", [P, 2, TT])
        self.IDX = sb("IDX", [P, 2, TT], U32)
        self.SLOT = slots or sb("SLOT", [P, 2, TT], U32)
        self.PAD = sb("PAD", [P, self.sets, TOP], U32)
        self.PF = sb("PF", [P, TOP])
        self.CNT = sb("CNT", [P, TOP])
        self.GT = sb("GT", [P, TOP, TT])
        self.NB = sb("NB", [P, TOP])
        self.SQ = sb("SQ", [P, TOP, TOP])
        self.END = sb("END", [P, TOP])
        self.BEG = sb("BEG", [P, TOP])
        self.K = sb("K", [P, TOP])
        self.GE = sb("GE", [P, blocks, TOP])
        self.ON = sb("ON", [P, blocks, TOP])
        self.RJ = sb("RJ", [P, blocks, TOP])
        self.EJ = sb("EJ", [P, blocks + 2 * UN])
        self.RB = sb("RB", [P, blocks])
        words = blocks // UN + 1
        self.WE = sb("WE", [P, words, UN + 2])
        self.WF = sb("WF", [P, words + blocks // 2])
        self.TAB = sb("TAB", [P, self.sets, words + blocks // 2], I32)

    def choose(self, st, dve):
        wide = [P, TT, TOP]
        V, EQ, LOW = self.V[:, :, :], self.EQ[:, :, :], self.LOW
        for j in range(2):
            best = self.BEST[:, j, :]
            st(dve.tensor_reduce, best, V, AX.X, ALU.max)
            st(dve.tensor_tensor, EQ, V, best.rearrange("p (t a) -> p t a", a=1).broadcast_to(wide), ALU.is_equal)
            st(dve.tensor_tensor, EQ, EQ, across(self.const["column_less"], wide), ALU.mult)
            st(dve.tensor_reduce, LOW[:, :], EQ, AX.X, ALU.min)
            st(dve.tensor_tensor, self.HOT[:, j, :, :], EQ,
               LOW[:, :].rearrange("p (t a) -> p t a", a=1).broadcast_to(wide), ALU.is_equal)
            if j == 0:
                st(dve.tensor_scalar, EQ, self.HOT[:, 0, :, :], 0.5, -3e38, ALU.subtract, ALU.mult)
                st(dve.tensor_tensor, V, V, EQ, ALU.min)
        if self.together:
            return st(dve.tensor_tensor, self.HB[:, 0, :, :], self.HOT[:, 0, :, :], self.HOT[:, 1, :, :], ALU.add)
        return st(dve.tensor_copy, self.HB[:, :, :, :], self.HOT[:, :, :, :])

    def count(self, pe, PO, sem):
        for i in range(self.sets):
            pe.matmul(PO[:, i, 0:TT, :], self.const["before_b"], self.HB[:, i, :, :], start=True, stop=False,
                      skip_group_check=True)
            for t in range(TT):
                m = pe.matmul(PO[:, i, t + 1:TT + 1, :], self.const["ones_b"],
                              self.HB[:, i, t:t + 1, :].broadcast_to([P, TT - t, TOP]), start=False,
                              stop=(t == TT - 1), skip_group_check=True)
        m.then_inc(sem, 1)

    def place(self, st, dve, PO):
        wide = [P, TT, TOP]
        base = self.const["base"]
        for j in range(2):
            if j < self.sets:
                st(dve.tensor_tensor, self.AT[:, :, :], PO[:, j, 0:TT, :], across(base, wide), ALU.add)
            st(dve.tensor_tensor, self.EQ[:, :, :], self.AT[:, :, :], self.HOT[:, j, :, :], ALU.mult)
            st(dve.tensor_reduce, self.DEST[:, j, :], self.EQ[:, :, :], AX.X, ALU.add)
        st(dve.tensor_copy, self.IDX[:, :, :], self.DEST[:, :, :])
        for i in range(self.sets):
            st(dve.tensor_tensor, self.PF[:, :], PO[:, i, TT, :], base, ALU.add)
            n = st(dve.tensor_scalar, self.PAD[:, i, :], self.PF[:, :], self.const["row"], None, ALU.add)
        return n

    def table(self, st, dve, PO):
        E, N, const = self.E, self.N, self.const
        for i in range(self.sets):
            st(dve.tensor_copy, self.CNT[:, :], PO[:, i, TT, :])
            st(dve.tensor_tensor, self.GT[:, :, :], self.CNT[:, :].rearrange("p (e a) -> p e a", a=1).broadcast_to(
                [P, TOP, TT]), across(const["steps"], [P, TOP, TT]), ALU.is_gt)
            st(dve.tensor_reduce, self.NB[:, :], self.GT[:, :, :], AX.X, ALU.add)
            st(dve.tensor_tensor, self.SQ[:, :, :], across(self.NB[:, :], [P, TOP, TOP]),
               const["upto"].rearrange("p (a e) -> p a e", a=TOP), ALU.mult)
            st(dve.tensor_reduce, self.END[:, :], self.SQ[:, :, :], AX.X, ALU.add)
            st(dve.tensor_tensor, self.BEG[:, :], self.END[:, :], self.NB[:, :], ALU.subtract)
            st(dve.tensor_tensor, self.K[:, :], const["base_block"], self.BEG[:, :], ALU.subtract)
            shape = [P, N, E]
            block = const["block"][:, 0:N].rearrange("p (j a) -> p j a", a=1).broadcast_to(shape)
            GE, ON, RJ = (x[:, :, 0:E] for x in (self.GE, self.ON, self.RJ))
            st(dve.tensor_tensor, GE, block, across(self.END[:, 0:E], shape), ALU.is_ge)
            st(dve.tensor_tensor, ON, block, across(self.BEG[:, 0:E], shape), ALU.is_ge)
            st(dve.tensor_tensor, ON, ON, GE, ALU.subtract)
            st(dve.tensor_tensor, RJ, block, across(self.K[:, 0:E], shape), ALU.add)
            st(dve.tensor_tensor, RJ, RJ, ON, ALU.mult)
            st(dve.memset, self.EJ[:, :], 0.0)
            st(dve.tensor_reduce, self.EJ[:, 2:2 + N], GE, AX.X, ALU.add)
            st(dve.tensor_scalar, self.EJ[:, :], self.EJ[:, :], float(TOP - 1), None, ALU.min)
            st(dve.tensor_reduce, self.RB[:, :], RJ, AX.X, ALU.add)
            W = N // UN + 1
            st(dve.tensor_tensor, self.WE[:, :, :], bass.AP(self.EJ, 0, [[N + 2 * UN, P], [UN, W], [1, UN + 2]]),
               const["powers"].rearrange("p (a d) -> p a d", a=1).broadcast_to([P, W, UN + 2]), ALU.mult)
            st(dve.tensor_reduce, self.WF[:, 0:W], self.WE[:, :, :], AX.X, ALU.add)
            pairs = self.RB[:, :].rearrange("p (j two) -> p j two", two=2)
            st(dve.scalar_tensor_tensor, self.WF[:, W:], pairs[:, :, 1], float(1 << RBITS), pairs[:, :, 0], ALU.mult,
               ALU.add)
            n = st(dve.tensor_copy, self.TAB[:, i, :], self.WF[:, :])
            for j in range(2) if self.together else (i,):
                st(dve.tensor_tensor, self.EQ[:, :, :], self.HOT[:, j, :, :], across(self.K[:, :], [P, TT, TOP]),
                   ALU.mult)
                st(dve.tensor_reduce, self.LOW[:, :], self.EQ[:, :, :], AX.X, ALU.add)
                n = st(dve.scalar_tensor_tensor, self.SLOT[:, j, 0:TT], self.LOW[:, :], float(-P), self.DEST[:, j, :],
                       ALU.mult, ALU.add)
        return n

    def scatter(self, pool, x, rows, sem, choices):
        for t in range(TT):
            for j in choices:
                at = bass.IndirectOffsetOnAxis(ap=self.IDX[:, j, t:t + 1], axis=0)
                pool.indirect_dma_start(rows, at, x(t), None).then_inc(sem, 16)
        return 16 * TT * len(choices)

    def pad(self, pool, zeros, rows, sem, i):
        for e in range(self.E):
            at = bass.IndirectOffsetOnAxis(ap=self.PAD[:, i, e:e + 1], axis=0)
            pool.indirect_dma_start(rows, at, zeros, None).then_inc(sem, 16)
        return 16 * self.E


def block_pass(nc, L, const, table, rows, results, blocks, weights, down, width, bias=None, meanwhile=None):
    F = width
    HB = F // P
    N = blocks
    gated = bias is None
    with nc.cleanup_on_exit(), ExitStack() as ctx:
        def sb(name, shape, dt=F32):
            return ctx.enter_context(nc.sbuf_tensor(L + name, shape, dt))

        def sem(name):
            return nc.alloc_semaphore(name=L + name)

        def ps(name, shape):
            return ctx.enter_context(nc.psum_tensor(L + name, shape, F32))

        XB = sb("xb", [P, UN, D])
        XT = sb("xt", [P, 2, P])
        SG = sb("sg", [P, 2, F])
        HH = sb("hh", [P, 2, F])
        HT = sb("ht", [P, 2, F])
        YS = sb("ys", [P, UN, D])
        UP = ps("up", [P, 2, len(weights), S])
        TX = ps("tx", [P, S])
        TH = ps("th", [P, S])
        Y = ps("y", [P, 2, S])
        s_in = [sem(f"in{i}") for i in range(UN)]
        s_out = [sem(f"ot{i}") for i in range(UN)]
        s_tx = sem("stx")
        s_xt = sem("sxt")
        s_up = sem("sup")
        s_sg = sem("ssg")
        s_h = sem("sh")
        s_th = sem("sth")
        s_ht = sem("sht")
        s_y = sem("sy")
        s_ys = sem("sys")
        passed = sem("passed")
        block = ctx.enter_context(nc.Block())

        def walk(eng, step, lag, first=1, last=0, field=None):
            def load(k):
                def word(at):
                    return eng.value_load(table[0:1, bass.ds(at, 1)], min_val=0, max_val=(1 << 18) - 1)
                if field == "expert":
                    return [word(k)]
                if field == "row" and (not isinstance(k, int) or k < N // UN):
                    return [word(N // UN + 1 + k * (UN // 2) + i) for i in range(UN // 2)]
                return []

            def take(words, place):
                if field == "expert":
                    return (words[0] >> (EBITS * (place + 2))) & (TOP - 1)
                return ((words[place // 2] >> (RBITS * (place % 2))) & ((1 << RBITS) - 1)) * P

            def run(steps):
                for i in steps:
                    if i % UN == 0:
                        run.words = load(i // UN)
                    step(i // UN, i % UN, lambda d: 0 <= i - d < N, lambda d: take(run.words, i % UN - d))

            run(range(first * UN))
            with eng.Fori(first, N // UN - last) as k:
                words = load(k)
                for u in range(UN):
                    step(k, u, lambda d: True, lambda d: take(words, u - d))
            run(range(N - last * UN, N + lag))

        def nth(k, u, d):
            return k * UN + u - d, (u - d) % UN, k + (u - d) // UN

        def wait_if(eng, sem, value, apart=False):
            if isinstance(value, int) and value <= 0:
                return
            if apart:
                wait_apart(eng, sem, value, passed)
            else:
                eng.wait_ge(sem, value)

        if meanwhile:
            block.gpsimd(meanwhile)

        @block.sync
        def _(sp):
            def step(k, u, has, value):
                if has(0):
                    i, q, n = nth(k, u, 0)
                    wait_if(sp, s_tx, i - UN + 1, True)
                    sp.dma_start(XB[:, q, :], rows[bass.ds(value(0), P)]).then_inc(s_in[q], 16)
                if has(UN + 2):
                    i, q, n = nth(k, u, UN + 2)
                    wait_if(sp, s_ys, i + 1, True)
                    sp.dma_start(results[bass.ds(i * P, P)], YS[:, q, :]).then_inc(s_out[q], 16)

            walk(sp, step, UN + 2, first=2, field="row")
            for q in range(UN):
                sp.wait_ge(s_out[q], 16 * (N // UN))

        @block.tensor
        def _(pe):
            pe.wait_ge(s_in[0], 16)
            pe.transpose(TX[:, 0:P], XB[:, 0, :], const["ident"]).then_inc(s_tx, 1)

            def turn_rows(k, u):
                i, q, n = nth(k, u, -1)
                pe.wait_ge(s_in[q], 16 * n + 16)
                pe.transpose(TX[:, 0:P], XB[:, q, :], const["ident"]).then_inc(s_tx, 1)

            def step(k, u, has, value):
                if has(0):
                    i = nth(k, u, 0)[0]
                    e = value(0)
                    pe.wait_ge(s_xt, i + 1)
                    wait_if(pe, s_h, i - 1)
                    for w, weight in enumerate(weights):
                        m = pe.matmul(UP[:, u % 2, w, 0:F], XT[:, u % 2, :], weight[:, bass.ds(e * F, F)], start=True,
                                      stop=True)
                    m.then_inc(s_up, 1)
                if has(-1):
                    turn_rows(k, u)
                if has(1):
                    i = nth(k, u, 1)[0]
                    pe.wait_ge(s_h, i + 1)
                    wait_if(pe, s_ht, i)
                    for c in range(HB):
                        m = pe.transpose(TH[:, c * P:(c + 1) * P], HH[:, (u - 1) % 2, c * P:(c + 1) * P],
                                         const["ident"])
                    m.then_inc(s_th, 1)
                if has(2):
                    i = nth(k, u, 2)[0]
                    e = value(2)
                    pe.wait_ge(s_ht, i + 1)
                    wait_if(pe, s_ys, i - 1)
                    for c in range(HB):
                        m = pe.matmul(Y[:, u % 2, 0:D], HT[:, u % 2, c * P:(c + 1) * P],
                                      down[:, bass.ds(e * HB * D + c * D, D)], start=(c == 0), stop=(c == HB - 1))
                    m.then_inc(s_y, 1)

            walk(pe, step, 2, last=1, field="expert")

        @block.scalar
        def _(act):
            act.wait_ge(s_tx, 1)
            act.copy(XT[:, 0, :], TX[:, 0:P]).then_inc(s_xt, 1)

            def step(k, u, has, value):
                if has(0) and gated:
                    i = nth(k, u, 0)[0]
                    act.wait_ge(s_up, i + 1)
                    act.activation(SG[:, u % 2, :], UP[:, u % 2, 0, 0:F], ACT.Silu).then_inc(s_sg, 1)
                if has(-1):
                    i = nth(k, u, -1)[0]
                    act.wait_ge(s_tx, i + 1)
                    act.copy(XT[:, (u + 1) % 2, :], TX[:, 0:P]).then_inc(s_xt, 1)
                if has(1):
                    i = nth(k, u, 1)[0]
                    act.wait_ge(s_th, i + 1)
                    act.activation(HT[:, (u - 1) % 2, :], TH[:, 0:F], ACT.Copy if gated else ACT.Relu).then_inc(s_ht, 1)

            walk(act, step, 2, last=1)

        @block.vector
        def _(dve):
            def step(k, u, has, value):
                if has(0):
                    i = nth(k, u, 0)[0]
                    if gated:
                        dve.wait_ge(s_sg, i + 1)
                        one, two, op = SG[:, u % 2, :], UP[:, u % 2, 1, 0:F], ALU.mult
                    else:
                        e = value(0)
                        dve.wait_ge(s_up, i + 1)
                        one, two, op = UP[:, u % 2, 0, 0:F], bias[0][:, bass.ds(e * F, F)], ALU.add
                    dve.tensor_tensor(HH[:, u % 2, :], one, two, op).then_inc(s_h, 1)
                if has(2):
                    i, q, n = nth(k, u, 2)
                    if not gated:
                        e = value(2)
                    dve.wait_ge(s_y, i + 1)
                    wait_if(dve, s_out[q], 16 * n)
                    if gated:
                        m = dve.tensor_copy(YS[:, q, :], Y[:, u % 2, 0:D])
                    else:
                        m = dve.tensor_tensor(YS[:, q, :], Y[:, u % 2, 0:D], bias[1][:, bass.ds(e * D, D)], ALU.add)
                    m.then_inc(s_ys, 1)

            walk(dve, step, 2, first=2, field=None if gated else "expert")


def mixture0(nc, X, const, scratch, due, router, gate, up, down, sgate, sup, sdown):
    rows_dram, results_dram = scratch
    with nc.cleanup_on_exit(), ExitStack() as ctx:
        def sb(name, shape, dt=F32):
            return ctx.enter_context(nc.sbuf_tensor("a" + name, shape, dt))

        WG = sb("wg", [P, NX0, F0])
        WU = sb("wu", [P, NX0, F0])
        WD = sb("wd", [P, NX0, HB0, D])
        SLOT, W12 = due
        route = Routing(nc, ctx, "a", const, NE0, True, BLOCKS0, SLOT)
        route_and_share(nc, X, const, route, W12, (WG, WU, WD), rows_dram, router, gate, up, down, sgate, sup, sdown)
        flat = [w[:, :, :].rearrange("p e f -> p (e f)") for w in (WG, WU)]
        block_pass(nc, "ab", const, route.TAB[0:1, 0, :], rows_dram, results_dram, BLOCKS0, flat,
                   WD[:, :, :, :].rearrange("p e c d -> p (e c d)"), F0)


def route_and_share(nc, X, const, route, W12, weights, rows_dram, router, gate, up, down, sgate, sup, sdown):
    WG, WU, WD = weights
    with nc.cleanup_on_exit(), ExitStack() as ctx:
        def sb(name, shape, dt=F32):
            return ctx.enter_context(nc.sbuf_tensor("a" + name, shape, dt))

        def sem(name):
            return nc.alloc_semaphore(name="a" + name)

        def ps(name, shape):
            return ctx.enter_context(nc.psum_tensor("a" + name, shape, F32))

        RW = sb("rw", [TOP, D])
        RT = sb("rt", [P, TOP])
        XN = sb("xn", [P, TT, D])
        XS = sb("xs", [P, S])
        XT = sb("xT", [P, B * S])
        ZE = sb("ze", [P, D])
        xn = sb("xN", [P, NT, D])
        SG = sb("sg", [P, 2, S])
        HT = sb("ht", [P, 2, S])
        G = ps("g", [P, 2, S])
        U = ps("u", [P, 2, S])
        Y = ps("y", [P, 2, NT * D])
        TP = ps("tp", [P, S])
        RB = ps("rb", [P, TT, TOP])
        PO = TP[:, 0:(TT + 1) * TOP].rearrange("p (a t e) -> p a t e", a=1, e=TOP)
        passed = sem("passed")
        norm = Norm(nc, ctx, "a", const["minus_half"][:, 0:NT], passed)
        s_rw = sem("rw")
        s_sw = sem("sw")
        s_w = sem("w")
        s_rt = sem("rt")
        s_rtc = sem("rtc")
        s_ze = sem("ze")
        s_tp = sem("tp")
        s_cp = sem("cp")
        s_xs = sem("xs")
        s_xt = sem("xt")
        s_rb = sem("rb")
        s_r = sem("r")
        s_e = sem("e")
        s_po = sem("po")
        s_sc = sem("sc")
        s_gu = sem("gu")
        s_sg = sem("sg")
        s_h = sem("h")
        s_y = sem("y")
        s_c = sem("c")
        K, SH = HB0, NE0
        marks = {}
        block = ctx.enter_context(nc.Block())

        @block.vector
        def _(dve):
            st = Steps(dve, s_r)
            st(dve.memset, RT[:, :], 0.0)
            st(dve.memset, route.SLOT[:, :, TT:], 0)
            st(dve.memset, route.V[:, :, :], -3e38)
            dve.wait_ge(s_rt, 1)
            st.wait()
            dve.tensor_copy(RT[:, 0:NE0], TP[:, 0:NE0]).then_inc(s_rtc, 1)

            norm_all(dve, norm, X, xn, s_tp, s_cp)
            dve.wait_ge(s_rb, B)
            st(dve.tensor_copy, route.V[:, :, 0:NE0], RB[:, :, 0:NE0])
            marks["chosen"] = route.choose(st, dve)
            marks["apart"] = st(dve.tensor_tensor, W12[:, 1, :], route.BEST[:, 1, :], route.BEST[:, 0, :], ALU.subtract)

            def hidden(b):
                for k in range(K):
                    dve.wait_ge(s_sg, b * K + k + 1)
                    dve.tensor_tensor(HT[:, k % 2, :], SG[:, k % 2, :], U[:, k % 2, :], ALU.mult).then_inc(s_h, 1)

            def add(b):
                now = X[:, bass.ds(b * NT, NT), :].rearrange("p t d -> p (t d)")
                dve.wait_ge(s_y, b + 1)
                dve.tensor_tensor(now, now, Y[:, 0, :], ALU.add).then_inc(s_c, 1)

            hidden(0)
            dve.wait_ge(s_po, 1)
            marks["placed"] = route.place(st, dve, PO)
            add(0)
            dve.wait_ge(s_e, 1)
            st(dve.tensor_scalar, W12[:, 0, :], W12[:, 1, :], 1.0, None, ALU.add)
            st(dve.reciprocal, W12[:, 0, :], W12[:, 0, :])
            st(dve.tensor_tensor, W12[:, 1, :], W12[:, 0, :], W12[:, 1, :], ALU.mult)
            route.table(st, dve, PO)
            with dve.Fori(1, B) as b:
                hidden(b)
                add(b)

        @block.sync
        def _(sp):
            sp.dma_start(RW[0:NE0, :], router).then_inc(s_rw, 16)
            for dst, shared in ((WG, sgate), (WU, sup)):
                sp.dma_start(dst[:, SH, :], shared[0]).then_inc(s_sw, 16)
            sp.dma_start(WD[:, SH, :, :], sdown[0].rearrange("(c h) d -> h c d", h=P)).then_inc(s_sw, 16)
            for dst, routed in ((WG, gate), (WU, up)):
                sp.dma_start(dst[:, 0:NE0, :], routed.rearrange("e d h -> d e h")).then_inc(s_w, 16)
            for e in range(NE0):
                sp.dma_start(WD[:, e, :, :], down[e].rearrange("(c h) d -> h c d", h=P)).then_inc(s_w, 16)
            sp.wait_ge(s_w, 16 * (2 + NE0))

        @block.tensor
        def _(pe):
            pe.wait_ge(s_rw, 16)
            pe.transpose(TP[:, 0:NE0], RW[0:NE0, :], const["ident"][0:NE0, 0:NE0]).then_inc(s_rt, 1)
            pe.wait_ge(s_rtc, 1)

            def turn(b):
                pe.wait_ge(norm.s_out, b + 1)
                for t in range(NT):
                    m = pe.transpose(TP[:, t * P:(t + 1) * P], xn[:, t, :], const["ident"])
                m.then_inc(s_tp, 1)
                pe.wait_ge(s_xs, b + 1)
                for t in range(NT):
                    m = pe.matmul(RB[:, b * NT + t, :], XS[:, t * P:(t + 1) * P], RT[:, :], start=True, stop=True,
                                  skip_group_check=True)
                m.then_inc(s_rb, 1)
                pe.wait_ge(s_xt, b + 1)

            with pe.Fori(0, B) as b:
                turn(b)
            pe.wait_ge(s_sw, 48)

            def down_(b, k):
                pe.wait_ge(s_h, b * K + k + 1)
                for t in range(NT):
                    m = pe.matmul(Y[:, 0, t * D:(t + 1) * D], HT[:, k % 2, t * P:(t + 1) * P],
                                  WD[:, SH, k, :], start=(k == 0 and t == 0), stop=(k == K - 1),
                                  skip_group_check=True)
                if k == K - 1:
                    m.then_inc(s_y, 1)

            def body(b, first):
                for k in range(K):
                    if not first or k > 1:
                        pe.wait_ge(s_h, b * K + k - 1)
                    for dst, wt in ((G, WG), (U, WU)):
                        m = pe.matmul(dst[:, k % 2, :], wt[:, SH, k * P:(k + 1) * P], XT[:, bass.ds(b * S, S)],
                                      start=True, stop=True)
                    m.then_inc(s_gu, 1)
                    if k == 0 and not first:
                        down_(b - 1, K - 1)
                    if k == 1 and not first:
                        pe.wait_ge(s_c, b)
                    if k:
                        down_(b, k - 1)

            body(0, True)
            pe.wait_ge(s_r, marks["chosen"])
            route.count(pe, PO, s_po)
            with pe.Fori(1, B) as b:
                body(b, False)
            down_(B - 1, K - 1)

        @block.scalar
        def _(act):
            with act.Fori(0, B) as b:
                act.wait_ge(s_tp, b + 1)
                act.copy(XS[:, :], TP[:, :]).then_inc(s_xs, 1)
                act.copy(XT[:, bass.ds(b * S, S)], TP[:, :]).then_inc(s_xt, 1)
            act.wait_ge(s_r, marks["apart"])
            act.activation(W12[:, 1, :], W12[:, 1, :], ACT.Exp).then_inc(s_e, 1)
            with act.Fori(0, B) as b:
                for k in range(K):
                    act.wait_ge(s_gu, b * K + k + 1)
                    act.activation(SG[:, k % 2, :], G[:, k % 2, :], ACT.Silu).then_inc(s_sg, 1)

        @block.gpsimd
        def _(pool):
            def sequence(b):
                norm.pool(pool, b)
                wait_apart(pool, norm.s_out, b + 1, passed)
                pool.tensor_copy(XN[:, bass.ds(b * NT, NT), :], xn[:, :, :]).then_inc(s_cp, 1)

            sequence(0)
            with pool.Fori(1, B) as b:
                sequence(b)
            pool.memset(ZE[:, :], 0.0).then_inc(s_ze, 1)
            pool.wait_ge(s_ze, 1)
            pool.wait_ge(s_cp, B)
            pool.wait_ge(s_r, marks["placed"])
            n = route.scatter(pool, lambda t: XN[:, t, :], rows_dram, s_sc, (0, 1))
            n += route.pad(pool, ZE[:, :], rows_dram, s_sc, 0)
            pool.wait_ge(s_sc, n)


def gather(pool, route, YG, results_dram, sems, choices, place=0, after=None):
    n = 16 * NT * len(choices)
    for b in range(B):
        if b > 1:
            pool.wait_ge(sems[b % 2], n * (b // 2))
        for t in range(b * NT, (b + 1) * NT):
            for at, j in enumerate(choices):
                pool.indirect_dma_start(YG[:, place + at, t, :], None, results_dram,
                                        bass.IndirectOffsetOnAxis(ap=route.SLOT[:, j, t:t + 1], axis=0)
                                        ).then_inc(sems[b % 2], 16)
        if after and b:
            after(b - 1)
    if after:
        after(B - 1)


def gathered(dve, sems, n, sequence):
    def pair(k):
        for odd in range(2):
            dve.wait_ge(sems[odd], 16 * n * (k + 1))
            sequence(2 * k + odd)

    pair(0)
    with dve.Fori(1, B // 2) as k:
        pair(k)


def mixture1(nc, X, const, scratch, out_dram, gate_w, gate_b, w1, b1, w2, b2, gamma, beta):
    rows_dram, results_dram = scratch
    with nc.cleanup_on_exit(), ExitStack() as ctx:
        def sb(name, shape, dt=F32):
            return ctx.enter_context(nc.sbuf_tensor("b" + name, shape, dt))

        W1 = sb("w1", [P, NE1, F1])
        W2 = sb("w2", [P, NE1, HB1, D])
        B1 = sb("b1", [P, NE1, F1])
        B2 = sb("b2", [P, NE1, D])
        GA = sb("ga", [P, D])
        BE = sb("be", [P, D])
        XN = sb("xn", [P, TT, D])
        OR = sb("or", [P, 2, TT, D])
        ZE = sb("zeros", [P, D])
        route = Routing(nc, ctx, "b", const, NE1, False, BLOCKS1)
        route_gate(nc, X, XN, const, route, (W1, W2, B1, B2, GA, BE), rows_dram[0], gate_w, gate_b, w1, b1, w2, b2,
                   gamma, beta)
        flat = W1[:, :, :].rearrange("p e f -> p (e f)")
        s_ze, s_pad = (nc.alloc_semaphore(name="b" + n) for n in ("zz", "pad"))

        def pad_second(pool):
            pool.memset(ZE[:, :], 0.0).then_inc(s_ze, 1)
            pool.wait_ge(s_ze, 1)
            n = route.pad(pool, ZE[:, :], rows_dram[1], s_pad, 1)
            pool.wait_ge(s_pad, n)

        for r in range(ROUNDS):
            block_pass(nc, f"b{r}", const, route.TAB[0:1, r, :], rows_dram[r], results_dram[r], BLOCKS1, [flat],
                       W2[:, :, :, :].rearrange("p e c d -> p (e c d)"), F1,
                       bias=(B1[:, :, :].rearrange("p e f -> p (e f)"), B2[:, :, :].rearrange("p e d -> p (e d)")),
                       meanwhile=pad_second if r == 0 else None)
            if r == 0:
                boost(nc, XN, OR, route, rows_dram[1], results_dram[0])
        finish(nc, X, XN, OR, const, route, GA, BE, results_dram[1], out_dram)


def route_gate(nc, X, XN, const, route, weights, rows_dram, gate_w, gate_b, w1, b1, w2, b2, gamma, beta):
    W1, W2, B1, B2, GA, BE = weights
    with nc.cleanup_on_exit(), ExitStack() as ctx:
        def sb(name, shape, dt=F32):
            return ctx.enter_context(nc.sbuf_tensor("b" + name, shape, dt))

        def sem(name):
            return nc.alloc_semaphore(name="b" + name)

        def ps(name, shape):
            return ctx.enter_context(nc.psum_tensor("b" + name, shape, F32))

        GW = sb("gw", [P, NE1])
        GB = sb("gb", [P, NE1])
        XS = sb("xs", [P, S])
        ZE = sb("ze", [P, D])
        xn = sb("xN", [P, NT, D])
        MX = sb("mx", [P, TT, 1])
        TP = ps("tp", [P, S])
        RB = ps("rb", [P, TT, TOP])
        PO = ps("po", [P, 2, S])
        PO = PO[:, :, 0:(TT + 1) * TOP].rearrange("p a (t e) -> p a t e", e=TOP)
        passed = sem("passed")
        norm = Norm(nc, ctx, "b", const["minus_half"][:, 0:NT], passed)
        s_gate = sem("gate")
        s_w = sem("w")
        s_ze = sem("ze")
        s_tp = sem("tp")
        s_cp = sem("cp")
        s_xs = sem("xs")
        s_rb = sem("rb")
        s_r = sem("r")
        s_e = sem("e")
        s_po = sem("po")
        s_sc = sem("sc")
        marks = {}
        block = ctx.enter_context(nc.Block())

        @block.vector
        def _(dve):
            norm_all(dve, norm, X, xn, s_tp, s_cp)
            st = Steps(dve, s_r)
            wide = [P, TT, TOP]
            V = route.V[:, :, :]
            dve.wait_ge(s_gate, 32)
            dve.wait_ge(s_rb, B)
            st(dve.tensor_tensor, V, RB[:, :, :], across(GB[:, :], wide), ALU.add)
            st(dve.tensor_reduce, MX[:, :, 0], V, AX.X, ALU.max)
            marks["less"] = st(dve.tensor_tensor, V, V, MX[:, :, :].broadcast_to(wide), ALU.subtract)
            dve.wait_ge(s_e, 1)
            st(dve.tensor_reduce, MX[:, :, 0], V, AX.X, ALU.add)
            st(dve.reciprocal, MX[:, :, :], MX[:, :, :])
            st(dve.tensor_tensor, V, V, MX[:, :, :].broadcast_to(wide), ALU.mult)
            marks["chosen"] = route.choose(st, dve)
            dve.wait_ge(s_po, 1)
            marks["placed"] = route.place(st, dve, PO)
            route.table(st, dve, PO)

        @block.sync
        def _(sp):
            sp.dma_start(GW[:, :], gate_w).then_inc(s_gate, 16)
            sp.dma_start(GB[:, :], gate_b.partition_broadcast(P)).then_inc(s_gate, 16)
            sp.dma_start(W1[:, :, :], w1.rearrange("e d h -> d e h")).then_inc(s_w, 16)
            sp.dma_start(W2[:, :, :, :], w2.rearrange("e (c h) d -> h e c d", h=P)).then_inc(s_w, 16)
            sp.dma_start(B1[:, :, :], b1.rearrange("e h -> (e h)").partition_broadcast(P)).then_inc(s_w, 16)
            sp.dma_start(B2[:, :, :], b2.rearrange("e d -> (e d)").partition_broadcast(P)).then_inc(s_w, 16)
            sp.dma_start(GA[:, :], gamma.partition_broadcast(P)).then_inc(s_w, 16)
            sp.dma_start(BE[:, :], beta.partition_broadcast(P)).then_inc(s_w, 16)
            sp.wait_ge(s_w, 96)

        @block.tensor
        def _(pe):
            pe.wait_ge(s_gate, 32)
            with pe.Fori(0, B) as b:
                pe.wait_ge(norm.s_out, b + 1)
                for t in range(NT):
                    m = pe.transpose(TP[:, t * P:(t + 1) * P], xn[:, t, :], const["ident"])
                m.then_inc(s_tp, 1)
                pe.wait_ge(s_xs, b + 1)
                for t in range(NT):
                    m = pe.matmul(RB[:, b * NT + t, :], XS[:, t * P:(t + 1) * P], GW[:, :], start=True, stop=True,
                                  skip_group_check=True)
                m.then_inc(s_rb, 1)
            pe.wait_ge(s_r, marks["chosen"])
            route.count(pe, PO, s_po)

        @block.scalar
        def _(act):
            with act.Fori(0, B) as b:
                act.wait_ge(s_tp, b + 1)
                act.copy(XS[:, :], TP[:, :]).then_inc(s_xs, 1)
            act.wait_ge(s_r, marks["less"])
            act.activation(route.V[:, :, :], route.V[:, :, :], ACT.Exp).then_inc(s_e, 1)

        @block.gpsimd
        def _(pool):
            def sequence(b):
                norm.pool(pool, b)
                wait_apart(pool, norm.s_out, b + 1, passed)
                pool.tensor_copy(XN[:, bass.ds(b * NT, NT), :], xn[:, :, :]).then_inc(s_cp, 1)

            sequence(0)
            with pool.Fori(1, B) as b:
                sequence(b)
            pool.memset(ZE[:, :], 0.0).then_inc(s_ze, 1)
            pool.wait_ge(s_ze, 1)
            pool.wait_ge(s_cp, B)
            pool.wait_ge(s_r, marks["placed"])
            n = route.scatter(pool, lambda t: XN[:, t, :], rows_dram, s_sc, (0,))
            n += route.pad(pool, ZE[:, :], rows_dram, s_sc, 0)
            pool.wait_ge(s_sc, n)


def boost(nc, XN, OR, route, rows_dram, results_dram):
    with nc.cleanup_on_exit(), ExitStack() as ctx:
        BO = ctx.enter_context(nc.sbuf_tensor("dbo", [P, TT, D], F32))
        s_g = [nc.alloc_semaphore(name=f"dg{i}") for i in range(2)]
        s_b = nc.alloc_semaphore(name="db")
        s_sc = nc.alloc_semaphore(name="ds")
        block = ctx.enter_context(nc.Block())

        @block.gpsimd
        def _(pool):
            gather(pool, route, OR, results_dram, s_g, (0,))
            pool.wait_ge(s_b, B)
            n = route.scatter(pool, lambda t: BO[:, t, :], rows_dram, s_sc, (1,))
            pool.wait_ge(s_sc, n)

        @block.vector
        def _(dve):
            def sequence(b):
                t = bass.ds(b * NT, NT)
                dve.scalar_tensor_tensor(BO[:, t, :], OR[:, 0, t, :], BOOST, XN[:, t, :], ALU.mult, ALU.add
                                         ).then_inc(s_b, 1)

            gathered(dve, s_g, NT, sequence)


def finish(nc, X, XN, OR, const, route, GA, BE, results_dram, out_dram):
    with nc.cleanup_on_exit(), ExitStack() as ctx:
        F = ctx.enter_context(nc.sbuf_tensor("ef", [P, NT, D], F32))
        s_g = [nc.alloc_semaphore(name=f"eg{i}") for i in range(2)]
        s_f = nc.alloc_semaphore(name="ef")
        s_out = ctx.enter_context(nc.semaphore("eo"))
        passed = nc.alloc_semaphore(name="ep")
        norm = Norm(nc, ctx, "e", const["minus_half"][:, 0:NT], passed)
        block = ctx.enter_context(nc.Block())

        @block.gpsimd
        def _(pool):
            gather(pool, route, OR, results_dram, s_g, (1,), 1, after=lambda b: norm.pool(pool, b))

        @block.sync
        def _(sp):
            for b in range(B):
                sp.wait_ge(s_f, 5 * b + 5)
                sp.dma_start(out_dram[b].rearrange("(t p) d -> p t d", p=P), X[:, b * NT:(b + 1) * NT, :]
                             ).then_inc(s_out, 16)
            sp.wait_ge(s_out, 16 * B)

        @block.vector
        def _(dve):
            def sequence(b):
                if not (isinstance(b, int) and b == 0):
                    dve.wait_ge(s_f, 5 * b)
                for r in range(ROUNDS):
                    for t in range(NT):
                        x = XN[:, b * NT + t, :] if r == 0 else F[:, t, :]
                        m = dve.scalar_tensor_tensor(F[:, t, :], OR[:, r, b * NT + t, :],
                                                     route.BEST[:, r, bass.ds(b * NT + t, 1)], x, ALU.mult, ALU.add)
                    m.then_inc(s_f, 1)
                    dve.wait_ge(s_f, 5 * b + r + 1)
                norm.vector_stats(dve, b, lambda t: F[:, t, :])
                norm.vector_rows(dve, b, lambda t: F[:, t, :], lambda t: F[:, t, :])
                dve.wait_ge(norm.s_out, b + 1)
                for i, (row, op) in enumerate(((GA, ALU.mult), (BE, ALU.add))):
                    dve.tensor_tensor(F[:, :, :], F[:, :, :], across(row[:, :], [P, NT, D]), op).then_inc(s_f, 1)
                    dve.wait_ge(s_f, 5 * b + 3 + i)
                now = X[:, bass.ds(b * NT, NT), :]
                dve.tensor_tensor(now, now, F[:, :, :], ALU.add).then_inc(s_f, 1)

            gathered(dve, s_g, NT, sequence)


def build(nc, c, x, w0qkv, w0out, router, gate, up, down, sgate, sup, sdown, w1qkv, w1out, gate_w, gate_b, w1, b1,
          w2, b2, gamma, beta, out):
    at = constants()[1]
    with ExitStack() as ctx:
        X = ctx.enter_context(nc.sbuf_tensor("X", [P, B * NT, D], F32))
        const, attn0, attn1 = setup(nc, ctx, c, at, x, X, w0qkv, w0out, w1qkv, w1out)
        parts = nc.dram_tensor("qk_parts", [2, KR, H, S], BF16).ap()
        rows0 = nc.dram_tensor("maxima_0", [3 * HG * SPLIT, S], BF16).ap()
        rows1 = nc.dram_tensor("maxima_1", [HG * SPLIT, S], BF16).ap()
        attention(nc, X, const, attn0, (parts, rows0), False)
        rows = [nc.dram_tensor(f"rows_{i}", [P << RBITS, D], F32).ap() for i in range(3)]
        results = [nc.dram_tensor(f"results_{i}", [n * P, D], F32).ap() for i, n in enumerate(
            (BLOCKS0, BLOCKS1, BLOCKS1))]
        slots = ctx.enter_context(nc.sbuf_tensor("slots", [P, 2, TT + NT], U32))
        weights = ctx.enter_context(nc.sbuf_tensor("weights", [P, 2, TT], F32))
        mixture0(nc, X, const, (rows[0], results[0]), (slots, weights), router, gate, up, down, sgate, sup, sdown)
        attention(nc, X, const, attn1, (parts, rows1), True, (slots, weights, results[0]))
        mixture1(nc, X, const, (rows[1:], results[1:]), out, gate_w, gate_b, w1, b1, w2, b2, gamma, beta)


INPUTS = ["L0_attn_x", "L0_attn_w_qkv", "L0_attn_w_out", "L0_ffn_router_w", "L0_ffn_w_gate", "L0_ffn_w_up",
          "L0_ffn_w_down", "L0_ffn_sw_gate", "L0_ffn_sw_up", "L0_ffn_sw_down", "L1_attn_W_qkv", "L1_attn_W_out",
          "L1_ffn_gate_W", "L1_ffn_gate_b", "L1_ffn_W1", "L1_ffn_b1", "L1_ffn_W2", "L1_ffn_b2", "L1_ffn_ln_gamma",
          "L1_ffn_ln_beta"]


def kernel(**inputs):
    import numpy as np
    import concourse.bacc as bacc
    from concourse.bass_utils import run_bass_kernel_spmd

    nc = bacc.Bacc("TRN2", target_bir_lowering=False, num_devices=1)
    arrays = {"constants": constants()[0]}
    for name in INPUTS:
        arrays[name] = np.ascontiguousarray(inputs[name])
    args = [nc.dram_tensor(name, a.shape, mybir.dt.from_np(a.dtype), kind="ExternalInput").ap()
            for name, a in arrays.items()]
    out = nc.dram_tensor("out", (B, S, D), F32, kind="ExternalOutput").ap()
    build(nc, *args, out)
    result = run_bass_kernel_spmd(nc, [arrays], core_ids=[0])
    return result.results[0]["out"]
```
